# Optimizing a Trainium2 kernel written in Bass

```python
import numpy as np
import jax
import jax.numpy as jnp

def _softmax(x, axis=-1):
    return jax.nn.softmax(x, axis=axis)

def _gelu(x):
    return jax.nn.gelu(x, approximate=True)

def _silu(x):
    return jax.nn.silu(x)

def _sigmoid(x):
    return jax.nn.sigmoid(x)

def _layernorm(x, axis=-1, eps=1e-05):
    m = jnp.mean(x, axis=axis, keepdims=True)
    v = jnp.var(x, axis=axis, keepdims=True)
    return (x - m) / jnp.sqrt(v + eps)

def _scatter_add(tgt, idx, src, axis=0):
    return tgt.at[idx].add(src)

def _segment_sum(src, seg, n):
    return jax.ops.segment_sum(src, seg, n)
kernel_name = 'mk_perceiver_d1_seqx_r4_28bd5e'

def setup_inputs(seed: int=0):
    np.random.seed(seed)
    _w = jnp.asarray

    def _rec_inputs():
        import jax
        import jax.numpy as jnp
        _rk = jax.random.key(seed)
        x = 0.002226 + 0.9996 * jax.random.normal(jax.random.fold_in(_rk, 1), (64, 32, 256), jnp.float32)
        _lenS = 32 - jax.random.randint(jax.random.fold_in(_rk, 7), (64,), 0, max(1, 32 // 4) + 1, jnp.int32)
        _lenS2 = 257 - jax.random.randint(jax.random.fold_in(_rk, 8), (64,), 0, max(1, 257 // 4) + 1, jnp.int32)
        _ctx_1024P = jax.random.normal(jax.random.fold_in(_rk, 11), (64, 16, 256), jnp.float32)
        _ctx_1024c = jax.random.dirichlet(jax.random.fold_in(_rk, 511), 0.3 * jnp.ones((16,), jnp.float32), (64, 257))
        _ctx_1024t = jnp.einsum('bsk,bkd->bsd', _ctx_1024c, _ctx_1024P)
        _ctx_1024t = _ctx_1024t * jax.lax.rsqrt(jnp.mean(jnp.square(_ctx_1024t)) + 1e-12) * 0.953939
        ctx_1024 = -7.10856e-05 + 0.999911 * (_ctx_1024t + 0.3 * jax.random.normal(jax.random.fold_in(_rk, 611), (64, 257, 256), jnp.float32))
        return (x, ctx_1024)
    x, ctx_1024 = _rec_inputs()

    def _L0_xattn_setup():
        import jax, jax.numpy as jnp
        import numpy as np
        DIM = 256
        HEAD_DIM = 64
        NUM_HEADS = 8
        INNER = HEAD_DIM * NUM_HEADS
        ROT_DIM = HEAD_DIM
        ROPE_BASE = 10000.0
        EPS = 1e-05

        def layer_norm(x, g, b):
            mu = jnp.mean(x, axis=-1, keepdims=True)
            var = jnp.var(x, axis=-1, keepdims=True)
            return (x - mu) * jax.lax.rsqrt(var + EPS) * g + b

        def rope_rotate_k(k):
            n = k.shape[1]
            half = ROT_DIM // 2
            inv_freq = 1.0 / ROPE_BASE ** (jnp.arange(0, ROT_DIM, 2, dtype=jnp.float32) / ROT_DIM)
            theta = jnp.arange(n, dtype=jnp.float32)[:, None] * inv_freq[None, :]
            angles = jnp.concatenate([theta, theta], axis=-1)
            cos = jnp.cos(angles)[None, :, None, :].astype(k.dtype)
            sin = jnp.sin(angles)[None, :, None, :].astype(k.dtype)
            k_rope, k_pass = (k[..., :ROT_DIM], k[..., ROT_DIM:])
            neg_half = jnp.concatenate([-k_rope[..., half:], k_rope[..., :half]], axis=-1)
            k_rope = k_rope * cos + neg_half * sin
            return jnp.concatenate([k_rope, k_pass], axis=-1)
        key = jax.random.key(seed)
        ks = jax.random.split(key, 5)
        b, n, m = (8, 2048, 64)
        s = 1.0 / np.sqrt(DIM)
        return {'x': jax.random.normal(ks[0], (b, n, DIM), jnp.float32), 'latents': jax.random.normal(ks[1], (b, m, DIM), jnp.float32), 'gamma_x': jnp.ones((DIM,), jnp.float32), 'beta_x': jnp.zeros((DIM,), jnp.float32), 'gamma_l': jnp.ones((DIM,), jnp.float32), 'beta_l': jnp.zeros((DIM,), jnp.float32), 'Wq': jax.random.normal(ks[2], (DIM, INNER), jnp.float32) * s, 'Wkv': jax.random.normal(ks[3], (DIM, 2 * INNER), jnp.float32) * s, 'Wo': jax.random.normal(ks[4], (INNER, DIM), jnp.float32) * (1.0 / np.sqrt(INNER))}
    _L0_xattn_all = _L0_xattn_setup()
    _L0_xattn_in = {k: v for k, v in _L0_xattn_all.items() if k in ('gamma_x', 'beta_x', 'gamma_l', 'beta_l', 'Wq', 'Wkv', 'Wo')}
    del _L0_xattn_all

    def _L0_attn_setup():
        import jax, jax.numpy as jnp
        import numpy as np
        D_MODEL = 256
        HEADDIM = 64
        EXPAND = 2
        D_STATE = 128
        D_CONV = 4
        NGROUPS = 1
        D_INNER = EXPAND * D_MODEL
        NHEADS = D_INNER // HEADDIM
        CONV_DIM = D_INNER + 2 * NGROUPS * D_STATE
        D_IN_PROJ = 2 * D_INNER + 2 * NGROUPS * D_STATE + NHEADS
        BATCH = 2
        SEQLEN = 256
        EPS = 1e-05

        def silu(v):
            return v * jax.nn.sigmoid(v)

        def _mamba2(x, in_proj_w, conv_w, conv_b, dt_bias, A_log, D, norm_w, out_proj_w):
            b, l, _ = x.shape
            zxbcdt = x @ in_proj_w.T
            z, xBC, dt = jnp.split(zxbcdt, [D_INNER, D_INNER + CONV_DIM], axis=-1)
            dt = jax.nn.softplus(dt + dt_bias)
            rhs = conv_w.T[:, None, :]
            xBC = jax.lax.conv_general_dilated(xBC, rhs, window_strides=(1,), padding=[(D_CONV - 1, 0)], dimension_numbers=('NWC', 'WIO', 'NWC'), feature_group_count=CONV_DIM)
            xBC = silu(xBC + conv_b)
            xs, Bm, Cm = jnp.split(xBC, [D_INNER, D_INNER + D_STATE], axis=-1)
            xs = xs.reshape(b, l, NHEADS, HEADDIM)
            A = -jnp.exp(A_log)
            dA = jnp.exp(dt * A)

            def step(h, inp):
                dA_t, x_t, B_t, dt_t, C_t = inp
                h = h * dA_t[:, :, None, None] + jnp.einsum('bh,bhp,bn->bhpn', dt_t, x_t, B_t)
                y = jnp.einsum('bhpn,bn->bhp', h, C_t)
                return (h, y)
            h0 = jnp.zeros((b, NHEADS, HEADDIM, D_STATE), x.dtype)
            xs_t = xs.transpose(1, 0, 2, 3)
            _, ys = jax.lax.scan(step, h0, (dA.transpose(1, 0, 2), xs_t, Bm.transpose(1, 0, 2), dt.transpose(1, 0, 2), Cm.transpose(1, 0, 2)))
            y = ys.transpose(1, 0, 2, 3) + D[None, None, :, None] * xs
            y = y.reshape(b, l, D_INNER)
            y = y * silu(z)
            y = y * jax.lax.rsqrt(jnp.mean(y * y, axis=-1, keepdims=True) + EPS) * norm_w
            return y @ out_proj_w.T
        key = jax.random.key(seed)
        ks = jax.random.split(key, 8)
        s = 0.02
        return {'x': jax.random.normal(ks[0], (BATCH, SEQLEN, D_MODEL), jnp.float32), 'in_proj_w': jax.random.normal(ks[1], (D_IN_PROJ, D_MODEL), jnp.float32) * s, 'conv_w': jax.random.normal(ks[2], (CONV_DIM, D_CONV), jnp.float32) * 0.2, 'conv_b': jax.random.normal(ks[3], (CONV_DIM,), jnp.float32) * 0.02, 'dt_bias': jax.random.normal(ks[4], (NHEADS,), jnp.float32) * 0.1, 'A_log': jax.random.normal(ks[5], (NHEADS,), jnp.float32) * 0.5, 'D': jax.random.normal(ks[6], (NHEADS,), jnp.float32) * 0.5, 'norm_w': jnp.ones((D_INNER,), jnp.float32), 'out_proj_w': jax.random.normal(ks[7], (D_MODEL, D_INNER), jnp.float32) * s}
    _L0_attn_all = _L0_attn_setup()
    _L0_attn_in = {k: v for k, v in _L0_attn_all.items() if k in ('in_proj_w', 'conv_w', 'conv_b', 'dt_bias', 'A_log', 'D', 'norm_w', 'out_proj_w')}
    del _L0_attn_all

    def _L0_ffn_setup():
        import jax, jax.numpy as jnp
        import numpy as np
        N_HEAD = 16
        NUM_EXPERTS = 8
        TOP_K = 2
        LN_EPS = 1e-05

        def _layernorm(x, g, b):
            mu = jnp.mean(x, axis=-1, keepdims=True)
            var = jnp.mean(jnp.square(x - mu), axis=-1, keepdims=True)
            return (x - mu) * jax.lax.rsqrt(var + LN_EPS) * g + b

        def _attention(h, Wq, bq, Wk, bk, Wv, bv, Wp, bp):
            B, T, D = h.shape
            hd = D // N_HEAD

            def split(z):
                return z.reshape(B, T, N_HEAD, hd).transpose(0, 2, 1, 3)
            q = split(h @ Wq + bq)
            k = split(h @ Wk + bk)
            v = split(h @ Wv + bv)
            att = jnp.einsum('bhqd,bhkd->bhqk', q, k) / jnp.sqrt(jnp.float32(hd))
            causal = jnp.tril(jnp.ones((T, T), bool))
            att = jnp.where(causal, att, -jnp.inf)
            att = jax.nn.softmax(att, axis=-1)
            y = jnp.einsum('bhqk,bhkd->bhqd', att, v)
            y = y.transpose(0, 2, 1, 3).reshape(B, T, D)
            return y @ Wp + bp

        def _token_moe(h, gate_W, gate_b, exp_W1, exp_b1, exp_W2, exp_b2):
            B, T, D = h.shape
            flat = h.reshape(-1, D)
            N = flat.shape[0]
            logits = flat @ gate_W + gate_b
            top_v, top_i = jax.lax.top_k(logits, TOP_K)
            w = jax.nn.softmax(top_v, axis=-1)
            w_full = jnp.zeros((N, NUM_EXPERTS), flat.dtype)
            w_full = w_full.at[jnp.arange(N)[:, None], top_i].add(w)
            out = jnp.zeros_like(flat)
            for e in range(NUM_EXPERTS):
                mid = jax.nn.gelu(flat @ exp_W1[e] + exp_b1[e], approximate=False)
                y_e = mid @ exp_W2[e] + exp_b2[e]
                out = out + w_full[:, e:e + 1] * y_e
            return out.reshape(B, T, D)
        key = jax.random.key(seed)
        B, T, D = (8, 256, 256)
        H = 4 * D
        E = NUM_EXPERTS
        ks = jax.random.split(key, 24)
        s = 0.02
        inp = {'x': jax.random.normal(ks[0], (B, T, D), jnp.float32), 'ln1_g': jnp.ones((D,), jnp.float32), 'ln1_b': jnp.zeros((D,), jnp.float32), 'ln2_g': jnp.ones((D,), jnp.float32), 'ln2_b': jnp.zeros((D,), jnp.float32), 'Wq': jax.random.normal(ks[1], (D, D), jnp.float32) * s, 'bq': jnp.zeros((D,), jnp.float32), 'Wk': jax.random.normal(ks[2], (D, D), jnp.float32) * s, 'bk': jnp.zeros((D,), jnp.float32), 'Wv': jax.random.normal(ks[3], (D, D), jnp.float32) * s, 'bv': jnp.zeros((D,), jnp.float32), 'Wp': jax.random.normal(ks[4], (D, D), jnp.float32) * s, 'bp': jnp.zeros((D,), jnp.float32), 'gate_W': jax.random.normal(ks[5], (D, E), jnp.float32) * s, 'gate_b': jnp.zeros((E,), jnp.float32), 'exp_W1': jax.random.normal(ks[6], (E, D, H), jnp.float32) * s, 'exp_b1': jnp.zeros((E, H), jnp.float32), 'exp_W2': jax.random.normal(ks[7], (E, H, D), jnp.float32) * s, 'exp_b2': jnp.zeros((E, D), jnp.float32)}
        return inp
    _L0_ffn_all = _L0_ffn_setup()
    _L0_ffn_in = {k: v for k, v in _L0_ffn_all.items() if k in ('ln1_g', 'ln1_b', 'ln2_g', 'ln2_b', 'Wq', 'bq', 'Wk', 'bk', 'Wv', 'bv', 'Wp', 'bp', 'gate_W', 'gate_b', 'exp_W1', 'exp_b1', 'exp_W2', 'exp_b2')}
    del _L0_ffn_all
    return {'x': x, 'ctx_1024': ctx_1024, 'L0_xattn_gamma_x': _L0_xattn_in['gamma_x'], 'L0_xattn_beta_x': _L0_xattn_in['beta_x'], 'L0_xattn_gamma_l': _L0_xattn_in['gamma_l'], 'L0_xattn_beta_l': _L0_xattn_in['beta_l'], 'L0_xattn_Wq': _L0_xattn_in['Wq'], 'L0_xattn_Wkv': _L0_xattn_in['Wkv'], 'L0_xattn_Wo': _L0_xattn_in['Wo'], 'L0_attn_in_proj_w': _L0_attn_in['in_proj_w'], 'L0_attn_conv_w': _L0_attn_in['conv_w'], 'L0_attn_conv_b': _L0_attn_in['conv_b'], 'L0_attn_dt_bias': _L0_attn_in['dt_bias'], 'L0_attn_A_log': _L0_attn_in['A_log'], 'L0_attn_D': _L0_attn_in['D'], 'L0_attn_norm_w': _L0_attn_in['norm_w'], 'L0_attn_out_proj_w': _L0_attn_in['out_proj_w'], 'L0_ffn_ln1_g': _L0_ffn_in['ln1_g'], 'L0_ffn_ln1_b': _L0_ffn_in['ln1_b'], 'L0_ffn_ln2_g': _L0_ffn_in['ln2_g'], 'L0_ffn_ln2_b': _L0_ffn_in['ln2_b'], 'L0_ffn_Wq': _L0_ffn_in['Wq'], 'L0_ffn_bq': _L0_ffn_in['bq'], 'L0_ffn_Wk': _L0_ffn_in['Wk'], 'L0_ffn_bk': _L0_ffn_in['bk'], 'L0_ffn_Wv': _L0_ffn_in['Wv'], 'L0_ffn_bv': _L0_ffn_in['bv'], 'L0_ffn_Wp': _L0_ffn_in['Wp'], 'L0_ffn_bp': _L0_ffn_in['bp'], 'L0_ffn_gate_W': _L0_ffn_in['gate_W'], 'L0_ffn_gate_b': _L0_ffn_in['gate_b'], 'L0_ffn_exp_W1': _L0_ffn_in['exp_W1'], 'L0_ffn_exp_b1': _L0_ffn_in['exp_b1'], 'L0_ffn_exp_W2': _L0_ffn_in['exp_W2'], 'L0_ffn_exp_b2': _L0_ffn_in['exp_b2']}

def reference(x, ctx_1024, L0_xattn_gamma_x, L0_xattn_beta_x, L0_xattn_gamma_l, L0_xattn_beta_l, L0_xattn_Wq, L0_xattn_Wkv, L0_xattn_Wo, L0_attn_in_proj_w, L0_attn_conv_w, L0_attn_conv_b, L0_attn_dt_bias, L0_attn_A_log, L0_attn_D, L0_attn_norm_w, L0_attn_out_proj_w, L0_ffn_ln1_g, L0_ffn_ln1_b, L0_ffn_ln2_g, L0_ffn_ln2_b, L0_ffn_Wq, L0_ffn_bq, L0_ffn_Wk, L0_ffn_bk, L0_ffn_Wv, L0_ffn_bv, L0_ffn_Wp, L0_ffn_bp, L0_ffn_gate_W, L0_ffn_gate_b, L0_ffn_exp_W1, L0_ffn_exp_b1, L0_ffn_exp_W2, L0_ffn_exp_b2):
    import jax
    import jax.numpy as jnp

    def _L0_xattn_ref(x, latents, gamma_x, beta_x, gamma_l, beta_l, Wq, Wkv, Wo):
        import jax, jax.numpy as jnp
        import numpy as np
        DIM = 256
        HEAD_DIM = 64
        NUM_HEADS = 8
        INNER = HEAD_DIM * NUM_HEADS
        ROT_DIM = HEAD_DIM
        ROPE_BASE = 10000.0
        EPS = 1e-05

        def layer_norm(x, g, b):
            mu = jnp.mean(x, axis=-1, keepdims=True)
            var = jnp.var(x, axis=-1, keepdims=True)
            return (x - mu) * jax.lax.rsqrt(var + EPS) * g + b

        def rope_rotate_k(k):
            n = k.shape[1]
            half = ROT_DIM // 2
            inv_freq = 1.0 / ROPE_BASE ** (jnp.arange(0, ROT_DIM, 2, dtype=jnp.float32) / ROT_DIM)
            theta = jnp.arange(n, dtype=jnp.float32)[:, None] * inv_freq[None, :]
            angles = jnp.concatenate([theta, theta], axis=-1)
            cos = jnp.cos(angles)[None, :, None, :].astype(k.dtype)
            sin = jnp.sin(angles)[None, :, None, :].astype(k.dtype)
            k_rope, k_pass = (k[..., :ROT_DIM], k[..., ROT_DIM:])
            neg_half = jnp.concatenate([-k_rope[..., half:], k_rope[..., :half]], axis=-1)
            k_rope = k_rope * cos + neg_half * sin
            return jnp.concatenate([k_rope, k_pass], axis=-1)
        b, n, _ = x.shape
        m = latents.shape[1]
        h, d = (NUM_HEADS, HEAD_DIM)
        scale = d ** (-0.5)
        xn = layer_norm(x, gamma_x, beta_x)
        ln = layer_norm(latents, gamma_l, beta_l)
        q = (ln @ Wq).reshape(b, m, h, d)
        kv_x = xn @ Wkv
        k_x, v_x = (kv_x[..., :INNER], kv_x[..., INNER:])
        kv_l = ln @ Wkv
        k_l, v_l = (kv_l[..., :INNER], kv_l[..., INNER:])
        k_x = k_x.reshape(b, n, h, d)
        v_x = v_x.reshape(b, n, h, d)
        k_x = rope_rotate_k(k_x)
        q = jnp.transpose(q, (0, 2, 1, 3)) * scale
        k_x = jnp.transpose(k_x, (0, 2, 1, 3))
        v_x = jnp.transpose(v_x, (0, 2, 1, 3))
        k_l = jnp.transpose(k_l.reshape(b, m, h, d), (0, 2, 1, 3))
        v_l = jnp.transpose(v_l.reshape(b, m, h, d), (0, 2, 1, 3))
        k = jnp.concatenate([k_x, k_l], axis=2)
        v = jnp.concatenate([v_x, v_l], axis=2)
        sim = jnp.einsum('bhid,bhjd->bhij', q, k)
        attn = jax.nn.softmax(sim, axis=-1)
        out = jnp.einsum('bhij,bhjd->bhid', attn, v)
        out = jnp.transpose(out, (0, 2, 1, 3)).reshape(b, m, INNER)
        return out @ Wo

    def _L0_attn_ref(x, in_proj_w, conv_w, conv_b, dt_bias, A_log, D, norm_w, out_proj_w):
        import jax, jax.numpy as jnp
        import numpy as np
        D_MODEL = 256
        HEADDIM = 64
        EXPAND = 2
        D_STATE = 128
        D_CONV = 4
        NGROUPS = 1
        D_INNER = EXPAND * D_MODEL
        NHEADS = D_INNER // HEADDIM
        CONV_DIM = D_INNER + 2 * NGROUPS * D_STATE
        D_IN_PROJ = 2 * D_INNER + 2 * NGROUPS * D_STATE + NHEADS
        BATCH = 2
        SEQLEN = 256
        EPS = 1e-05

        def silu(v):
            return v * jax.nn.sigmoid(v)

        def _mamba2(x, in_proj_w, conv_w, conv_b, dt_bias, A_log, D, norm_w, out_proj_w):
            b, l, _ = x.shape
            zxbcdt = x @ in_proj_w.T
            z, xBC, dt = jnp.split(zxbcdt, [D_INNER, D_INNER + CONV_DIM], axis=-1)
            dt = jax.nn.softplus(dt + dt_bias)
            rhs = conv_w.T[:, None, :]
            xBC = jax.lax.conv_general_dilated(xBC, rhs, window_strides=(1,), padding=[(D_CONV - 1, 0)], dimension_numbers=('NWC', 'WIO', 'NWC'), feature_group_count=CONV_DIM)
            xBC = silu(xBC + conv_b)
            xs, Bm, Cm = jnp.split(xBC, [D_INNER, D_INNER + D_STATE], axis=-1)
            xs = xs.reshape(b, l, NHEADS, HEADDIM)
            A = -jnp.exp(A_log)
            dA = jnp.exp(dt * A)

            def step(h, inp):
                dA_t, x_t, B_t, dt_t, C_t = inp
                h = h * dA_t[:, :, None, None] + jnp.einsum('bh,bhp,bn->bhpn', dt_t, x_t, B_t)
                y = jnp.einsum('bhpn,bn->bhp', h, C_t)
                return (h, y)
            h0 = jnp.zeros((b, NHEADS, HEADDIM, D_STATE), x.dtype)
            xs_t = xs.transpose(1, 0, 2, 3)
            _, ys = jax.lax.scan(step, h0, (dA.transpose(1, 0, 2), xs_t, Bm.transpose(1, 0, 2), dt.transpose(1, 0, 2), Cm.transpose(1, 0, 2)))
            y = ys.transpose(1, 0, 2, 3) + D[None, None, :, None] * xs
            y = y.reshape(b, l, D_INNER)
            y = y * silu(z)
            y = y * jax.lax.rsqrt(jnp.mean(y * y, axis=-1, keepdims=True) + EPS) * norm_w
            return y @ out_proj_w.T
        return x + _mamba2(x, in_proj_w, conv_w, conv_b, dt_bias, A_log, D, norm_w, out_proj_w)

    def _L0_ffn_ref(x, ln1_g, ln1_b, ln2_g, ln2_b, Wq, bq, Wk, bk, Wv, bv, Wp, bp, gate_W, gate_b, exp_W1, exp_b1, exp_W2, exp_b2):
        import jax, jax.numpy as jnp
        import numpy as np
        N_HEAD = 16
        NUM_EXPERTS = 8
        TOP_K = 2
        LN_EPS = 1e-05

        def _layernorm(x, g, b):
            mu = jnp.mean(x, axis=-1, keepdims=True)
            var = jnp.mean(jnp.square(x - mu), axis=-1, keepdims=True)
            return (x - mu) * jax.lax.rsqrt(var + LN_EPS) * g + b

        def _attention(h, Wq, bq, Wk, bk, Wv, bv, Wp, bp):
            B, T, D = h.shape
            hd = D // N_HEAD

            def split(z):
                return z.reshape(B, T, N_HEAD, hd).transpose(0, 2, 1, 3)
            q = split(h @ Wq + bq)
            k = split(h @ Wk + bk)
            v = split(h @ Wv + bv)
            att = jnp.einsum('bhqd,bhkd->bhqk', q, k) / jnp.sqrt(jnp.float32(hd))
            causal = jnp.tril(jnp.ones((T, T), bool))
            att = jnp.where(causal, att, -jnp.inf)
            att = jax.nn.softmax(att, axis=-1)
            y = jnp.einsum('bhqk,bhkd->bhqd', att, v)
            y = y.transpose(0, 2, 1, 3).reshape(B, T, D)
            return y @ Wp + bp

        def _token_moe(h, gate_W, gate_b, exp_W1, exp_b1, exp_W2, exp_b2):
            B, T, D = h.shape
            flat = h.reshape(-1, D)
            N = flat.shape[0]
            logits = flat @ gate_W + gate_b
            top_v, top_i = jax.lax.top_k(logits, TOP_K)
            w = jax.nn.softmax(top_v, axis=-1)
            w_full = jnp.zeros((N, NUM_EXPERTS), flat.dtype)
            w_full = w_full.at[jnp.arange(N)[:, None], top_i].add(w)
            out = jnp.zeros_like(flat)
            for e in range(NUM_EXPERTS):
                mid = jax.nn.gelu(flat @ exp_W1[e] + exp_b1[e], approximate=False)
                y_e = mid @ exp_W2[e] + exp_b2[e]
                out = out + w_full[:, e:e + 1] * y_e
            return out.reshape(B, T, D)
        x = x + _attention(_layernorm(x, ln1_g, ln1_b), Wq, bq, Wk, bk, Wv, bv, Wp, bp)
        x = x + _token_moe(_layernorm(x, ln2_g, ln2_b), gate_W, gate_b, exp_W1, exp_b1, exp_W2, exp_b2)
        return x
    x = x + _L0_xattn_ref(ctx_1024, _layernorm(x, axis=-1), L0_xattn_gamma_x, L0_xattn_beta_x, L0_xattn_gamma_l, L0_xattn_beta_l, L0_xattn_Wq, L0_xattn_Wkv, L0_xattn_Wo)
    x = x + _L0_attn_ref(_layernorm(x, axis=-1), L0_attn_in_proj_w, L0_attn_conv_w, L0_attn_conv_b, L0_attn_dt_bias, L0_attn_A_log, L0_attn_D, L0_attn_norm_w, L0_attn_out_proj_w)
    x = x + _L0_ffn_ref(_layernorm(x, axis=-1), L0_ffn_ln1_g, L0_ffn_ln1_b, L0_ffn_ln2_g, L0_ffn_ln2_b, L0_ffn_Wq, L0_ffn_bq, L0_ffn_Wk, L0_ffn_bk, L0_ffn_Wv, L0_ffn_bv, L0_ffn_Wp, L0_ffn_bp, L0_ffn_gate_W, L0_ffn_gate_b, L0_ffn_exp_W1, L0_ffn_exp_b1, L0_ffn_exp_W2, L0_ffn_exp_b2)
    return x

_drawn_inputs = setup_inputs


def setup_inputs(seed=0):
    import zlib

    import numpy as np

    out = dict(_drawn_inputs(seed))
    spreads = {'L0_xattn_gamma_x': (1.0, 0.2),
     'L0_xattn_beta_x': (0.0, 0.1),
     'L0_xattn_gamma_l': (1.0, 0.2),
     'L0_xattn_beta_l': (0.0, 0.352),
     'L0_attn_norm_w': (1.0, 0.2),
     'L0_ffn_ln1_g': (1.0, 0.6),
     'L0_ffn_ln1_b': (0.0, 0.8),
     'L0_ffn_ln2_g': (1.0, 0.6),
     'L0_ffn_ln2_b': (0.0, 0.724),
     'L0_ffn_bq': (0.0, 0.8),
     'L0_ffn_bk': (0.0, 0.8),
     'L0_ffn_bv': (0.0, 0.74),
     'L0_ffn_bp': (0.0, 0.1),
     'L0_ffn_gate_b': (0.0, 0.363),
     'L0_ffn_exp_b1': (0.0, 0.8),
     'L0_ffn_exp_b2': (0.0, 0.346)}
    factors = {'L0_attn_dt_bias': 8.0,
     'L0_attn_A_log': 8.0,
     'L0_ffn_Wq': 8.0,
     'L0_ffn_Wk': 8.0,
     'L0_ffn_Wv': 2.827}
    for name, (base, spread) in spreads.items():
        noise = np.random.default_rng([zlib.crc32(name.encode()), seed]).standard_normal(out[name].shape)
        drawn = base * np.exp(spread * noise) if base else spread * noise
        out[name] = jnp.asarray(drawn.astype(out[name].dtype))
    for name, factor in factors.items():
        out[name] = (out[name] * factor).astype(out[name].dtype)
    return out
```

```python
from contextlib import ExitStack

import concourse.bass as bass
import numpy as np
from concourse import mybir

F32 = mybir.dt.float32
F32R = mybir.dt.float32r
ALU = mybir.AluOpType
ACT = mybir.ActivationFunctionType
AXX = mybir.AxisListType.X

P = 128
B, L, D = 64, 32, 256
S = 257
H, DH = 8, 64
GRP = B * L // P
BPG = P // L
KEYS = S + L
TAIL = KEYS - 256
EPS = 1e-5


def mm3(eng, out, a, b, start, stop):
    eng.matmul(out, a[0], b[0], start=start, stop=False)
    eng.matmul(out, a[0], b[1], start=False, stop=False)
    return eng.matmul(out, a[1], b[0], start=False, stop=stop)


def wait_ahead(dve, sem, value, tick):
    dve.wait_ge(sem, value)
    dve.memset(tick[:, :], 0.0)


def latents_phase(nc, sem, io, X, kv):
    qT, KX, xe = kv["qT"], kv["KX"], kv["xe"]
    C = 4
    with ExitStack() as ctx:
        def sb(name, shape, dt=F32):
            return ctx.enter_context(nc.sbuf_tensor("l_" + name, shape, dt))

        wq = sb("wq", [P, 2, 512])
        wk = sb("wk", [P, 2, 512])
        gb = sb("gb", [P, 4, D])
        ident = sb("ident", [P, P])
        edge = sb("edge", [P, 2])
        last = sb("last", [B, D])
        n1 = sb("n1", [P, GRP, D])
        ln = sb("ln", [P, GRP, D])
        st = sb("st", [P, GRP, 6])
        mv = sb("mv", [P, GRP, 2])
        ve = sb("ve", [P, GRP])
        rs = sb("rs", [P, GRP])
        half = sb("half", [P, GRP])
        st2 = sb("st2", [B, 6])
        mv2 = sb("mv2", [B, 2])
        ve2 = sb("ve2", [B, 2])
        xl = sb("xl", [B, D])
        lnT = sb("lnT", [P, 2, 2, 512])
        lastT = sb("lastT", [P, 2, B])
        t1 = sb("t1", [P, 2, B])
        t2 = sb("t2", [P, 2, B])
        psT = ctx.enter_context(nc.psum_tensor("l_psT", [P, 2, 512], F32))
        psJ = ctx.enter_context(nc.psum_tensor("l_psJ", [P, 4, 512], F32))
        psL = ctx.enter_context(nc.psum_tensor("l_psL", [P, 2, 512], F32))

        x_in, w_in = sem("l_x_in"), sem("l_w_in")
        half_set, stats, aggr, var, rstd = (sem("l_" + n) for n in ("half_set", "stats", "aggr", "var", "rstd"))
        norm, scaled, ln_ready = sem("l_norm"), sem("l_scaled"), sem("l_ln_ready")
        turned, turned_out, proj, proj_out = (sem("l_" + n) for n in ("turned", "turned_out", "proj", "proj_out"))
        stored = sem("l_stored")
        last_ready, last_var, last_rstd, last_t, last_tout, last_k, last_mul, last_keys = (
            sem("l_last" + n) for n in "abcdefgh")
        block = ctx.enter_context(nc.Block())

        @block.sync
        def _(sp):
            sp.dma_start(X[:, :, :], io["x"]).then_inc(x_in, 16)
            for dst, src in ((gb, "gb"), (ident, "ident"), (wq, "wq"), (wk, "wk"), (edge, "edge"), (last, "ctx_last")):
                d = dst.ap() if not hasattr(dst, "__getitem__") else dst
                sp.dma_start(d[tuple(slice(None) for _ in dst.shape)], io[src]).then_inc(w_in, 16)
            for c in range(C):
                sp.wait_ge(ln_ready, c + 1)
                for g in range(4 * c, 4 * c + 4):
                    for b in range(BPG):
                        sp.dma_start(xe[4 * g + b, 0:L, :], ln[L * b:L * b + L, g, :]).then_inc(stored, 16)
            sp.wait_ge(last_ready, 4)
            sp.dma_start(xe[:, L, :], xl[:, :]).then_inc(stored, 16)
            sp.wait_ge(stored, 16 * (B + 1))

        @block.gpsimd
        def _(pool):
            pool.memset(half[:, :], -0.5).then_inc(half_set, 1)
            pool.wait_ge(half_set, 1)
            for i in range(2 * C):
                c = i // 2
                pool.wait_ge(var, i + 1)
                pool.tensor_tensor(rs[:, 4 * c:4 * c + 4], ve[:, 4 * c:4 * c + 4], half[:, 0:4], ALU.pow).then_inc(rstd, 1)
            pool.wait_ge(last_var, 1)
            pool.tensor_tensor(ve2[:, 1:2], ve2[:, 0:1], half[0:B, 0:1], ALU.pow).then_inc(last_rstd, 1)

        @block.vector
        def _(dve):
            dve.wait_ge(x_in, 16)
            dve.wait_ge(w_in, 96)

            def layer_norm(i, c, src, dst):
                for g in range(4 * c, 4 * c + 4):
                    dve.bn_stats(st[:, g, :], src[:, g, :]).then_inc(stats, 1)
                dve.wait_ge(stats, 4 * (i + 1))
                for g in range(4 * c, 4 * c + 4):
                    dve.bn_aggr(mv[:, g, :], st[:, g, :]).then_inc(aggr, 1)
                dve.wait_ge(aggr, 4 * (i + 1))
                dve.tensor_scalar(ve[:, 4 * c:4 * c + 4], mv[:, 4 * c:4 * c + 4, 1], EPS, None, ALU.add).then_inc(var, 1)
                dve.wait_ge(rstd, i + 1)
                for g in range(4 * c, 4 * c + 4):
                    dve.tensor_scalar(dst[:, g, :], src[:, g, :], mv[:, g, 0:1], rs[:, g:g + 1],
                                      ALU.subtract, ALU.mult).then_inc(norm, 1)
                dve.wait_ge(norm, 4 * (i + 1))

            for c in range(C):
                a, z = 4 * c, 4 * c + 4
                layer_norm(2 * c, c, X, n1)
                layer_norm(2 * c + 1, c, n1, ln)
                dve.tensor_tensor(ln[:, a:z, :], ln[:, a:z, :], gb[:, 2:3, :].to_broadcast([P, 4, D]),
                                  ALU.mult).then_inc(scaled, 1)
                dve.wait_ge(scaled, c + 1)
                dve.tensor_tensor(ln[:, a:z, :], ln[:, a:z, :], gb[:, 3:4, :].to_broadcast([P, 4, D]),
                                  ALU.add).then_inc(ln_ready, 1)
            dve.bn_stats(st2[:, :], last[:, :]).then_inc(last_ready, 1)
            dve.wait_ge(last_ready, 1)
            dve.bn_aggr(mv2[:, :], st2[:, :]).then_inc(last_ready, 1)
            dve.wait_ge(last_ready, 2)
            dve.tensor_scalar(ve2[:, 0:1], mv2[:, 1:2], EPS, None, ALU.add).then_inc(last_var, 1)
            dve.scalar_tensor_tensor(xl[:, :], last[:, :], mv2[:, 0:1], gb[0:B, 0, :],
                                     ALU.subtract, ALU.mult).then_inc(last_ready, 1)
            dve.wait_ge(last_ready, 3)
            dve.wait_ge(last_rstd, 1)
            dve.scalar_tensor_tensor(xl[:, :], xl[:, :], ve2[:, 1:2], gb[0:B, 1, :],
                                     ALU.mult, ALU.add).then_inc(last_ready, 1)
            dve.wait_ge(last_k, 1)
            k = psL[:, 1, 0:4 * B].rearrange("p (g a b) -> p g a b", g=2, a=2)
            dve.tensor_scalar(t1[:, :, :], k[:, :, 1, :], edge[:, 1:2], None, ALU.mult).then_inc(last_mul, 1)
            dve.tensor_scalar(t2[:, :, :], k[:, :, 0, :], edge[:, 1:2], None, ALU.mult).then_inc(last_mul, 1)
            dve.wait_ge(last_mul, 2)
            for g in range(2):
                dve.scalar_tensor_tensor(KX[:, 2 * g, :, L], k[:, g, 0, :], edge[:, 0:1], t1[:, g, :],
                                         ALU.mult, ALU.subtract)
                dve.scalar_tensor_tensor(KX[:, 2 * g + 1, :, L], k[:, g, 1, :], edge[:, 0:1], t2[:, g, :],
                                         ALU.mult, ALU.add).then_inc(last_keys, 1)

        @block.tensor
        def _(pe):
            pe.wait_ge(w_in, 96)
            n = 0
            for c in range(C):
                pe.wait_ge(ln_ready, c + 1)
                if c:
                    pe.wait_ge(turned_out, c)
                for k in range(2):
                    for j in range(4):
                        t = pe.transpose(psT[:, k, j * P:(j + 1) * P], ln[:, 4 * c + j, k * P:(k + 1) * P], ident[:, :])
                t.then_inc(turned, 1)
                pe.wait_ge(turned_out, c + 1)
                for w in (wq, wk):
                    for m in range(4):
                        if n >= 4:
                            pe.wait_ge(proj_out, n - 3)
                        for k in range(2):
                            t = pe.matmul(psJ[:, n % 4, :], w[:, k, m * P:(m + 1) * P], lnT[:, c % 2, k, :],
                                          start=(k == 0), stop=(k == 1))
                        t.then_inc(proj, 1)
                        n += 1
            pe.wait_ge(last_ready, 4)
            for k in range(2):
                t = pe.transpose(psL[:, 0, k * B:(k + 1) * B], xl[:, k * P:(k + 1) * P], ident[0:B, 0:B])
            t.then_inc(last_t, 1)
            pe.wait_ge(last_tout, 1)
            for m in range(4):
                for k in range(2):
                    t = pe.matmul(psL[:, 1, m * B:(m + 1) * B], wk[:, k, m * P:(m + 1) * P], lastT[:, k, :],
                                  start=(k == 0), stop=(k == 1))
            t.then_inc(last_k, 1)

        @block.scalar
        def _(act):
            n = 0
            for c in range(C):
                act.wait_ge(turned, c + 1)
                if c >= 2:
                    act.wait_ge(proj, 8 * (c - 1))
                act.activation(lnT[:, c % 2, :, :], psT[:, :, :], ACT.Copy).then_inc(turned_out, 1)
                for w in range(2):
                    for m in range(4):
                        act.wait_ge(proj, n + 1)
                        if w == 0:
                            act.activation(qT[:, m, 512 * c:512 * c + 512], psJ[:, n % 4, :], ACT.Copy,
                                           scale=DH ** -0.5).then_inc(proj_out, 1)
                        else:
                            act.activation(KX[:, m, 16 * c:16 * c + 16, 0:L],
                                           psJ[:, n % 4, :].rearrange("p (b i) -> p b i", i=L),
                                           ACT.Copy).then_inc(proj_out, 1)
                        n += 1
            act.wait_ge(last_t, 1)
            act.activation(lastT[:, :, :], psL[:, 0, 0:2 * B].rearrange("p (k b) -> p k b", k=2),
                           ACT.Copy).then_inc(last_tout, 1)


def xattn_phase(nc, sem, io, X, kv):
    qT, KX, xe = kv["qT"], kv["KX"], kv["xe"]
    with ExitStack() as ctx:
        def sb(name, shape, dt=F32):
            return ctx.enter_context(nc.sbuf_tensor("a_" + name, shape, dt))

        def pb(name, shape):
            return ctx.enter_context(nc.psum_tensor("a_" + name, shape, F32))

        wk = sb("wk", [P, 2, 512])
        wkh, wkl = sb("wkh", [P, 2, 512], F32R), sb("wkl", [P, 2, 512], F32R)
        wv = sb("wv", [P, 2, 512])
        wo = sb("wo", [P, 4, D])
        gb = sb("gb", [P, 4, D])
        ident = sb("ident", [P, P])
        cos = sb("cos", [P, 256])
        sin = sb("sin", [P, 2, 256])
        C = [sb(f"C{i}", [P, 2, D]) for i in range(2)]
        cen = [sb(f"cen{i}", [P, 2, D]) for i in range(2)]
        xn = [sb(f"xn{i}", [P, 2, D]) for i in range(4)]
        xt = [sb(f"xt{i}", [TAIL, D]) for i in range(4)]
        xh = [sb(f"xh{i}", [P, 2, 256], F32R) for i in range(2)]
        xl = [sb(f"xl{i}", [P, 2, 256], F32R) for i in range(2)]
        st = [sb(f"st{i}", [P, 2, 6]) for i in range(2)]
        mv = [sb(f"mv{i}", [P, 2, 2]) for i in range(2)]
        ve = [sb(f"ve{i}", [P, 2]) for i in range(2)]
        rs = [sb(f"rs{i}", [P, 2]) for i in range(2)]
        tick = sb("tick", [P, 1])
        half = sb("half", [P, 2])
        r1 = [sb(f"r1{i}", [P, 2, 256]) for i in range(2)]
        r2 = [sb(f"r2{i}", [P, 2, 256]) for i in range(2)]
        K = [sb(f"K{i}", [P, 4, KEYS]) for i in range(2)]
        Q = [sb(f"Q{i}", [P, 4, P]) for i in range(2)]
        mx = [sb(f"mx{i}", [P, 2]) for i in range(2)]
        nm = [sb(f"nm{i}", [P, 2]) for i in range(2)]
        sm = [sb(f"sm{i}", [P, 2]) for i in range(2)]
        ri = [sb(f"ri{i}", [P, 2]) for i in range(2)]
        pr = [sb(f"pr{i}", [P, 2, KEYS]) for i in range(2)]
        pT = [sb(f"pT{i}", [P, 3, 256]) for i in range(2)]
        px = sb("px", [P, 2, H, BPG, L])
        uT = sb("uT", [P, 4, P])

        psT = pb("psT", [P, 2, 256])
        psK = [pb(f"psK{i}", [P, 2, 256]) for i in range(2)]
        psS = [pb(f"psS{i}", [P, 512]) for i in range(2)]
        psP = [pb(f"psP{i}", [P, 512]) for i in range(2)]
        psV = pb("psV", [P, 512])

        names = ("w_in", "w_hi", "w_lo", "half_set", "zeroed", "stats", "aggr", "var", "rstd", "centred", "normed",
                 "turned", "xt_hi", "xt_lo", "projected", "rotated", "keys", "tails", "blocks", "scored", "peak",
                 "peak_neg", "exped", "recip", "probs", "pturned", "pt_out", "attended", "px_out", "valued", "u_out",
                 "outed", "added")
        s = {n: sem("a_" + n) for n in names}
        c_in = [sem(f"a_c_in{i}") for i in range(2)]
        t_in = [sem(f"a_t_in{i}") for i in range(4)]
        block = ctx.enter_context(nc.Block())
        LASTG = GRP - 1


        @block.sync
        def _(sp):
            for dst, src in ((wk, "wk"), (gb, "gb"), (ident, "ident"), (cos, "cos"), (wv, "wv")):
                sp.dma_start(dst[tuple(slice(None) for _ in dst.shape)], io[src]).then_inc(s["w_in"], 16)
            sp.dma_start(sin[:, :, :], io["sin"]).then_inc(s["w_in"], 16)
            sp.dma_start(wo[:, :, :], io["wo"]).then_inc(s["w_in"], 16)

            def load(g, j, first=False):
                n = 4 * g + j
                if not (first and j < 2):
                    sp.wait_ge(s["normed"], n - 1)
                sp.dma_start(C[j % 2][:, :, :], io["ctx"][n]).then_inc(c_in[j % 2], 16)
                if not first:
                    sp.wait_ge(s["attended"], n - 3)
                sp.dma_start(xt[j][:, :], xe[n]).then_inc(t_in[j], 16)

            for j in range(4):
                load(0, j, True)
            with sp.Fori(1, GRP) as g:
                for j in range(4):
                    load(g, j)

        @block.gpsimd
        def _(pool):
            pool.memset(half[:, :], -0.5).then_inc(s["half_set"], 1)
            for i in range(2):
                pool.memset(Q[i][:, :, :], 0.0).then_inc(s["zeroed"], 1)
            pool.wait_ge(s["half_set"], 1)

            def power(g, j):
                n = 4 * g + j
                pool.wait_ge(s["var"], n + 1)
                pool.tensor_tensor(rs[j % 2][:, :], ve[j % 2][:, :], half[:, :], ALU.pow).then_inc(s["rstd"], 1)

            def rope_add(g, j, G, first=False):
                n = 4 * g + j
                if not (first and j < 2) and G == 0:
                    pool.wait_ge(s["scored"], 2 * (n - 1))
                pool.wait_ge(s["rotated"], 3 * (2 * n + G + 1))
                pool.tensor_tensor(K[j % 2][:, 2 * G:2 * G + 2, 0:256], r1[G][:, :, :], r2[G][:, :, :],
                                   ALU.add).then_inc(s["keys"], 1)

            def slot(g, j, first=False, last=False):
                rope_add(g, j, 0, first)
                if not (last and j >= 2):
                    power(g, j + 2) if j < 2 else power(g + 1, j - 2)
                rope_add(g, j, 1, first)

            power(0, 0)
            power(0, 1)
            for j in range(4):
                slot(0, j, first=True)
            with pool.Fori(1, LASTG) as g:
                for j in range(4):
                    slot(g, j)
            for j in range(4):
                slot(LASTG, j, last=True)

        @block.vector
        def _(dve):
            dve.wait_ge(s["w_in"], 16 * 7)
            dve.tensor_copy(wkh[:, :, :], wk[:, :, :]).then_inc(s["w_hi"], 1)
            dve.wait_ge(s["w_hi"], 1)
            dve.tensor_tensor(wkl[:, :, :], wk[:, :, :], wkh[:, :, :].bitcast(F32), ALU.subtract).then_inc(s["w_lo"], 1)

            def statistics(g, j):
                n = 4 * g + j
                dve.wait_ge(c_in[j % 2], 16 * (2 * g + j // 2 + 1))
                for t in range(2):
                    dve.bn_stats(st[j % 2][:, t, :], C[j % 2][:, t, :]).then_inc(s["stats"], 1)
                wait_ahead(dve, s["stats"], 2 * (n + 1), tick)
                for t in range(2):
                    dve.bn_aggr(mv[j % 2][:, t, :], st[j % 2][:, t, :]).then_inc(s["aggr"], 1)
                dve.wait_ge(s["aggr"], 2 * (n + 1))
                dve.tensor_scalar(ve[j % 2][:, :], mv[j % 2][:, :, 1], EPS, None, ALU.add).then_inc(s["var"], 1)

            def normalise(g, j, first=False):
                n = 4 * g + j
                for t in range(2):
                    dve.scalar_tensor_tensor(cen[j % 2][:, t, :], C[j % 2][:, t, :], mv[j % 2][:, t, 0:1], gb[:, 0, :],
                                             ALU.subtract, ALU.mult).then_inc(s["centred"], 1)
                dve.wait_ge(s["rstd"], n + 1)
                dve.wait_ge(s["centred"], 2 * (n + 1))
                if not first:
                    dve.wait_ge(s["attended"], n - 3)
                dve.scalar_tensor_tensor(xn[j][:, 0, :], cen[j % 2][:, 0, :], rs[j % 2][:, 0:1], gb[:, 1, :],
                                         ALU.mult, ALU.add)
                dve.scalar_tensor_tensor(xn[j][:, 1, :], cen[j % 2][:, 1, :], rs[j % 2][:, 1:2], gb[:, 1, :],
                                         ALU.mult, ALU.add).then_inc(s["normed"], 1)

            def low(g, j):
                n = 4 * g + j
                dve.wait_ge(s["xt_hi"], n + 1)
                dve.tensor_tensor(xl[j % 2][:, :, :], psT[:, :, :], xh[j % 2][:, :, :].bitcast(F32),
                                  ALU.subtract).then_inc(s["xt_lo"], 1)

            def rotate(g, j, G, first=False):
                n = 4 * g + j
                dve.wait_ge(s["projected"], 2 * n + G + 1)
                if not (first and j == 0):
                    dve.wait_ge(s["keys"], 2 * n + G - 1)
                dve.tensor_tensor(r1[G][:, :, :], psK[G][:, :, :], cos[:, :].unsqueeze(1).to_broadcast([P, 2, 256]),
                                  ALU.mult).then_inc(s["rotated"], 1)
                for a in range(2):
                    dve.tensor_tensor(r2[G][:, a, :], psK[G][:, 1 - a, :], sin[:, a, :], ALU.mult).then_inc(s["rotated"], 1)

            def peaks(g, j):
                n = 4 * g + j
                for G in range(2):
                    dve.wait_ge(s["scored"], 2 * n + G + 1)
                    dve.reduce_max(mx[j % 2][:, G:G + 1], psS[G][:, 0:KEYS], AXX).then_inc(s["peak"], 1)
                dve.wait_ge(s["peak"], 2 * (n + 1))
                dve.tensor_scalar(nm[j % 2][:, :], mx[j % 2][:, :], -1.0, None, ALU.mult).then_inc(s["peak_neg"], 1)

            def shares(g, j):
                n = 4 * g + j
                dve.wait_ge(s["exped"], 2 * (n + 1))
                dve.reciprocal(ri[j % 2][:, :], sm[j % 2][:, :]).then_inc(s["recip"], 1)
                dve.wait_ge(s["recip"], n + 1)
                for G in range(2):
                    dve.tensor_scalar(pr[j % 2][:, G, :], pr[j % 2][:, G, :], ri[j % 2][:, G:G + 1], None,
                                      ALU.mult).then_inc(s["probs"], 1)

            def residual(g):
                dve.wait_ge(s["outed"], g + 1)
                dve.tensor_tensor(X[:, g, :], X[:, g, :], psV[:, 0:D], ALU.add).then_inc(s["added"], 1)

            def slot(g, j, first=False, last=False, batches=(True, True)):
                prev = (g, j - 1) if j else (g - 1, 3)
                if batches[0] and not (last and j >= 2):
                    statistics(g + (j + 2) // 4, (j + 2) % 4)
                if batches[0]:
                    rotate(g, j, 0, first)
                if batches[1] and not (first and j == 0):
                    peaks(*prev)
                if batches[0] and not (last and j == 3):
                    low(g + (j + 1) // 4, (j + 1) % 4)
                if batches[1] and not (first and j == 0):
                    shares(*prev)
                if j == 2 and not first:
                    residual(g - 1)
                if batches[0]:
                    rotate(g, j, 1, first)
                if batches[0] and not (last and j >= 2):
                    normalise(g + (j + 2) // 4, (j + 2) % 4, first and j < 2)

            for j in range(2):
                statistics(0, j)
            for j in range(2):
                normalise(0, j, True)
            low(0, 0)
            for j in range(4):
                slot(0, j, first=True)
            with dve.Fori(1, LASTG) as g:
                for j in range(4):
                    slot(g, j)
            for j in range(4):
                slot(LASTG, j, last=True)
            slot(GRP, 0, batches=(False, True))
            slot(GRP, 2, batches=(False, False))

        @block.scalar
        def _(act):
            act.wait_ge(s["zeroed"], 2)

            def operands(g, j, first=False):
                n = 4 * g + j
                if not (first and j < 2):
                    act.wait_ge(s["scored"], 2 * (n - 1))
                act.activation(K[j % 2][:, :, 256:KEYS], KX[:, :, n, :], ACT.Copy).then_inc(s["tails"], 1)
                for h in range(4):
                    act.activation(Q[j % 2][32 * h:32 * h + 32, :, 32 * h:32 * h + 32],
                                   qT[32 * h:32 * h + 32, :, bass.ds(n * L, L)], ACT.Copy).then_inc(s["blocks"], 1)

            def high(g, j, first=False):
                n = 4 * g + j
                act.wait_ge(s["turned"], n + 1)
                if not (first and j < 2):
                    act.wait_ge(s["projected"], 2 * (n - 1))
                act.activation(xh[j % 2][:, :, :], psT[:, :, :], ACT.Copy).then_inc(s["xt_hi"], 1)

            def exps(g, j, first=False):
                n = 4 * g + j
                act.wait_ge(s["peak_neg"], n + 1)
                if not (first and j < 2):
                    act.wait_ge(s["pturned"], 2 * (n - 1))
                for G in range(2):
                    act.activation(pr[j % 2][:, G, :], psS[G][:, 0:KEYS], ACT.Exp, bias=nm[j % 2][:, G:G + 1],
                                   accum_out=sm[j % 2][:, G:G + 1]).then_inc(s["exped"], 1)

            def turned_probs(g, j, first=False):
                n = 4 * g + j
                if not (first and j < 2):
                    act.wait_ge(s["attended"], n - 1)
                for G in range(2):
                    act.wait_ge(s["pturned"], 2 * n + G + 1)
                    p3 = psP[G][:, 0:384].rearrange("p (t c) -> p t c", t=3)
                    act.activation(pT[j % 2][:, 0:2, G * P:(G + 1) * P], p3[:, 0:2, :], ACT.Copy).then_inc(s["pt_out"], 1)
                    act.activation(pT[j % 2][0:TAIL, 2, G * P:(G + 1) * P], p3[0:TAIL, 2, :],
                                   ACT.Copy).then_inc(s["pt_out"], 1)

            def mixed(g, j, first=False):
                n = 4 * g + j
                act.wait_ge(s["attended"], n + 1)
                if j == 0 and not first:
                    act.wait_ge(s["valued"], g)
                for k in range(2):
                    act.activation(px[:, k, :, j, :], psV[:, 256 * k:256 * k + 256].rearrange("p (h i) -> p h i", h=H),
                                   ACT.Copy).then_inc(s["px_out"], 1)

            def values(g):
                act.wait_ge(s["valued"], g + 1)
                act.activation(uT[:, :, :], psV[:, :].rearrange("p (m t) -> p m t", m=4), ACT.Copy).then_inc(s["u_out"], 1)

            def slot(g, j, first=False, last=False, batches=(True, True)):
                prev = (g, j - 1) if j else (g - 1, 3)
                prev2 = (g, j - 2) if j >= 2 else (g - 1, j + 2)
                if j == 2 and not first:
                    values(g - 1)
                if batches[0]:
                    operands(g, j, first)
                if batches[0] and not (last and j == 3):
                    high(g + (j + 1) // 4, (j + 1) % 4, first and j == 0)
                if batches[1] and not (first and j == 0):
                    exps(*prev, first and j - 1 < 2)
                if not (first and j < 2) and not (not batches[0] and j == 2):
                    turned_probs(*prev2, first)
                    mixed(*prev2, first)

            high(0, 0, True)
            for j in range(4):
                slot(0, j, first=True)
            with act.Fori(1, LASTG) as g:
                for j in range(4):
                    slot(g, j)
            for j in range(4):
                slot(LASTG, j, last=True)
            slot(GRP, 0, batches=(False, True))
            slot(GRP, 1, batches=(False, False))
            slot(GRP, 2, batches=(False, False))

        @block.tensor
        def _(pe):
            pe.wait_ge(s["w_lo"], 1)

            def turn(g, j, first=False):
                n = 4 * g + j
                pe.wait_ge(s["normed"], n + 1)
                if not (first and j == 0):
                    pe.wait_ge(s["xt_lo"], n)
                for k in range(2):
                    for t in range(2):
                        i = pe.transpose(psT[:, k, t * P:(t + 1) * P], xn[j][:, t, k * P:(k + 1) * P], ident[:, :])
                i.then_inc(s["turned"], 1)

            def project(g, j, G, first=False):
                n = 4 * g + j
                if G == 0:
                    pe.wait_ge(s["xt_lo"], n + 1)
                if not (first and j == 0):
                    pe.wait_ge(s["rotated"], 3 * (2 * n + G - 1))
                for a in range(2):
                    m = 2 * G + a
                    for k in range(2):
                        i = mm3(pe, psK[G][:, a, :], (wkh[:, k, m * P:(m + 1) * P], wkl[:, k, m * P:(m + 1) * P]),
                                (xh[j % 2][:, k, :], xl[j % 2][:, k, :]), k == 0, k == 1)
                i.then_inc(s["projected"], 1)

            def score(g, j, first=False):
                n = 4 * g + j
                pe.wait_ge(s["tails"], n + 1)
                pe.wait_ge(s["blocks"], 4 * (n + 1))
                for G in range(2):
                    pe.wait_ge(s["keys"], 2 * n + G + 1)
                    if not (first and j == 0):
                        pe.wait_ge(s["exped"], 2 * n + G - 1)
                    for a in range(2):
                        i = pe.matmul(psS[G][:, 0:KEYS], Q[j % 2][:, 2 * G + a, :], K[j % 2][:, 2 * G + a, :],
                                      start=(a == 0), stop=(a == 1))
                    i.then_inc(s["scored"], 1)

            def turn_probs(g, j, first=False):
                n = 4 * g + j
                pe.wait_ge(s["probs"], 2 * (n + 1))
                for G in range(2):
                    if not (first and j == 0):
                        pe.wait_ge(s["pt_out"], 2 * (2 * n + G - 1))
                    for t in range(3):
                        w = P if t < 2 else TAIL
                        i = pe.transpose(psP[G][0:w, t * P:(t + 1) * P], pr[j % 2][:, G, t * P:t * P + w], ident[:, :])
                    i.then_inc(s["pturned"], 1)

            def attend(g, j, first=False):
                n = 4 * g + j
                pe.wait_ge(s["pt_out"], 4 * (n + 1))
                pe.wait_ge(t_in[j], 16 * (g + 1))
                if not (first and j == 0):
                    pe.wait_ge(s["px_out"], 2 * n)
                for k in range(2):
                    for t in range(3):
                        w, v = (P, xn[j][:, t, k * P:(k + 1) * P]) if t < 2 else (TAIL, xt[j][:, k * P:(k + 1) * P])
                        i = pe.matmul(psV[:, 256 * k:256 * k + 256], v, pT[j % 2][0:w, t, :], start=(t == 0), stop=(t == 2))
                i.then_inc(s["attended"], 1)

            def value(g):
                pe.wait_ge(s["px_out"], 8 * (g + 1))
                for h in range(H):
                    for k in range(2):
                        i = pe.matmul(psV[64 * (h % 2):64 * (h % 2) + 64, P * (h // 2):P * (h // 2) + P],
                                      wv[:, k, DH * h:DH * h + DH], px[:, k, h, :, :], start=(k == 0), stop=(k == 1))
                i.then_inc(s["valued"], 1)

            def out(g):
                pe.wait_ge(s["u_out"], g + 1)
                for m in range(4):
                    i = pe.matmul(psV[:, 0:D], uT[:, m, :], wo[:, m, :], start=(m == 0), stop=(m == 3))
                i.then_inc(s["outed"], 1)

            def slot(g, j, first=False, last=False, batches=(True, True)):
                prev = (g, j - 1) if j else (g - 1, 3)
                prev2 = (g, j - 2) if j >= 2 else (g - 1, j + 2)
                if batches[0]:
                    project(g, j, 0, first)
                if j == 2 and not first:
                    value(g - 1)
                if batches[1] and not (first and j == 0):
                    score(*prev, first)
                if batches[0] and not (last and j == 3):
                    turn(g + (j + 1) // 4, (j + 1) % 4)
                if j == 2 and not first:
                    out(g - 1)
                attends = not (first and j < 2) and not (not batches[0] and j == 2)
                if attends:
                    turn_probs(*prev2, first)
                if batches[0]:
                    project(g, j, 1, first)
                if attends:
                    if j == 2 and not first:
                        pe.wait_ge(s["added"], g)
                    attend(*prev2, first)

            turn(0, 0, True)
            for j in range(4):
                slot(0, j, first=True)
            with pe.Fori(1, LASTG) as g:
                for j in range(4):
                    slot(g, j)
            for j in range(4):
                slot(LASTG, j, last=True)
            slot(GRP, 0, batches=(False, True))
            slot(GRP, 1, batches=(False, False))
            slot(GRP, 2, batches=(False, False))

DI, NH, CONVT, ZT = 512, 8, 6, 4


def past(eng, sem, value):
    if isinstance(value, int) and value <= 0:
        return
    eng.wait_ge(sem, value)


def slots(eng, slot, units, peeled, depth):
    for n in range(peeled):
        slot(n, n % 2)
    with eng.Fori(peeled // 2, units // 2 - 1) as i:
        slot(2 * i, 0)
        slot(2 * i + 1, 1)
    for n in range(units - 2, units + depth):
        slot(n, n % 2)


def unit(n):
    return not isinstance(n, int) or 0 <= n < GRP


def mamba_phase(nc, sem, io, X):
    with ExitStack() as ctx:
        def sb(name, shape, dt=F32):
            return ctx.enter_context(nc.sbuf_tensor("m_" + name, shape, dt))

        def pb(name, shape):
            return ctx.enter_context(nc.psum_tensor("m_" + name, shape, F32))

        DIN = 2 * DI + 2 * P
        w = sb("w", [P, 2, DIN + NH])
        wh, wl = sb("wh", [P, 2, DIN], F32R), sb("wl", [P, 2, DIN], F32R)
        wout = sb("wout", [P, 4, D])
        ident = sb("ident", [P, P])
        tri = sb("tri", [P, P])
        aft = sb("aft", [P, P])
        cols = sb("cols", [P, CONVT * 5 + 8])
        rows = sb("rows", [P, 2, NH])
        A = sb("A", [P, NH])
        tick = sb("tick", [P, 1])
        half = sb("half", [P, 1])
        ones = sb("ones", [P, 1])
        xn = [sb(f"xn{i}", [P, D]) for i in range(2)]
        xh = [sb(f"xh{i}", [P, 2, P], F32R) for i in range(2)]
        xl = [sb(f"xl{i}", [P, 2, P], F32R) for i in range(2)]
        st = sb("st", [P, 2, 6])
        mv = sb("mv", [P, 2, 2])
        ve = sb("ve", [P, 2])
        rs = sb("rs", [P, 2])
        pad = sb("pad", [P, CONVT, BPG, L + 3])
        acc = sb("acc", [P, CONVT, P])
        xa = [sb(f"xa{i}", [P, CONVT, P]) for i in range(2)]
        zs = [sb(f"zs{i}", [P, ZT, P]) for i in range(2)]
        sp = sb("sp", [P, 8, NH])
        dt = sb("dt", [P, GRP, NH])
        da = sb("da", [P, GRP, NH])
        ta = sb("ta", [P, NH, P])
        dec = sb("dec", [P, NH, P])
        gm = sb("gm", [P, P])
        mm = sb("mm", [P, NH, P])
        xd = sb("xd", [P, DI])
        yd = sb("yd", [P, ZT, P])
        yz = [sb(f"yz{i}", [P, ZT, P]) for i in range(2)]
        y2 = [sb(f"y2{i}", [P, ZT, P]) for i in range(2)]
        fe = sb("fe", [P, 2])
        fr = sb("fr", [P, 2])

        psT = pb("psT", [P, 512])
        psA = pb("psA", [P, 4, P])
        psB = pb("psB", [P, 512])
        psO = pb("psO", [P, 512])
        psL = pb("psL", [P, 2, 4, P])
        psX = pb("psX", [P, 512])
        psY = pb("psY", [P, 4, P])
        DT, SS = psT[:, 256:256 + NH], psO[:, 256:257]

        s = {n: sem("m_" + n) for n in (
            "w_in", "w_hi", "w_lo", "consts", "a_exp", "a_set", "wout_set",
            "stats", "aggr", "var", "rstd", "xn", "added", "turned", "xt_hi", "xt_lo",
            "projA", "projB", "projZ", "dt_mm", "padA", "padB", "tap", "taps", "conv", "xact", "zact",
            "sp_v", "sp_n", "sp_min", "sp_exp", "sp_u", "sp_ln", "sp_c", "sp_s", "dt", "da",
            "ta", "logs", "dec", "cb", "gm", "mm", "xturn", "xd", "y", "yd", "yz", "y2",
            "out", "f_var", "f_rstd", "f_out")}
        block = ctx.enter_context(nc.Block())
        WIN = 7
        tap = lambda m, k: cols[:, 4 * m + k:4 * m + k + 1]
        cbias = lambda m: cols[:, 24 + m:25 + m]
        skip = lambda q: cols[:, 30 + q:31 + q]
        normw = lambda q: cols[:, 34 + q:35 + q]

        @block.sync
        def _(sy):
            for d, src in ((w, "m_w"), (cols, "m_cols"), (rows, "m_rows"), (ident, "ident"), (tri, "tri"), (aft, "aft"),
                           (wout, "m_out")):
                sy.dma_start(d[tuple(slice(None) for _ in d.shape)], io[src]).then_inc(s["w_in"], 16)
            sy.wait_ge(s["w_in"], 16 * WIN)

        @block.gpsimd
        def _(pool):
            pool.memset(half[:, :], -0.5).then_inc(s["consts"], 1)
            pool.memset(ones[:, :], 1.0).then_inc(s["consts"], 1)
            pool.memset(pad[:, :, :, :], 0.0).then_inc(s["consts"], 1)
            pool.wait_ge(s["consts"], 3)
            pool.wait_ge(s["w_in"], 16 * WIN)

            def ln_power(n, p):
                if not unit(n):
                    return
                pool.wait_ge(s["var"], n + 1)
                pool.tensor_tensor(rs[:, p:p + 1], ve[:, p:p + 1], half[:, :], ALU.pow).then_inc(s["rstd"], 1)

            def ln_add(n, p):
                if not unit(n):
                    return
                pool.wait_ge(s["xn"], n + 1)
                pool.tensor_tensor(X[:, n, :], X[:, n, :], xn[p][:, :], ALU.add).then_inc(s["added"], 1)

            def decays(n):
                if not unit(n):
                    return
                pool.wait_ge(s["da"], n + 1)
                past(pool, s["logs"], n)
                pool.tensor_tensor(ta[:, :, :], tri[:, :].unsqueeze(1).to_broadcast([P, NH, P]),
                                   da[:, n, :].unsqueeze(2).to_broadcast([P, NH, P]), ALU.mult).then_inc(s["ta"], 1)

            def out_power(n, p):
                if not unit(n):
                    return
                pool.wait_ge(s["f_var"], n + 1)
                pool.tensor_tensor(fr[:, p:p + 1], fe[:, p:p + 1], half[:, :], ALU.pow).then_inc(s["f_rstd"], 1)

            def gate(n, p):
                if not unit(n):
                    return
                pool.wait_ge(s["yd"], 4 * (n + 1))
                pool.wait_ge(s["zact"], n + 1)
                past(pool, s["out"], n - 1)
                past(pool, s["y2"], n - 1)
                pool.tensor_tensor(yz[p][:, :, :], yd[:, :, :], zs[p][:, :, :], ALU.mult).then_inc(s["yz"], 1)

            def slot(n, p):
                out_power(n - 2, p)
                ln_power(n + 2, p)
                decays(n)
                ln_add(n + 2, p)
                gate(n - 1, 1 - p)

            for n in range(2):
                ln_power(n, n)
                ln_add(n, n)
            slots(pool, slot, GRP, 4, 2)

        @block.vector
        def _(dve):
            dve.wait_ge(s["w_in"], 16 * WIN)
            dve.wait_ge(s["consts"], 3)
            dve.tensor_copy(wh[:, :, :], w[:, :, 0:DIN]).then_inc(s["w_hi"], 1)
            dve.wait_ge(s["w_hi"], 1)
            dve.tensor_tensor(wl[:, :, :], w[:, :, 0:DIN], wh[:, :, :].bitcast(F32), ALU.subtract).then_inc(s["w_lo"], 1)
            for q in range(4):
                dve.tensor_scalar(wout[:, q, :], wout[:, q, :], normw(q), None, ALU.mult).then_inc(s["wout_set"], 1)
            dve.wait_ge(s["a_exp"], 1)
            dve.tensor_scalar(A[:, :], A[:, :], -1.0, None, ALU.mult).then_inc(s["a_set"], 1)

            def ln_stats(n, p):
                if not unit(n):
                    return
                dve.bn_stats(st[:, p, :], X[:, n, :]).then_inc(s["stats"], 1)
                wait_ahead(dve, s["stats"], n + 1, tick)
                dve.bn_aggr(mv[:, p, :], st[:, p, :]).then_inc(s["aggr"], 1)
                dve.wait_ge(s["aggr"], n + 1)
                dve.tensor_scalar(ve[:, p:p + 1], mv[:, p, 1:2], EPS, None, ALU.add).then_inc(s["var"], 1)

            def ln_apply(n, p):
                if not unit(n):
                    return
                dve.wait_ge(s["rstd"], n + 1)
                past(dve, s["turned"], n - 1)
                past(dve, s["added"], n - 1)
                dve.tensor_scalar(xn[p][:, :], X[:, n, :], mv[:, p, 0:1], rs[:, p:p + 1],
                                  ALU.subtract, ALU.mult).then_inc(s["xn"], 1)

            def low(n, p):
                if not unit(n):
                    return
                dve.wait_ge(s["xt_hi"], n + 1)
                dve.tensor_tensor(xl[p][:, :, :], psT[:, 0:256].rearrange("p (k t) -> p k t", k=2),
                                  xh[p][:, :, :].bitcast(F32), ALU.subtract).then_inc(s["xt_lo"], 1)

            def conv(n, tiles, padded):
                if not unit(n):
                    return
                dve.wait_ge(s[padded], n + 1)
                for k in range(2, -1, -1):
                    for m in tiles:
                        if k == 2:
                            dve.wait_ge(s["tap"], CONVT * n + m + 1)
                        else:
                            dve.wait_ge(s["taps"], 3 * CONVT * n + 3 * tiles[0] + (m - tiles[0]) + len(tiles) * (1 - k) + 1)
                        a = acc[:, m, :].rearrange("p (b t) -> p b t", t=L)
                        dve.scalar_tensor_tensor(a, pad[:, m, :, k:k + L], tap(m, k), a, ALU.mult, ALU.add).then_inc(s["taps"], 1)

            def softplus_a(n):
                if not unit(n):
                    return
                dve.wait_ge(s["dt_mm"], n + 1)
                past(dve, s["dt"], n)
                dve.tensor_tensor(sp[:, 0, :], DT, rows[:, 0, :], ALU.add).then_inc(s["sp_v"], 1)
                dve.wait_ge(s["sp_v"], n + 1)
                dve.tensor_scalar(sp[:, 1, :], sp[:, 0, :], -1.0, None, ALU.mult).then_inc(s["sp_n"], 1)
                dve.wait_ge(s["sp_n"], n + 1)
                dve.tensor_tensor(sp[:, 2, :], sp[:, 0, :], sp[:, 1, :], ALU.min).then_inc(s["sp_min"], 1)

            def softplus_b(n):
                if not unit(n):
                    return
                dve.wait_ge(s["sp_exp"], n + 1)
                dve.tensor_scalar(sp[:, 4, :], sp[:, 3, :], 1.0, None, ALU.add).then_inc(s["sp_u"], 1)

            def softplus_c(n):
                if not unit(n):
                    return
                dve.wait_ge(s["sp_u"], n + 1)
                dve.scalar_tensor_tensor(sp[:, 6, :], sp[:, 4, :], 1.0, sp[:, 3, :], ALU.subtract, ALU.subtract).then_inc(s["sp_c"], 1)
                dve.wait_ge(s["sp_ln"], n + 1)
                dve.wait_ge(s["sp_c"], n + 1)
                dve.tensor_tensor(sp[:, 7, :], sp[:, 5, :], sp[:, 6, :], ALU.subtract).then_inc(s["sp_s"], 1)
                dve.wait_ge(s["sp_s"], n + 1)
                dve.scalar_tensor_tensor(dt[:, n, :], sp[:, 0, :], 0.0, sp[:, 7, :], ALU.max, ALU.add).then_inc(s["dt"], 1)
                dve.wait_ge(s["dt"], n + 1)
                if isinstance(n, int) and n == 0:
                    dve.wait_ge(s["a_set"], 1)
                dve.tensor_tensor(da[:, n, :], dt[:, n, :], A[:, :], ALU.mult).then_inc(s["da"], 1)

            def scan(n, p):
                if not unit(n):
                    return
                dve.wait_ge(s["cb"], n + 1)
                dve.tensor_tensor(gm[:, :], psO[:, 384:512], tri[:, :], ALU.mult).then_inc(s["gm"], 1)
                dve.wait_ge(s["gm"], n + 1)
                dve.wait_ge(s["dec"], 2 * (n + 1))
                past(dve, s["y"], n)
                dve.tensor_tensor(mm[:, :, :], dec[:, :, :], gm[:, :].unsqueeze(1).to_broadcast([P, NH, P]),
                                  ALU.mult).then_inc(s["mm"], 1)
                dve.wait_ge(s["xturn"], n + 1)
                dve.tensor_tensor(xd[:, :].rearrange("p (h c) -> p h c", h=NH), psX[:, :].rearrange("p (h c) -> p h c", h=NH),
                                  dt[:, n, :].unsqueeze(2).to_broadcast([P, NH, DI // NH]), ALU.mult).then_inc(s["xd"], 1)

            def skips(n, p):
                if not unit(n):
                    return
                dve.wait_ge(s["y"], n + 1)
                past(dve, s["yz"], n)
                for q in range(ZT):
                    dve.scalar_tensor_tensor(yd[:, q, :], xa[p][:, q, :], skip(q), psY[:, q, :],
                                             ALU.mult, ALU.add).then_inc(s["yd"], 1)

            def out_var(n, p):
                if not unit(n):
                    return
                dve.wait_ge(s["out"], n + 1)
                dve.tensor_scalar(fe[:, p:p + 1], SS, 1.0 / DI, EPS, ALU.mult, ALU.add).then_inc(s["f_var"], 1)

            def finish(n, p):
                if not unit(n):
                    return
                dve.wait_ge(s["f_rstd"], n + 1)
                dve.wait_ge(s["added"], n + 1)
                dve.scalar_tensor_tensor(X[:, n, :], psO[:, 0:D], fr[:, p:p + 1], X[:, n, :],
                                         ALU.mult, ALU.add).then_inc(s["f_out"], 1)

            def slot(n, p):
                low(n + 1, 1 - p)
                out_var(n - 2, p)
                ln_stats(n + 2, p)
                finish(n - 2, p)
                scan(n - 1, 1 - p)
                conv(n, (0, 1, 2, 3), "padA")
                softplus_a(n + 1)
                conv(n, (4, 5), "padB")
                softplus_b(n + 1)
                skips(n - 1, 1 - p)
                softplus_c(n + 1)
                ln_apply(n + 2, p)

            for n in range(2):
                ln_stats(n, n)
                ln_apply(n, n)
            low(0, 0)
            softplus_a(0)
            softplus_b(0)
            softplus_c(0)
            slots(dve, slot, GRP, 4, 2)

        @block.scalar
        def _(act):
            act.wait_ge(s["w_in"], 16 * WIN)
            act.wait_ge(s["consts"], 3)
            act.activation(A[:, :], rows[:, 1, :], ACT.Exp).then_inc(s["a_exp"], 1)

            def high(n, p):
                if not unit(n):
                    return
                act.wait_ge(s["turned"], n + 1)
                past(act, s["projZ"], n - 1)
                act.activation(xh[p][:, :, :], psT[:, 0:256].rearrange("p (k t) -> p k t", k=2), ACT.Copy).then_inc(s["xt_hi"], 1)

            def decay(n):
                if not unit(n):
                    return
                act.wait_ge(s["logs"], n + 1)
                past(act, s["mm"], n)
                for i in range(2):
                    act.activation(dec[:, 4 * i:4 * i + 4, :], psL[:, i, :, :], ACT.Exp).then_inc(s["dec"], 1)

            def pads(n, tiles, ps, proj, padded):
                if not unit(n):
                    return
                act.wait_ge(s[proj], n + 1)
                past(act, s["xact"], n)
                past(act, s["taps"], 3 * CONVT * n)
                for m in tiles:
                    act.activation(acc[:, m, :], ps(m), ACT.Identity, bias=cbias(m), scale=tap(m, 3)).then_inc(s["tap"], 1)
                    i = act.activation(pad[:, m, :, 3:3 + L], ps(m).rearrange("p (b t) -> p b t", t=L), ACT.Copy)
                i.then_inc(s[padded], 1)

            def softplus_exp(n):
                if not unit(n):
                    return
                act.wait_ge(s["sp_min"], n + 1)
                act.activation(sp[:, 3, :], sp[:, 2, :], ACT.Exp).then_inc(s["sp_exp"], 1)

            def softplus_ln(n):
                if not unit(n):
                    return
                act.wait_ge(s["sp_u"], n + 1)
                act.activation(sp[:, 5, :], sp[:, 4, :], ACT.Ln).then_inc(s["sp_ln"], 1)

            def silus(n, p):
                if not unit(n):
                    return
                act.wait_ge(s["projZ"], n + 1)
                past(act, s["yz"], n - 1)
                act.activation(zs[p][:, :, :], psA[:, :, :], ACT.Silu).then_inc(s["zact"], 1)
                act.wait_ge(s["taps"], 3 * CONVT * (n + 1))
                past(act, s["yd"], 4 * (n - 1))
                past(act, s["xturn"], n - 1)
                past(act, s["cb"], n - 1)
                act.activation(xa[p][:, :, :], acc[:, :, :], ACT.Silu).then_inc(s["xact"], 1)

            def squares(n, p):
                if not unit(n):
                    return
                act.wait_ge(s["yz"], n + 1)
                past(act, s["out"], n - 1)
                act.activation(y2[p][:, :, :], yz[p][:, :, :], ACT.Square).then_inc(s["y2"], 1)

            def slot(n, p):
                high(n + 1, 1 - p)
                decay(n - 1)
                pads(n, (0, 1, 2, 3), lambda m: psA[:, m, :], "projA", "padA")
                pads(n, (4, 5), lambda m: psB[:, P * (m - 4):P * (m - 3)], "projB", "padB")
                softplus_exp(n + 1)
                softplus_ln(n + 1)
                silus(n, p)
                squares(n - 1, 1 - p)

            high(0, 0)
            softplus_exp(0)
            softplus_ln(0)
            slots(act, slot, GRP, 4, 2)

        @block.tensor
        def _(pe):
            pe.wait_ge(s["w_lo"], 1)
            pe.wait_ge(s["consts"], 3)

            def turn(n, p):
                if not unit(n):
                    return
                pe.wait_ge(s["xn"], n + 1)
                past(pe, s["xt_lo"], n)
                past(pe, s["sp_v"], n)
                for k in range(2):
                    i = pe.transpose(psT[:, k * P:(k + 1) * P], xn[p][:, k * P:(k + 1) * P], ident[:, :])
                i.then_inc(s["turned"], 1)

            def project(n, p, out, w0, tiles, done):
                for m in tiles:
                    for k in range(2):
                        c = w0 + m * P
                        i = mm3(pe, out(m), (wh[:, k, c:c + P], wl[:, k, c:c + P]), (xh[p][:, k, :], xl[p][:, k, :]),
                                k == 0, k == 1)
                i.then_inc(s[done], 1)

            def project_a(n, p):
                if not unit(n):
                    return
                pe.wait_ge(s["xt_lo"], n + 1)
                past(pe, s["zact"], n)
                project(n, p, lambda m: psA[:, m, :], DI, (0, 1, 2, 3), "projA")

            def project_b(n, p):
                if not unit(n):
                    return
                past(pe, s["padB"], n)
                project(n, p, lambda m: psB[:, P * (m - 4):P * (m - 3)], DI, (4, 5), "projB")

            def project_z(n, p):
                if not unit(n):
                    return
                pe.wait_ge(s["padA"], n + 1)
                project(n, p, lambda m: psA[:, m, :], 0, (0, 1, 2, 3), "projZ")

            def steps(n, p):
                if not unit(n):
                    return
                pe.wait_ge(s["xt_lo"], n + 1)
                parts = [(x[p], k) for k in range(2) for x in (xh, xl)]
                for i, (x, k) in enumerate(parts):
                    t = pe.matmul(DT, x[:, k, :].bitcast(F32), w[:, k, DIN:DIN + NH], start=(i == 0), stop=(i == 3))
                t.then_inc(s["dt_mm"], 1)

            def logs(n):
                if not unit(n):
                    return
                pe.wait_ge(s["ta"], n + 1)
                past(pe, s["dec"], 2 * n)
                for i in range(2):
                    t = pe.matmul(psL[:, i, :, :], aft[:, :], ta[:, 4 * i:4 * i + 4, :], start=True, stop=True)
                t.then_inc(s["logs"], 1)

            def cb_and_x(n, p):
                if not unit(n):
                    return
                pe.wait_ge(s["xact"], n + 1)
                past(pe, s["f_out"], n)
                pe.matmul(psO[:, 384:512], xa[p][:, 4, :], xa[p][:, 5, :], start=True, stop=True).then_inc(s["cb"], 1)
                past(pe, s["xd"], n)
                for q in range(4):
                    t = pe.transpose(psX[:, q * P:(q + 1) * P], xa[p][:, q, :], ident[:, :])
                t.then_inc(s["xturn"], 1)

            def scan(n):
                if not unit(n):
                    return
                pe.wait_ge(s["mm"], n + 1)
                pe.wait_ge(s["xd"], n + 1)
                past(pe, s["yd"], 4 * n)
                for h in range(NH):
                    t = pe.matmul(psY[64 * (h % 2):64 * (h % 2) + 64, h // 2, :], xd[:, 64 * h:64 * h + 64], mm[:, h, :],
                                  start=True, stop=True)
                t.then_inc(s["y"], 1)

            def out(n, p):
                if not unit(n):
                    return
                pe.wait_ge(s["y2"], n + 1)
                pe.wait_ge(s["gm"], n + 1)
                for q in range(ZT):
                    pe.matmul(SS, y2[p][:, q, :], ones[:, :], start=(q == 0), stop=(q == 3))
                for q in range(ZT):
                    t = pe.matmul(psO[:, 0:D], yz[p][:, q, :], wout[:, q, :], start=(q == 0), stop=(q == 3))
                t.then_inc(s["out"], 1)

            def slot(n, p):
                turn(n + 1, 1 - p)
                out(n - 2, p)
                logs(n - 1)
                project_a(n, p)
                cb_and_x(n - 1, 1 - p)
                project_b(n, p)
                steps(n + 1, 1 - p)
                project_z(n, p)
                scan(n - 1)

            turn(0, 0)
            steps(0, 0)
            pe.wait_ge(s["wout_set"], 4)
            slots(pe, slot, GRP, 4, 2)

NHF, DF = 16, 16
E, FH = 8, 1024


def attention_phase(nc, sem, io, X, keep):
    mh, ml, logits = keep["mh"], keep["ml"], keep["logits"]
    with ExitStack() as ctx:
        def sb(name, shape, dt=F32):
            return ctx.enter_context(nc.sbuf_tensor("s_" + name, shape, dt))

        def pb(name, shape):
            return ctx.enter_context(nc.psum_tensor("s_" + name, shape, F32))

        wq, wk, wv, wp = (sb(n, [P, 2, D]) for n in ("wq", "wk", "wv", "wp"))
        gw = sb("gw", [P, 2, E])
        cols = sb("cols", [P, 8, 2])
        rows = sb("rows", [P, D])
        gbias = sb("gbias", [P, E])
        ident = sb("ident", [P, P])
        heads = sb("heads", [P, 8])
        causal = sb("causal", [P, L])
        tick = sb("tick", [P, 1])
        half = sb("half", [P, 1])
        h0 = sb("h0", [P, GRP, D])
        xn = [sb(f"xn{i}", [P, D]) for i in range(2)]
        hT = [sb(f"hT{i}", [P, 2, P]) for i in range(2)]
        stat = [sb(f"st{i}", [P, 2, 6]) for i in range(3)]
        mv = [sb(f"mv{i}", [P, 2, 2]) for i in range(3)]
        ve = [sb(f"ve{i}", [P, 2]) for i in range(3)]
        rs = [sb(f"rs{i}", [P, 2]) for i in range(3)]
        qT = [sb(f"qT{i}", [P, 2, P]) for i in range(2)]
        kT = [sb(f"kT{i}", [P, 2, P]) for i in range(2)]
        qx = sb("qx", [P, 2, BPG, 8, L])
        vx = [sb(f"vx{i}", [P, BPG, 4, 4, DF]) for i in range(2)]
        sc = sb("sc", [P, 16, L])
        mx = sb("mx", [P, 16])
        su = sb("su", [P, 16])
        ri = sb("ri", [P, 16])
        pr = sb("pr", [P, 16, L])
        pT = [sb(f"pT{i}", [P, 16, L]) for i in range(2)]
        yT = [sb(f"yT{i}", [P, 2, P]) for i in range(2)]
        h1 = [sb(f"h1{i}", [P, D]) for i in range(2)]
        n2 = [sb(f"n2{i}", [P, D]) for i in range(2)]
        mf = [sb(f"mf{i}", [P, 2, P]) for i in range(2)]

        psT = pb("psT", [P, 4, P])
        psQ = pb("psQ", [P, 4, P])
        psV = pb("psV", [P, 512])
        psS = pb("psS", [P, 16, L])
        psY = pb("psY", [P, 4, P])
        psO = pb("psO", [P, 512])
        psU = pb("psU", [P, 4, P])
        psG = pb("psG", [P, 512])
        s = {n: sem("s_" + n) for n in (
            "w_in", "consts", "stats0", "aggr0", "var0", "rstd0", "norm0", "stats1", "aggr1", "var1", "rstd1", "norm1",
            "stats2", "aggr2", "var2", "rstd2", "norm2", "biased", "turned", "hT", "qk", "v", "q_out", "k_out",
            "qx", "vx_a", "vx_d", "scored", "masked", "peak", "shifted", "exped", "summed", "recip", "probs", "pT",
            "attended", "yT", "outed", "h1", "added", "turned2", "mf", "mh", "ml", "gate", "logits")}
        block = ctx.enter_context(nc.Block())
        WIN = 11
        col = lambda i, k: cols[:, i, k:k + 1]

        @block.sync
        def _(sy):
            for d, src in ((wq, "s_wq"), (wk, "s_wk"), (wv, "s_wv"), (wp, "s_wp"), (gw, "s_gw"), (cols, "s_cols"), (rows, "s_bp"),
                           (gbias, "s_gb"), (ident, "ident"), (heads, "heads"), (causal, "causal")):
                sy.dma_start(d[tuple(slice(None) for _ in d.shape)], io[src]).then_inc(s["w_in"], 16)
            sy.wait_ge(s["w_in"], 16 * WIN)

        @block.gpsimd
        def _(pool):
            pool.memset(half[:, :], -0.5).then_inc(s["consts"], 1)
            for i in range(2):
                pool.memset(vx[i][:, :, :, :, :], 0.0).then_inc(s["consts"], 1)
            pool.wait_ge(s["consts"], 3)
            pool.wait_ge(s["w_in"], 16 * WIN)

            def power(which, n, p):
                if not unit(n):
                    return
                pool.wait_ge(s[f"var{which}"], n + 1)
                pool.tensor_tensor(rs[which][:, p:p + 1], ve[which][:, p:p + 1], half[:, :], ALU.pow).then_inc(s[f"rstd{which}"], 1)

            def bias(n):
                if not unit(n):
                    return
                pool.wait_ge(s["norm1"], n + 1)
                pool.tensor_tensor(h0[:, n, :], h0[:, n, :], rows[:, :], ALU.add).then_inc(s["biased"], 1)

            def by_head(n, p):
                if not unit(n):
                    return
                pool.wait_ge(s["q_out"], n + 1)
                past(pool, s["scored"], n)
                for k in range(2):
                    q = qT[p][:, k, :].rearrange("p (b t) -> p b t", t=L).unsqueeze(2).to_broadcast([P, BPG, 8, L])
                    own = heads[:, :].unsqueeze(1).unsqueeze(3).to_broadcast([P, BPG, 8, L])
                    pool.tensor_tensor(qx[:, k, :, :, :], q, own, ALU.mult).then_inc(s["qx"], 1)

            def add(n, p):
                if not unit(n):
                    return
                pool.wait_ge(s["h1"], n + 1)
                pool.tensor_tensor(X[:, n, :], X[:, n, :], h1[p][:, :], ALU.add).then_inc(s["added"], 1)

            def slot(n, p):
                power(2, n - 3, 1 - p)
                power(0, n + 2, p)
                power(1, n + 2, p)
                by_head(n, p)
                add(n - 3, 1 - p)
                bias(n + 2)

            for n in range(2):
                power(0, n, n)
                power(1, n, n)
                bias(n)
            slots(pool, slot, GRP, 6, 4)

        @block.vector
        def _(dve):
            dve.wait_ge(s["w_in"], 16 * WIN)
            dve.wait_ge(s["consts"], 3)

            def norm_stats(which, n, p, src):
                dve.bn_stats(stat[which][:, p, :], src).then_inc(s[f"stats{which}"], 1)
                wait_ahead(dve, s[f"stats{which}"], n + 1, tick)
                dve.bn_aggr(mv[which][:, p, :], stat[which][:, p, :]).then_inc(s[f"aggr{which}"], 1)
                dve.wait_ge(s[f"aggr{which}"], n + 1)
                dve.tensor_scalar(ve[which][:, p:p + 1], mv[which][:, p, 1:2], EPS, None, ALU.add).then_inc(s[f"var{which}"], 1)

            def norm_apply(which, n, p, src, dst):
                dve.wait_ge(s[f"rstd{which}"], n + 1)
                dve.tensor_scalar(dst, src, mv[which][:, p, 0:1], rs[which][:, p:p + 1],
                                  ALU.subtract, ALU.mult).then_inc(s[f"norm{which}"], 1)

            def norms_a(n, p):
                if unit(n):
                    norm_stats(0, n, p, X[:, n, :])

            def norms_b(n, p):
                if unit(n):
                    norm_apply(0, n, p, X[:, n, :], h0[:, n, :])
                    wait_ahead(dve, s["norm0"], n + 1, tick)
                    norm_stats(1, n, p, h0[:, n, :])

            def norms_c(n, p):
                if unit(n):
                    past(dve, s["turned"], n - 1)
                    norm_apply(1, n, p, h0[:, n, :], xn[p][:, :])

            def v_blocks(n, p):
                if not unit(n):
                    return
                dve.wait_ge(s["v"], n + 1)
                dve.wait_ge(s["vx_a"], n + 1)
                past(dve, s["attended"], n - 1)
                for b in range(2, 4):
                    for h in range(4):
                        i = dve.tensor_copy(vx[p][32 * h:32 * h + 32, b, :, h, :],
                                            psV[32 * b:32 * b + 32, 0:D].rearrange("p (g h d) -> p g h d", g=4, h=4)[:, :, h, :])
                i.then_inc(s["vx_d"], 1)

            def shift(n):
                if not unit(n):
                    return
                dve.wait_ge(s["scored"], n + 1)
                past(dve, s["exped"], n)
                dve.tensor_tensor(sc[:, :, :], psS[:, :, :], causal[:, :].unsqueeze(1).to_broadcast([P, 16, L]),
                                  ALU.add).then_inc(s["masked"], 1)
                dve.wait_ge(s["masked"], n + 1)
                dve.reduce_max(mx[:, :], sc[:, :, :], AXX).then_inc(s["peak"], 1)
                dve.wait_ge(s["peak"], n + 1)
                dve.tensor_tensor(sc[:, :, :], sc[:, :, :], mx[:, :].unsqueeze(2).to_broadcast([P, 16, L]),
                                  ALU.subtract).then_inc(s["shifted"], 1)

            def shares(n, p):
                if not unit(n):
                    return
                dve.wait_ge(s["exped"], n + 1)
                dve.reduce_sum(su[:, :], pr[:, :, :], AXX).then_inc(s["summed"], 1)
                dve.wait_ge(s["summed"], n + 1)
                dve.reciprocal(ri[:, :], su[:, :]).then_inc(s["recip"], 1)
                dve.wait_ge(s["recip"], n + 1)
                dve.tensor_tensor(pr[:, :, :], pr[:, :, :], ri[:, :].unsqueeze(2).to_broadcast([P, 16, L]),
                                  ALU.mult).then_inc(s["probs"], 1)
                dve.wait_ge(s["probs"], n + 1)
                past(dve, s["attended"], n - 1)
                dve.transpose(pT[p][:, :, :].rearrange("p a b -> p (a b)"),
                              pr[:, :, :].rearrange("p a b -> p (a b)")).then_inc(s["pT"], 1)

            def residual(n, p):
                if not unit(n):
                    return
                dve.wait_ge(s["outed"], n + 1)
                dve.wait_ge(s["biased"], n + 1)
                past(dve, s["added"], n - 1)
                dve.tensor_tensor(h1[p][:, :], psO[:, 0:D], h0[:, n, :], ALU.add).then_inc(s["h1"], 1)
                dve.wait_ge(s["h1"], n + 1)
                norm_stats(2, n, p, h1[p][:, :])

            def second_norm(n, p):
                if not unit(n):
                    return
                past(dve, s["turned2"], n - 1)
                norm_apply(2, n, p, h1[p][:, :], n2[p][:, :])

            def route(n, p):
                if not unit(n):
                    return
                dve.wait_ge(s["mh"], n + 1)
                dve.tensor_tensor(ml[:, :, bass.ds(n * P, P)], mf[p][:, :, :], mh[:, :, bass.ds(n * P, P)].bitcast(F32),
                                  ALU.subtract).then_inc(s["ml"], 1)
                dve.wait_ge(s["gate"], n + 1)
                dve.tensor_tensor(logits[:, n, :], psG[:, 0:E], gbias[:, :], ALU.add).then_inc(s["logits"], 1)

            def slot(n, p):
                norms_a(n + 2, p)
                residual(n - 3, 1 - p)
                norms_b(n + 2, p)
                shift(n - 1)
                second_norm(n - 3, 1 - p)
                norms_c(n + 2, p)
                v_blocks(n, p)
                route(n - 4, p)
                shares(n - 1, 1 - p)

            for n in range(2):
                norms_a(n, n)
                norms_b(n, n)
                norms_c(n, n)
            slots(dve, slot, GRP, 6, 4)

        @block.scalar
        def _(act):
            act.wait_ge(s["w_in"], 16 * WIN)
            act.wait_ge(s["consts"], 3)

            def affine(n, p):
                if not unit(n):
                    return
                act.wait_ge(s["turned"], n + 1)
                past(act, s["v"], n - 1)
                for k in range(2):
                    act.activation(hT[p][:, k, :], psT[:, k, :], ACT.Identity, bias=col(1, k), scale=col(0, k)).then_inc(s["hT"], 1)

            def biases(n, p):
                if not unit(n):
                    return
                act.wait_ge(s["qk"], n + 1)
                past(act, s["qx"], 2 * (n - 1))
                for k in range(2):
                    i = act.activation(qT[p][:, k, :], psQ[:, k, :], ACT.Identity, bias=col(2, k))
                i.then_inc(s["q_out"], 1)
                past(act, s["scored"], n - 1)
                for k in range(2):
                    i = act.activation(kT[p][:, k, :], psQ[:, 2 + k, :], ACT.Identity, bias=col(3, k))
                i.then_inc(s["k_out"], 1)

            def v_blocks(n, p):
                if not unit(n):
                    return
                act.wait_ge(s["v"], n + 1)
                past(act, s["attended"], n - 1)
                for b in range(2):
                    for h in range(4):
                        i = act.activation(vx[p][32 * h:32 * h + 32, b, :, h, :],
                                           psV[32 * b:32 * b + 32, 0:D].rearrange("p (g h d) -> p g h d", g=4, h=4)[:, :, h, :],
                                           ACT.Copy)
                i.then_inc(s["vx_a"], 1)

            def exps(n):
                if not unit(n):
                    return
                act.wait_ge(s["shifted"], n + 1)
                past(act, s["pT"], n)
                act.activation(pr[:, :, :], sc[:, :, :], ACT.Exp).then_inc(s["exped"], 1)

            def attended(n, p):
                if not unit(n):
                    return
                act.wait_ge(s["attended"], n + 1)
                past(act, s["outed"], n - 1)
                for k in range(2):
                    i = act.activation(yT[p][:, k, :], psY[:, k, :], ACT.Identity, bias=col(4, k))
                i.then_inc(s["yT"], 1)

            def affine2(n, p):
                if not unit(n):
                    return
                act.wait_ge(s["turned2"], n + 1)
                past(act, s["gate"], n - 1)
                past(act, s["ml"], n - 1)
                for k in range(2):
                    act.activation(mf[p][:, k, :], psU[:, k, :], ACT.Identity, bias=col(6, k), scale=col(5, k)).then_inc(s["mf"], 1)
                act.wait_ge(s["mf"], 2 * (n + 1))
                act.activation(mh[:, :, bass.ds(n * P, P)], mf[p][:, :, :], ACT.Copy).then_inc(s["mh"], 1)

            def slot(n, p):
                affine(n + 1, 1 - p)
                affine2(n - 4, p)
                biases(n, p)
                v_blocks(n, p)
                exps(n - 1)
                attended(n - 2, p)

            affine(0, 0)
            slots(act, slot, GRP, 6, 4)

        @block.tensor
        def _(pe):
            pe.wait_ge(s["w_in"], 16 * WIN)

            def turn(n, p):
                if not unit(n):
                    return
                pe.wait_ge(s["norm1"], n + 1)
                past(pe, s["hT"], 2 * n)
                for k in range(2):
                    i = pe.transpose(psT[:, k, :], xn[p][:, k * P:(k + 1) * P], ident[:, :])
                i.then_inc(s["turned"], 1)

            def project(n, p):
                if not unit(n):
                    return
                pe.wait_ge(s["hT"], 2 * (n + 1))
                past(pe, s["k_out"], n)
                for i, w in enumerate((wq, wk)):
                    for m in range(2):
                        for k in range(2):
                            t = pe.matmul(psQ[:, 2 * i + m, :], w[:, k, m * P:(m + 1) * P], hT[p][:, k, :],
                                          start=(k == 0), stop=(k == 1))
                t.then_inc(s["qk"], 1)
                past(pe, s["vx_d"], n)
                for k in range(2):
                    t = pe.matmul(psV[:, 0:D], hT[p][:, k, :], wv[:, k, :], start=(k == 0), stop=(k == 1))
                t.then_inc(s["v"], 1)

            def score(n, p):
                if not unit(n):
                    return
                pe.wait_ge(s["qx"], 2 * (n + 1))
                pe.wait_ge(s["k_out"], n + 1)
                past(pe, s["masked"], n)
                for g in range(4):
                    for b in range(BPG):
                        t = pe.matmul(psS[:, BPG * g + b, :], qx[:, g // 2, b, 4 * (g % 2):4 * (g % 2) + 4, :],
                                      kT[p][:, g // 2, L * b:L * b + L], start=True, stop=True)
                t.then_inc(s["scored"], 1)

            def attend(n, p):
                if not unit(n):
                    return
                pe.wait_ge(s["pT"], n + 1)
                pe.wait_ge(s["vx_d"], n + 1)
                past(pe, s["yT"], n)
                for g in range(4):
                    for b in range(BPG):
                        t = pe.matmul(psY[64 * (g % 2):64 * (g % 2) + 64, g // 2, L * b:L * b + L],
                                      vx[p][:, b, g, :, :], pT[p][:, BPG * g + b, :], start=True, stop=True)
                t.then_inc(s["attended"], 1)

            def output(n, p):
                if not unit(n):
                    return
                pe.wait_ge(s["yT"], n + 1)
                past(pe, s["h1"], n)
                for k in range(2):
                    t = pe.matmul(psO[:, 0:D], yT[p][:, k, :], wp[:, k, :], start=(k == 0), stop=(k == 1))
                t.then_inc(s["outed"], 1)

            def turn2(n, p):
                if not unit(n):
                    return
                pe.wait_ge(s["norm2"], n + 1)
                past(pe, s["mf"], 2 * n)
                for k in range(2):
                    t = pe.transpose(psU[:, k, :], n2[p][:, k * P:(k + 1) * P], ident[:, :])
                t.then_inc(s["turned2"], 1)

            def route(n, p):
                if not unit(n):
                    return
                pe.wait_ge(s["mf"], 2 * (n + 1))
                past(pe, s["logits"], n)
                for k in range(2):
                    t = pe.matmul(psG[:, 0:E], mf[p][:, k, :], gw[:, k, :], start=(k == 0), stop=(k == 1))
                t.then_inc(s["gate"], 1)

            def slot(n, p):
                turn(n + 1, 1 - p)
                turn2(n - 4, p)
                output(n - 3, 1 - p)
                project(n, p)
                route(n - 4, p)
                score(n - 1, 1 - p)
                attend(n - 2, p)

            turn(0, 0)
            slots(pe, slot, GRP, 6, 4)


def router_phase(nc, sem, io, keep):
    logits, gates = keep["logits"], keep["gates"]
    with ExitStack() as ctx:
        def sb(name, shape):
            return ctx.enter_context(nc.sbuf_tensor("r_" + name, shape, F32))

        idx = sb("idx", [P, E])
        t = [sb(f"t{i}", [P, GRP, E]) for i in range(8)]
        v = [sb(f"v{i}", [P, GRP]) for i in range(8)]
        got, step, exped = sem("r_in"), sem("r_step"), sem("r_exp")
        block = ctx.enter_context(nc.Block())
        wide = lambda a: a[:, :].unsqueeze(2).to_broadcast([P, GRP, E])

        @block.sync
        def _(sy):
            sy.dma_start(idx[:, :], io["experts"]).then_inc(got, 16)
            sy.wait_ge(got, 16)

        @block.scalar
        def _(act):
            act.wait_ge(step, 11)
            act.activation(v[5][:, :], v[4][:, :], ACT.Exp).then_inc(exped, 1)

        @block.vector
        def _(dve):
            dve.wait_ge(got, 16)
            count = [0]

            def link(i):
                count[0] += 1
                i.then_inc(step, 1)
                dve.wait_ge(step, count[0])

            ix = idx[:, :].unsqueeze(1).to_broadcast([P, GRP, E])

            def pick(src, top, first, onehot):
                link(dve.reduce_max(top[:, :], src[:, :, :], AXX))
                link(dve.tensor_tensor(t[6][:, :, :], src[:, :, :], wide(top), ALU.is_equal))
                link(dve.tensor_tensor(t[6][:, :, :], t[6][:, :, :], ix, ALU.mult))
                link(dve.reduce_max(first[:, :], t[6][:, :, :], AXX))
                link(dve.tensor_tensor(onehot[:, :, :], t[6][:, :, :], wide(first), ALU.is_equal))

            pick(logits, v[0], v[1], t[0])
            big = t[0][:, :, :].rearrange("p a b -> p (a b)")
            flat = lambda a: a[:, :, :].rearrange("p a b -> p (a b)")
            link(dve.scalar_tensor_tensor(flat(t[1]), big, -3.0e38, flat(logits), ALU.mult, ALU.add))
            pick_from = t[1]
            link(dve.reduce_max(v[2][:, :], pick_from[:, :, :], AXX))
            link(dve.tensor_tensor(t[6][:, :, :], pick_from[:, :, :], wide(v[2]), ALU.is_equal))
            link(dve.tensor_tensor(t[6][:, :, :], t[6][:, :, :], ix, ALU.mult))
            link(dve.reduce_max(v[3][:, :], t[6][:, :, :], AXX))
            link(dve.tensor_tensor(v[4][:, :], v[2][:, :], v[0][:, :], ALU.subtract))
            link(dve.tensor_tensor(t[2][:, :, :], t[6][:, :, :], wide(v[3]), ALU.is_equal))
            dve.wait_ge(exped, 1)
            link(dve.tensor_scalar(v[6][:, :], v[5][:, :], 1.0, None, ALU.add))
            link(dve.reciprocal(v[7][:, :], v[6][:, :]))
            link(dve.tensor_tensor(v[5][:, :], v[5][:, :], v[7][:, :], ALU.mult))
            link(dve.tensor_tensor(t[3][:, :, :], t[0][:, :, :], wide(v[7]), ALU.mult))
            link(dve.tensor_tensor(t[4][:, :, :], t[2][:, :, :], wide(v[5]), ALU.mult))
            link(dve.tensor_tensor(gates[:, :, :], t[3][:, :, :], t[4][:, :, :], ALU.add))


def moe_phase(nc, sem, io, X, keep):
    mh, ml, gates = keep["mh"], keep["ml"], keep["gates"]
    C, FT = 4, FH // P
    with ExitStack() as ctx:
        def sb(name, shape, dt=F32):
            return ctx.enter_context(nc.sbuf_tensor("e_" + name, shape, dt))

        w1 = sb("w1", [P, 2, FH])
        w2 = sb("w2", [P, FT, D])
        b1 = sb("b1", [P, E, FT])
        b2 = [sb(f"b2{i}", [1, D]) for i in range(2)]
        ones = sb("ones", [1, P])
        w1h = [sb(f"w1h{i}", [P, 2, FH], F32R) for i in range(2)]
        w1l = [sb(f"w1l{i}", [P, 2, FH], F32R) for i in range(2)]
        w2h = [sb(f"w2h{i}", [P, FT, D], F32R) for i in range(2)]
        w2l = [sb(f"w2l{i}", [P, FT, D], F32R) for i in range(2)]
        mid = [sb(f"mid{i}", [P, 512]) for i in range(2)]
        b1e = [sb(f"b1e{i}", [P, FT]) for i in range(2)]
        dh = sb("dh", [P, FT, 512], F32R)
        dl = sb("dl", [P, FT, 512], F32R)
        ps1 = [ctx.enter_context(nc.psum_tensor(f"e_ps1{i}", [P, 512], F32)) for i in range(4)]
        ps2 = [ctx.enter_context(nc.psum_tensor(f"e_ps2{i}", [P, 512], F32)) for i in range(4)]
        s = {n: sem("e_" + n) for n in ("w1_in", "w2_in", "b1_in", "b1e", "consts", "w1h", "w1l", "w2h", "w2l",
                                        "up", "gelu", "hi", "lo", "down", "sum")}
        b2_in = [sem(f"e_b2_in{i}") for i in range(2)]
        block = ctx.enter_context(nc.Block())

        @block.sync
        def _(sy):
            sy.dma_start(b1[:, :, :], io["e_b1"]).then_inc(s["b1_in"], 16)

            def load(e, p):
                past(sy, s["w1l"], e)
                sy.dma_start(w1[:, :, :], io["e_w1"][e]).then_inc(s["w1_in"], 16)
                past(sy, s["w2l"], e)
                sy.dma_start(w2[:, :, :], io["e_w2"][e]).then_inc(s["w2_in"], 16)
                past(sy, s["down"], 16 * (e - 1))
                sy.dma_start(b2[p][:, :], io["e_b2"][e]).then_inc(b2_in[p], 16)

            load(0, 0)
            load(1, 1)
            with sy.Fori(1, E // 2) as i:
                load(2 * i, 0)
                load(2 * i + 1, 1)

        @block.gpsimd
        def _(pool):
            pool.memset(ones[:, :], 1.0).then_inc(s["consts"], 1)

            def low_parts(e, p):
                pool.wait_ge(s["w1h"], e + 1)
                pool.tensor_tensor(w1l[p][:, :, :], w1[:, :, :], w1h[p][:, :, :].bitcast(F32), ALU.subtract).then_inc(s["w1l"], 1)
                pool.wait_ge(s["w2h"], e + 1)
                pool.tensor_tensor(w2l[p][:, :, :], w2[:, :, :], w2h[p][:, :, :].bitcast(F32), ALU.subtract).then_inc(s["w2l"], 1)

            low_parts(0, 0)
            low_parts(1, 1)
            with pool.Fori(1, E // 2) as i:
                low_parts(2 * i, 0)
                low_parts(2 * i + 1, 1)

        @block.scalar
        def _(act):
            act.wait_ge(s["b1_in"], 16)

            def chunk(e, p, c, first=False):
                q = 4 * e + c
                for f in range(FT):
                    n = FT * q + f
                    act.wait_ge(s["up"], n + 1)
                    if not (first and c == 0 and f < 2):
                        act.wait_ge(s["lo"], n - 1)
                    act.activation(mid[f % 2][:, :], ps1[f % 4][:, :], ACT.Gelu, bias=b1e[p][:, f:f + 1]).then_inc(s["gelu"], 1)

            def biases(e, p):
                act.activation(b1e[p][:, :], b1[:, e, :], ACT.Copy).then_inc(s["b1e"], 1)
                act.wait_ge(s["b1e"], e + 1)

            def high_parts(e, p):
                act.wait_ge(s["w1_in"], 16 * (e + 1))
                past(act, s["up"], 32 * (e - 1))
                act.activation(w1h[p][:, :, :], w1[:, :, :], ACT.Copy).then_inc(s["w1h"], 1)
                act.wait_ge(s["w2_in"], 16 * (e + 1))
                past(act, s["down"], 16 * (e - 1))
                act.activation(w2h[p][:, :, :], w2[:, :, :], ACT.Copy).then_inc(s["w2h"], 1)

            def expert(e, p, first=False, last=False):
                biases(e, p)
                for c in range(C):
                    chunk(e, p, c, first)
                    if c == 0 and not last:
                        high_parts(e + 1, 1 - p)

            high_parts(0, 0)
            expert(0, 0, first=True)
            expert(1, 1)
            with act.Fori(1, E // 2 - 1) as i:
                expert(2 * i, 0)
                expert(2 * i + 1, 1)
            expert(E - 2, 0)
            expert(E - 1, 1, last=True)

        @block.vector
        def _(dve):
            def hidden(e, c, f, first=False):
                n = FT * (4 * e + c) + f
                dve.wait_ge(s["gelu"], n + 1)
                if not (first and c == 0) and f == 0:
                    dve.wait_ge(s["down"], 4 * (4 * e + c))
                dve.tensor_copy(dh[:, f, :], mid[f % 2][:, :]).then_inc(s["hi"], 1)
                dve.wait_ge(s["hi"], n + 1)
                dve.tensor_tensor(dl[:, f, :], mid[f % 2][:, :], dh[:, f, :].bitcast(F32), ALU.subtract).then_inc(s["lo"], 1)

            def sums(e, c):
                for j in range(4):
                    q = 4 * (4 * e + c) + j
                    dve.wait_ge(s["down"], q + 1)
                    dve.scalar_tensor_tensor(X[:, 4 * c + j, :], ps2[j][:, 0:D], gates[:, 4 * c + j, bass.ds(e, 1)],
                                             X[:, 4 * c + j, :], ALU.mult, ALU.add).then_inc(s["sum"], 1)

            def chunk(e, c, first=False):
                for f in range(FT):
                    hidden(e, c, f, first)
                sums(e, c)

            for e in range(2):
                for c in range(C):
                    chunk(e, c, e == 0)
            with dve.Fori(1, E // 2) as i:
                for p in range(2):
                    for c in range(C):
                        chunk(2 * i + p, c)

        @block.tensor
        def _(pe):
            pe.wait_ge(s["consts"], 1)

            def up(e, p, c, first=False):
                pe.wait_ge(s["w1l"], e + 1)
                for f in range(FT):
                    n = FT * (4 * e + c) + f
                    if not (first and c == 0 and f < 4):
                        pe.wait_ge(s["gelu"], n - 3)
                    for k in range(2):
                        t = mm3(pe, ps1[f % 4][:, :], (w1h[p][:, k, f * P:(f + 1) * P], w1l[p][:, k, f * P:(f + 1) * P]),
                                (mh[:, k, 512 * c:512 * c + 512], ml[:, k, 512 * c:512 * c + 512]), k == 0, k == 1)
                    t.then_inc(s["up"], 1)

            def down(e, p, c, first=False):
                pe.wait_ge(s["w2l"], e + 1)
                pe.wait_ge(b2_in[p], 16 * ((e + 2) // 2) if isinstance(e, int) else 16 * (e // 2 + 1))
                pe.wait_ge(s["lo"], FT * (4 * e + c + 1))
                for j in range(4):
                    q = 4 * (4 * e + c) + j
                    if not (first and c == 0):
                        pe.wait_ge(s["sum"], q - 3)
                    for f in range(FT):
                        mm3(pe, ps2[j][:, 0:D], (dh[:, f, j * P:(j + 1) * P], dl[:, f, j * P:(j + 1) * P]),
                            (w2h[p][:, f, :], w2l[p][:, f, :]), f == 0, False)
                    pe.matmul(ps2[j][:, 0:D], ones[:, :], b2[p][:, :], start=False, stop=True).then_inc(s["down"], 1)

            for e in range(2):
                for c in range(C):
                    up(e, e, c, e == 0)
                    down(e, e, c, e == 0)
            with pe.Fori(1, E // 2) as i:
                for p in range(2):
                    for c in range(C):
                        up(2 * i + p, p, c)
                        down(2 * i + p, p, c)


def phase(nc, run, *args):
    with ExitStack() as ctx:
        made = []

        def sem(name):
            made.append(ctx.enter_context(nc.semaphore(name)))
            return made[-1]

        run(nc, sem, *args)
        nums = sorted(x.num for x in made)
        with nc.Block() as block:
            @block.sync
            def _(sp):
                while nums:
                    n = 1
                    while n < len(nums) and nums[n] == nums[0] + n:
                        n += 1
                    sp.sem_clear(range(nums[0], nums[0] + n))
                    del nums[:n]


def store_phase(nc, sem, out, X):
    stored = sem("z_stored")
    with nc.Block() as block:
        @block.sync
        def _(sp):
            sp.dma_start(out, X[:, :, :]).then_inc(stored, 16)
            sp.wait_ge(stored, 16)


def program(nc, io, out):
    with ExitStack() as ctx:
        X = ctx.enter_context(nc.sbuf_tensor("X", [P, GRP, D], F32))
        with ExitStack() as c2:
            kv = {
                "qT": c2.enter_context(nc.sbuf_tensor("qT", [P, 4, B * L], F32)),
                "KX": c2.enter_context(nc.sbuf_tensor("KX", [P, 4, B, TAIL], F32)),
                "xe": nc.dram_tensor("tail_values", (B, TAIL, D), F32, kind="Internal").ap(),
            }
            phase(nc, latents_phase, io, X, kv)
            phase(nc, xattn_phase, io, X, kv)
        if STAGES > 1:
            phase(nc, mamba_phase, io, X)
        if STAGES > 2:
            keep = {
                "mh": ctx.enter_context(nc.sbuf_tensor("mh", [P, 2, B * L], F32R)),
                "ml": ctx.enter_context(nc.sbuf_tensor("ml", [P, 2, B * L], F32R)),
                "logits": ctx.enter_context(nc.sbuf_tensor("logits", [P, GRP, E], F32)),
                "gates": ctx.enter_context(nc.sbuf_tensor("gates", [P, GRP, E], F32)),
            }
            phase(nc, attention_phase, io, X, keep)
            phase(nc, router_phase, io, keep)
            phase(nc, moe_phase, io, X, keep)
        phase(nc, store_phase, out, X)


def rope_tables():
    inv = (np.float32(1.0) / np.float32(10000.0) ** (np.arange(0, DH, 2, dtype=np.float32) / np.float32(DH))).astype(np.float32)
    theta = (np.arange(S, dtype=np.float32)[:, None] * inv[None, :]).astype(np.float32)
    cos, sin = np.cos(theta).T.astype(np.float32), np.sin(theta).T.astype(np.float32)
    return np.tile(cos, (4, 1)), np.tile(sin, (4, 1))


def layouts(v):
    c = np.ascontiguousarray

    def rows(w):
        return c(w.reshape(-1, P, w.shape[-1]).transpose(1, 0, 2))

    def every(*vs):
        return c(np.tile(np.stack(vs)[None], (P, 1, 1)))

    def split_heads(w):
        return rows(w.reshape(D, 2, 4, 2, 32).transpose(0, 1, 3, 2, 4).reshape(D, 512))

    a = {}
    a["x"] = rows(v["x"].reshape(B * L, D))
    a["ctx"] = c(v["ctx_1024"][:, :256].reshape(B, 2, P, D).transpose(0, 2, 1, 3))
    a["ctx_last"] = c(v["ctx_1024"][:, 256])
    a["wq"] = split_heads(v["L0_xattn_Wq"])
    a["wk"] = split_heads(v["L0_xattn_Wkv"][:, :512])
    a["wv"] = rows(v["L0_xattn_Wkv"][:, 512:])
    a["wo"] = rows(v["L0_xattn_Wo"])
    a["gb"] = every(v["L0_xattn_gamma_x"], v["L0_xattn_beta_x"], v["L0_xattn_gamma_l"], v["L0_xattn_beta_l"])
    a["ident"] = np.eye(P, dtype=np.float32)
    cos, sin = rope_tables()
    a["cos"] = c(cos[:, :256])
    a["sin"] = c(np.stack([-sin[:, :256], sin[:, :256]], 1))
    a["edge"] = c(np.stack([cos[:, 256], sin[:, 256]], 1))
    if STAGES > 1:
        more_layouts(a, v)
    return a


def more_layouts(a, v):
    c = np.ascontiguousarray

    def rows(w):
        return c(w.reshape(-1, P, w.shape[-1]).transpose(1, 0, 2))

    def column(x):
        return x.reshape(-1, P).T

    a["m_w"] = rows(v["L0_attn_in_proj_w"].T)
    a["m_out"] = rows(v["L0_attn_out_proj_w"].T)
    cw = v["L0_attn_conv_w"].reshape(CONVT, P, 4).transpose(1, 0, 2).reshape(P, 4 * CONVT)
    a["m_cols"] = c(np.concatenate([cw, column(v["L0_attn_conv_b"]), column(np.repeat(v["L0_attn_D"], DI // NH)),
                                    column(v["L0_attn_norm_w"])], 1))
    a["m_rows"] = c(np.tile(np.stack([v["L0_attn_dt_bias"], v["L0_attn_A_log"]])[None], (P, 1, 1)))
    i = np.arange(P)
    same = (i[:, None] // L) == (i[None, :] // L)
    a["tri"] = (same & (i[:, None] <= i[None, :])).astype(np.float32)
    a["aft"] = (same & (i[:, None] > i[None, :])).astype(np.float32)
    if STAGES > 2:
        for n in ("q", "k", "v", "p"):
            a["s_w" + n] = rows(v["L0_ffn_W" + n])
        a["s_gw"] = rows(v["L0_ffn_gate_W"])
        vs = [v["L0_ffn_" + n] for n in ("ln1_g", "ln1_b", "bq", "bk", "bv", "ln2_g", "ln2_b", "ln2_b")]
        a["s_cols"] = c(np.stack([column(x) for x in vs], 1))
        a["s_bp"] = c(np.tile(v["L0_ffn_bp"][None], (P, 1)))
        a["s_gb"] = c(np.tile(v["L0_ffn_gate_b"][None], (P, 1)))
        a["heads"] = np.where(i[:, None] // DF == np.arange(8)[None], np.float32(DF ** -0.5), np.float32(0))
        a["causal"] = np.where(np.arange(L)[None] > (i % L)[:, None], np.float32(-1e30), np.float32(0))
        a["experts"] = np.tile(np.arange(E, 0, -1, dtype=np.float32)[None], (P, 1))
        a["e_w1"] = c(v["L0_ffn_exp_W1"].reshape(E, 2, P, FH).transpose(0, 2, 1, 3))
        a["e_w2"] = c(v["L0_ffn_exp_W2"].reshape(E, FH // P, P, D).transpose(0, 2, 1, 3))
        a["e_b1"] = c(v["L0_ffn_exp_b1"].reshape(E, FH // P, P).transpose(2, 0, 1))
        a["e_b2"] = c(v["L0_ffn_exp_b2"].reshape(E, 1, D))

STAGES = 3


def kernel(**inputs):
    import concourse.bacc as bacc
    from concourse.bass_utils import run_bass_kernel_spmd

    arrays = layouts({k: np.asarray(v) for k, v in inputs.items()})
    nc = bacc.Bacc("TRN2", target_bir_lowering=False, num_devices=1)
    io = {k: nc.dram_tensor("in_" + k, a.shape, mybir.dt.from_np(a.dtype), kind="ExternalInput").ap() for k, a in arrays.items()}
    out = nc.dram_tensor("out_0", (P, GRP, D), F32, kind="ExternalOutput").ap()
    program(nc, io, out)
    r = run_bass_kernel_spmd(nc, [{"in_" + k: a for k, a in arrays.items()}], core_ids=[0])
    return np.ascontiguousarray(r.results[0]["out_0"].transpose(1, 0, 2)).reshape(B, L, D)
```

```python
from contextlib import ExitStack

import concourse.bass as bass
import numpy as np
from concourse import mybir

F32 = mybir.dt.float32
F32R = mybir.dt.float32r
ALU = mybir.AluOpType
ACT = mybir.ActivationFunctionType
AXX = mybir.AxisListType.X

P = 128
B, L, D = 64, 32, 256
S = 257
H, DH = 8, 64
GRP = B * L // P
BPG = P // L
KEYS = S + L
TAIL = KEYS - 256
EPS = 1e-5


def mm3(eng, out, a, b, start, stop):
    eng.matmul(out, a[0], b[0], start=start, stop=False)
    eng.matmul(out, a[0], b[1], start=False, stop=False)
    return eng.matmul(out, a[1], b[0], start=False, stop=stop)


def wait_ahead(dve, sem, value, tick):
    dve.wait_ge(sem, value)
    dve.memset(tick[:, :], 0.0)


def latents_phase(nc, sem, io, X, kv):
    qT, KX, xe = kv["qT"], kv["KX"], kv["xe"]
    C = 4
    with ExitStack() as ctx:
        def sb(name, shape, dt=F32):
            return ctx.enter_context(nc.sbuf_tensor("l_" + name, shape, dt))

        wq = sb("wq", [P, 2, 512])
        wk = sb("wk", [P, 2, 512])
        gb = sb("gb", [P, 4, D])
        ident = sb("ident", [P, P])
        edge = sb("edge", [P, 2])
        last = sb("last", [B, D])
        n1 = sb("n1", [P, GRP, D])
        ln = sb("ln", [P, GRP, D])
        st = sb("st", [P, GRP, 6])
        mv = sb("mv", [P, GRP, 2])
        ve = sb("ve", [P, GRP])
        rs = sb("rs", [P, GRP])
        half = sb("half", [P, GRP])
        st2 = sb("st2", [B, 6])
        mv2 = sb("mv2", [B, 2])
        ve2 = sb("ve2", [B, 2])
        xl = sb("xl", [B, D])
        lnT = sb("lnT", [P, 2, 2, 512])
        lastT = sb("lastT", [P, 2, B])
        t1 = sb("t1", [P, 2, B])
        t2 = sb("t2", [P, 2, B])
        psT = ctx.enter_context(nc.psum_tensor("l_psT", [P, 2, 512], F32))
        psJ = ctx.enter_context(nc.psum_tensor("l_psJ", [P, 4, 512], F32))
        psL = ctx.enter_context(nc.psum_tensor("l_psL", [P, 2, 512], F32))

        x_in, w_in = sem("l_x_in"), sem("l_w_in")
        half_set, stats, aggr, var, rstd = (sem("l_" + n) for n in ("half_set", "stats", "aggr", "var", "rstd"))
        norm, scaled, ln_ready = sem("l_norm"), sem("l_scaled"), sem("l_ln_ready")
        turned, turned_out, proj, proj_out = (sem("l_" + n) for n in ("turned", "turned_out", "proj", "proj_out"))
        stored = sem("l_stored")
        last_ready, last_var, last_rstd, last_t, last_tout, last_k, last_mul, last_keys = (
            sem("l_last" + n) for n in "abcdefgh")
        block = ctx.enter_context(nc.Block())

        @block.sync
        def _(sp):
            sp.dma_start(X[:, :, :], io["x"]).then_inc(x_in, 16)
            for dst, src in ((gb, "gb"), (ident, "ident"), (wq, "wq"), (wk, "wk"), (edge, "edge"), (last, "ctx_last")):
                d = dst.ap() if not hasattr(dst, "__getitem__") else dst
                sp.dma_start(d[tuple(slice(None) for _ in dst.shape)], io[src]).then_inc(w_in, 16)
            for c in range(C):
                sp.wait_ge(ln_ready, c + 1)
                for g in range(4 * c, 4 * c + 4):
                    for b in range(BPG):
                        sp.dma_start(xe[4 * g + b, 0:L, :], ln[L * b:L * b + L, g, :]).then_inc(stored, 16)
            sp.wait_ge(last_ready, 4)
            sp.dma_start(xe[:, L, :], xl[:, :]).then_inc(stored, 16)
            sp.wait_ge(stored, 16 * (B + 1))

        @block.gpsimd
        def _(pool):
            pool.memset(half[:, :], -0.5).then_inc(half_set, 1)
            pool.wait_ge(half_set, 1)
            for i in range(2 * C):
                c = i // 2
                pool.wait_ge(var, i + 1)
                pool.tensor_tensor(rs[:, 4 * c:4 * c + 4], ve[:, 4 * c:4 * c + 4], half[:, 0:4], ALU.pow).then_inc(rstd, 1)
            pool.wait_ge(last_var, 1)
            pool.tensor_tensor(ve2[:, 1:2], ve2[:, 0:1], half[0:B, 0:1], ALU.pow).then_inc(last_rstd, 1)

        @block.vector
        def _(dve):
            dve.wait_ge(x_in, 16)
            dve.wait_ge(w_in, 96)

            def layer_norm(i, c, src, dst):
                for g in range(4 * c, 4 * c + 4):
                    dve.bn_stats(st[:, g, :], src[:, g, :]).then_inc(stats, 1)
                dve.wait_ge(stats, 4 * (i + 1))
                for g in range(4 * c, 4 * c + 4):
                    dve.bn_aggr(mv[:, g, :], st[:, g, :]).then_inc(aggr, 1)
                dve.wait_ge(aggr, 4 * (i + 1))
                dve.tensor_scalar(ve[:, 4 * c:4 * c + 4], mv[:, 4 * c:4 * c + 4, 1], EPS, None, ALU.add).then_inc(var, 1)
                dve.wait_ge(rstd, i + 1)
                for g in range(4 * c, 4 * c + 4):
                    dve.tensor_scalar(dst[:, g, :], src[:, g, :], mv[:, g, 0:1], rs[:, g:g + 1],
                                      ALU.subtract, ALU.mult).then_inc(norm, 1)
                dve.wait_ge(norm, 4 * (i + 1))

            for c in range(C):
                a, z = 4 * c, 4 * c + 4
                layer_norm(2 * c, c, X, n1)
                layer_norm(2 * c + 1, c, n1, ln)
                dve.tensor_tensor(ln[:, a:z, :], ln[:, a:z, :], gb[:, 2:3, :].to_broadcast([P, 4, D]),
                                  ALU.mult).then_inc(scaled, 1)
                dve.wait_ge(scaled, c + 1)
                dve.tensor_tensor(ln[:, a:z, :], ln[:, a:z, :], gb[:, 3:4, :].to_broadcast([P, 4, D]),
                                  ALU.add).then_inc(ln_ready, 1)
            dve.bn_stats(st2[:, :], last[:, :]).then_inc(last_ready, 1)
            dve.wait_ge(last_ready, 1)
            dve.bn_aggr(mv2[:, :], st2[:, :]).then_inc(last_ready, 1)
            dve.wait_ge(last_ready, 2)
            dve.tensor_scalar(ve2[:, 0:1], mv2[:, 1:2], EPS, None, ALU.add).then_inc(last_var, 1)
            dve.scalar_tensor_tensor(xl[:, :], last[:, :], mv2[:, 0:1], gb[0:B, 0, :],
                                     ALU.subtract, ALU.mult).then_inc(last_ready, 1)
            dve.wait_ge(last_ready, 3)
            dve.wait_ge(last_rstd, 1)
            dve.scalar_tensor_tensor(xl[:, :], xl[:, :], ve2[:, 1:2], gb[0:B, 1, :],
                                     ALU.mult, ALU.add).then_inc(last_ready, 1)
            dve.wait_ge(last_k, 1)
            k = psL[:, 1, 0:4 * B].rearrange("p (g a b) -> p g a b", g=2, a=2)
            dve.tensor_scalar(t1[:, :, :], k[:, :, 1, :], edge[:, 1:2], None, ALU.mult).then_inc(last_mul, 1)
            dve.tensor_scalar(t2[:, :, :], k[:, :, 0, :], edge[:, 1:2], None, ALU.mult).then_inc(last_mul, 1)
            dve.wait_ge(last_mul, 2)
            for g in range(2):
                dve.scalar_tensor_tensor(KX[:, 2 * g, :, L], k[:, g, 0, :], edge[:, 0:1], t1[:, g, :],
                                         ALU.mult, ALU.subtract)
                dve.scalar_tensor_tensor(KX[:, 2 * g + 1, :, L], k[:, g, 1, :], edge[:, 0:1], t2[:, g, :],
                                         ALU.mult, ALU.add).then_inc(last_keys, 1)

        @block.tensor
        def _(pe):
            pe.wait_ge(w_in, 96)
            n = 0
            for c in range(C):
                pe.wait_ge(ln_ready, c + 1)
                if c:
                    pe.wait_ge(turned_out, c)
                for k in range(2):
                    for j in range(4):
                        t = pe.transpose(psT[:, k, j * P:(j + 1) * P], ln[:, 4 * c + j, k * P:(k + 1) * P], ident[:, :])
                t.then_inc(turned, 1)
                pe.wait_ge(turned_out, c + 1)
                for w in (wq, wk):
                    for m in range(4):
                        if n >= 4:
                            pe.wait_ge(proj_out, n - 3)
                        for k in range(2):
                            t = pe.matmul(psJ[:, n % 4, :], w[:, k, m * P:(m + 1) * P], lnT[:, c % 2, k, :],
                                          start=(k == 0), stop=(k == 1))
                        t.then_inc(proj, 1)
                        n += 1
            pe.wait_ge(last_ready, 4)
            for k in range(2):
                t = pe.transpose(psL[:, 0, k * B:(k + 1) * B], xl[:, k * P:(k + 1) * P], ident[0:B, 0:B])
            t.then_inc(last_t, 1)
            pe.wait_ge(last_tout, 1)
            for m in range(4):
                for k in range(2):
                    t = pe.matmul(psL[:, 1, m * B:(m + 1) * B], wk[:, k, m * P:(m + 1) * P], lastT[:, k, :],
                                  start=(k == 0), stop=(k == 1))
            t.then_inc(last_k, 1)

        @block.scalar
        def _(act):
            n = 0
            for c in range(C):
                act.wait_ge(turned, c + 1)
                if c >= 2:
                    act.wait_ge(proj, 8 * (c - 1))
                act.activation(lnT[:, c % 2, :, :], psT[:, :, :], ACT.Copy).then_inc(turned_out, 1)
                for w in range(2):
                    for m in range(4):
                        act.wait_ge(proj, n + 1)
                        if w == 0:
                            act.activation(qT[:, m, 512 * c:512 * c + 512], psJ[:, n % 4, :], ACT.Copy,
                                           scale=DH ** -0.5).then_inc(proj_out, 1)
                        else:
                            act.activation(KX[:, m, 16 * c:16 * c + 16, 0:L],
                                           psJ[:, n % 4, :].rearrange("p (b i) -> p b i", i=L),
                                           ACT.Copy).then_inc(proj_out, 1)
                        n += 1
            act.wait_ge(last_t, 1)
            act.activation(lastT[:, :, :], psL[:, 0, 0:2 * B].rearrange("p (k b) -> p k b", k=2),
                           ACT.Copy).then_inc(last_tout, 1)


def xattn_phase(nc, sem, io, X, kv):
    qT, KX, xe = kv["qT"], kv["KX"], kv["xe"]
    with ExitStack() as ctx:
        def sb(name, shape, dt=F32):
            return ctx.enter_context(nc.sbuf_tensor("a_" + name, shape, dt))

        def pb(name, shape):
            return ctx.enter_context(nc.psum_tensor("a_" + name, shape, F32))

        wk = sb("wk", [P, 2, 512])
        wkh, wkl = sb("wkh", [P, 2, 512], F32R), sb("wkl", [P, 2, 512], F32R)
        wv = sb("wv", [P, 2, 512])
        wo = sb("wo", [P, 4, D])
        gb = sb("gb", [P, 4, D])
        ident = sb("ident", [P, P])
        cos = sb("cos", [P, 256])
        sin = sb("sin", [P, 2, 256])
        C = [sb(f"C{i}", [P, 2, D]) for i in range(2)]
        cen = [sb(f"cen{i}", [P, 2, D]) for i in range(2)]
        xn = [sb(f"xn{i}", [P, 2, D]) for i in range(4)]
        xt = [sb(f"xt{i}", [TAIL, D]) for i in range(4)]
        xh = [sb(f"xh{i}", [P, 2, 256], F32R) for i in range(2)]
        xl = [sb(f"xl{i}", [P, 2, 256], F32R) for i in range(2)]
        st = [sb(f"st{i}", [P, 2, 6]) for i in range(2)]
        mv = [sb(f"mv{i}", [P, 2, 2]) for i in range(2)]
        ve = [sb(f"ve{i}", [P, 2]) for i in range(2)]
        rs = [sb(f"rs{i}", [P, 2]) for i in range(2)]
        tick = sb("tick", [P, 1])
        half = sb("half", [P, 2])
        r1 = [sb(f"r1{i}", [P, 2, 256]) for i in range(2)]
        r2 = [sb(f"r2{i}", [P, 2, 256]) for i in range(2)]
        K = [sb(f"K{i}", [P, 4, KEYS]) for i in range(2)]
        Q = [sb(f"Q{i}", [P, 4, P]) for i in range(2)]
        mx = [sb(f"mx{i}", [P, 2]) for i in range(2)]
        nm = [sb(f"nm{i}", [P, 2]) for i in range(2)]
        sm = [sb(f"sm{i}", [P, 2]) for i in range(2)]
        ri = [sb(f"ri{i}", [P, 2]) for i in range(2)]
        pr = [sb(f"pr{i}", [P, 2, KEYS]) for i in range(2)]
        pT = [sb(f"pT{i}", [P, 3, 256]) for i in range(2)]
        px = sb("px", [P, 2, H, BPG, L])
        uT = sb("uT", [P, 4, P])

        psT = pb("psT", [P, 2, 256])
        psK = [pb(f"psK{i}", [P, 2, 256]) for i in range(2)]
        psS = [pb(f"psS{i}", [P, 512]) for i in range(2)]
        psP = [pb(f"psP{i}", [P, 512]) for i in range(2)]
        psV = pb("psV", [P, 512])

        names = ("w_in", "w_hi", "w_lo", "half_set", "zeroed", "stats", "aggr", "var", "rstd", "centred", "normed",
                 "turned", "xt_hi", "xt_lo", "projected", "rotated", "keys", "tails", "blocks", "scored", "peak",
                 "peak_neg", "exped", "recip", "probs", "pturned", "pt_out", "attended", "px_out", "valued", "u_out",
                 "outed", "added")
        s = {n: sem("a_" + n) for n in names}
        c_in = [sem(f"a_c_in{i}") for i in range(2)]
        t_in = [sem(f"a_t_in{i}") for i in range(4)]
        block = ctx.enter_context(nc.Block())
        LASTG = GRP - 1


        @block.sync
        def _(sp):
            for dst, src in ((wk, "wk"), (gb, "gb"), (ident, "ident"), (cos, "cos"), (wv, "wv")):
                sp.dma_start(dst[tuple(slice(None) for _ in dst.shape)], io[src]).then_inc(s["w_in"], 16)
            sp.dma_start(sin[:, :, :], io["sin"]).then_inc(s["w_in"], 16)
            sp.dma_start(wo[:, :, :], io["wo"]).then_inc(s["w_in"], 16)

            def load(g, j, first=False):
                n = 4 * g + j
                if not (first and j < 2):
                    sp.wait_ge(s["normed"], n - 1)
                sp.dma_start(C[j % 2][:, :, :], io["ctx"][n]).then_inc(c_in[j % 2], 16)

            def load_tail(g, j, first=False):
                if not first:
                    sp.wait_ge(s["attended"], 4 * g + j - 3)
                sp.dma_start(xt[j][:, :], xe[4 * g + j]).then_inc(t_in[j], 16)

            for j in range(4):
                load(0, j, True)
                if j >= 2:
                    load_tail(0, j - 2, True)
            load(1, 0)
            load_tail(0, 2, True)
            load(1, 1)
            load_tail(0, 3, True)
            load(1, 2)
            load_tail(1, 0)
            load(1, 3)
            load_tail(1, 1)
            with sp.Fori(2, GRP) as g:
                for j in range(4):
                    load(g, j)
                    load_tail(g - (j < 2), (j + 2) % 4)
            load_tail(LASTG, 2)
            load_tail(LASTG, 3)

        @block.gpsimd
        def _(pool):
            pool.memset(half[:, :], -0.5).then_inc(s["half_set"], 1)
            for i in range(2):
                pool.memset(Q[i][:, :, :], 0.0).then_inc(s["zeroed"], 1)
            pool.wait_ge(s["half_set"], 1)

            def power(g, j):
                n = 4 * g + j
                pool.wait_ge(s["var"], n + 1)
                pool.tensor_tensor(rs[j % 2][:, :], ve[j % 2][:, :], half[:, :], ALU.pow).then_inc(s["rstd"], 1)

            def rope_add(g, j, G, first=False):
                n = 4 * g + j
                if not (first and j < 2) and G == 0:
                    pool.wait_ge(s["scored"], 2 * (n - 1))
                pool.wait_ge(s["rotated"], 3 * (2 * n + G + 1))
                pool.tensor_tensor(K[j % 2][:, 2 * G:2 * G + 2, 0:256], r1[G][:, :, :], r2[G][:, :, :],
                                   ALU.add).then_inc(s["keys"], 1)

            def slot(g, j, first=False, last=False):
                rope_add(g, j, 0, first)
                if not (last and j >= 2):
                    power(g, j + 2) if j < 2 else power(g + 1, j - 2)
                rope_add(g, j, 1, first)

            power(0, 0)
            power(0, 1)
            for j in range(4):
                slot(0, j, first=True)
            with pool.Fori(1, LASTG) as g:
                for j in range(4):
                    slot(g, j)
            for j in range(4):
                slot(LASTG, j, last=True)

        @block.vector
        def _(dve):
            dve.wait_ge(s["w_in"], 16 * 7)
            dve.tensor_copy(wkh[:, :, :], wk[:, :, :]).then_inc(s["w_hi"], 1)
            dve.wait_ge(s["w_hi"], 1)
            dve.tensor_tensor(wkl[:, :, :], wk[:, :, :], wkh[:, :, :].bitcast(F32), ALU.subtract).then_inc(s["w_lo"], 1)

            def statistics(g, j):
                n = 4 * g + j
                dve.wait_ge(c_in[j % 2], 16 * (2 * g + j // 2 + 1))
                for t in range(2):
                    dve.bn_stats(st[j % 2][:, t, :], C[j % 2][:, t, :]).then_inc(s["stats"], 1)
                wait_ahead(dve, s["stats"], 2 * (n + 1), tick)
                for t in range(2):
                    dve.bn_aggr(mv[j % 2][:, t, :], st[j % 2][:, t, :]).then_inc(s["aggr"], 1)
                dve.wait_ge(s["aggr"], 2 * (n + 1))
                dve.tensor_scalar(ve[j % 2][:, :], mv[j % 2][:, :, 1], EPS, None, ALU.add).then_inc(s["var"], 1)

            def normalise(g, j, first=False):
                n = 4 * g + j
                for t in range(2):
                    dve.scalar_tensor_tensor(cen[j % 2][:, t, :], C[j % 2][:, t, :], mv[j % 2][:, t, 0:1], gb[:, 0, :],
                                             ALU.subtract, ALU.mult).then_inc(s["centred"], 1)
                dve.wait_ge(s["rstd"], n + 1)
                dve.wait_ge(s["centred"], 2 * (n + 1))
                if not first:
                    dve.wait_ge(s["attended"], n - 3)
                dve.scalar_tensor_tensor(xn[j][:, 0, :], cen[j % 2][:, 0, :], rs[j % 2][:, 0:1], gb[:, 1, :],
                                         ALU.mult, ALU.add)
                dve.scalar_tensor_tensor(xn[j][:, 1, :], cen[j % 2][:, 1, :], rs[j % 2][:, 1:2], gb[:, 1, :],
                                         ALU.mult, ALU.add).then_inc(s["normed"], 1)

            def low(g, j):
                n = 4 * g + j
                dve.wait_ge(s["xt_hi"], n + 1)
                dve.tensor_tensor(xl[j % 2][:, :, :], psT[:, :, :], xh[j % 2][:, :, :].bitcast(F32),
                                  ALU.subtract).then_inc(s["xt_lo"], 1)

            def rotate(g, j, G, first=False):
                n = 4 * g + j
                dve.wait_ge(s["projected"], 2 * n + G + 1)
                if not (first and j == 0):
                    dve.wait_ge(s["keys"], 2 * n + G - 1)
                dve.tensor_tensor(r1[G][:, :, :], psK[G][:, :, :], cos[:, :].unsqueeze(1).to_broadcast([P, 2, 256]),
                                  ALU.mult).then_inc(s["rotated"], 1)
                for a in range(2):
                    dve.tensor_tensor(r2[G][:, a, :], psK[G][:, 1 - a, :], sin[:, a, :], ALU.mult).then_inc(s["rotated"], 1)

            def peaks(g, j):
                n = 4 * g + j
                for G in range(2):
                    dve.wait_ge(s["scored"], 2 * n + G + 1)
                    dve.reduce_max(mx[j % 2][:, G:G + 1], psS[G][:, 0:KEYS], AXX).then_inc(s["peak"], 1)
                dve.wait_ge(s["peak"], 2 * (n + 1))
                dve.tensor_scalar(nm[j % 2][:, :], mx[j % 2][:, :], -1.0, None, ALU.mult).then_inc(s["peak_neg"], 1)

            def shares(g, j):
                n = 4 * g + j
                dve.wait_ge(s["exped"], 2 * (n + 1))
                dve.reciprocal(ri[j % 2][:, :], sm[j % 2][:, :]).then_inc(s["recip"], 1)
                dve.wait_ge(s["recip"], n + 1)
                for G in range(2):
                    dve.tensor_scalar(pr[j % 2][:, G, :], pr[j % 2][:, G, :], ri[j % 2][:, G:G + 1], None,
                                      ALU.mult).then_inc(s["probs"], 1)

            def residual(g):
                dve.wait_ge(s["outed"], g + 1)
                dve.tensor_tensor(X[:, g, :], X[:, g, :], psV[:, 0:D], ALU.add).then_inc(s["added"], 1)

            def slot(g, j, first=False, last=False, batches=(True, True)):
                prev = (g, j - 1) if j else (g - 1, 3)
                if batches[0] and not (last and j == 3):
                    normalise(g + (j + 1) // 4, (j + 1) % 4, first and j < 3)
                if batches[0]:
                    rotate(g, j, 0, first)
                if batches[1] and not (first and j == 0):
                    peaks(*prev)
                if batches[0] and not (last and j == 3):
                    low(g + (j + 1) // 4, (j + 1) % 4)
                if batches[0] and not (last and j >= 2):
                    statistics(g + (j + 2) // 4, (j + 2) % 4)
                if batches[1] and not (first and j == 0):
                    shares(*prev)
                if j == 2 and not first:
                    residual(g - 1)
                if batches[0]:
                    rotate(g, j, 1, first)

            for j in range(2):
                statistics(0, j)
            normalise(0, 0, True)
            low(0, 0)
            for j in range(4):
                slot(0, j, first=True)
            with dve.Fori(1, LASTG) as g:
                for j in range(4):
                    slot(g, j)
            for j in range(4):
                slot(LASTG, j, last=True)
            slot(GRP, 0, batches=(False, True))
            slot(GRP, 2, batches=(False, False))

        @block.scalar
        def _(act):
            act.wait_ge(s["zeroed"], 2)

            def operands(g, j, first=False):
                n = 4 * g + j
                if not (first and j < 2):
                    act.wait_ge(s["scored"], 2 * (n - 1))
                act.activation(K[j % 2][:, :, 256:KEYS], KX[:, :, n, :], ACT.Copy).then_inc(s["tails"], 1)
                for h in range(4):
                    act.activation(Q[j % 2][32 * h:32 * h + 32, :, 32 * h:32 * h + 32],
                                   qT[32 * h:32 * h + 32, :, bass.ds(n * L, L)], ACT.Copy).then_inc(s["blocks"], 1)

            def high(g, j, first=False):
                n = 4 * g + j
                act.wait_ge(s["turned"], n + 1)
                if not (first and j < 2):
                    act.wait_ge(s["projected"], 2 * (n - 1))
                act.activation(xh[j % 2][:, :, :], psT[:, :, :], ACT.Copy).then_inc(s["xt_hi"], 1)

            def exps(g, j, first=False):
                n = 4 * g + j
                act.wait_ge(s["peak_neg"], n + 1)
                if not (first and j < 2):
                    act.wait_ge(s["pturned"], 2 * (n - 1))
                for G in range(2):
                    act.activation(pr[j % 2][:, G, :], psS[G][:, 0:KEYS], ACT.Exp, bias=nm[j % 2][:, G:G + 1],
                                   accum_out=sm[j % 2][:, G:G + 1]).then_inc(s["exped"], 1)

            def turned_probs(g, j, first=False):
                n = 4 * g + j
                if not (first and j < 2):
                    act.wait_ge(s["attended"], n - 1)
                for G in range(2):
                    act.wait_ge(s["pturned"], 2 * n + G + 1)
                    p3 = psP[G][:, 0:384].rearrange("p (t c) -> p t c", t=3)
                    act.activation(pT[j % 2][:, 0:2, G * P:(G + 1) * P], p3[:, 0:2, :], ACT.Copy).then_inc(s["pt_out"], 1)
                    act.activation(pT[j % 2][0:TAIL, 2, G * P:(G + 1) * P], p3[0:TAIL, 2, :],
                                   ACT.Copy).then_inc(s["pt_out"], 1)

            def mixed(g, j, first=False):
                n = 4 * g + j
                act.wait_ge(s["attended"], n + 1)
                if j == 0 and not first:
                    act.wait_ge(s["valued"], g)
                for k in range(2):
                    act.activation(px[:, k, :, j, :], psV[:, 256 * k:256 * k + 256].rearrange("p (h i) -> p h i", h=H),
                                   ACT.Copy).then_inc(s["px_out"], 1)

            def values(g):
                act.wait_ge(s["valued"], g + 1)
                act.activation(uT[:, :, :], psV[:, :].rearrange("p (m t) -> p m t", m=4), ACT.Copy).then_inc(s["u_out"], 1)

            def slot(g, j, first=False, last=False, batches=(True, True)):
                prev = (g, j - 1) if j else (g - 1, 3)
                prev2 = (g, j - 2) if j >= 2 else (g - 1, j + 2)
                if j == 2 and not first:
                    values(g - 1)
                attends = not (first and j < 2) and not (not batches[0] and j == 2)
                if batches[0]:
                    operands(g, j, first)
                if attends:
                    turned_probs(*prev2, first)
                if batches[0] and not (last and j == 3):
                    high(g + (j + 1) // 4, (j + 1) % 4, first and j == 0)
                if batches[1] and not (first and j == 0):
                    exps(*prev, first and j - 1 < 2)
                if attends:
                    mixed(*prev2, first)

            high(0, 0, True)
            for j in range(4):
                slot(0, j, first=True)
            with act.Fori(1, LASTG) as g:
                for j in range(4):
                    slot(g, j)
            for j in range(4):
                slot(LASTG, j, last=True)
            slot(GRP, 0, batches=(False, True))
            slot(GRP, 1, batches=(False, False))
            slot(GRP, 2, batches=(False, False))

        @block.tensor
        def _(pe):
            pe.wait_ge(s["w_lo"], 1)

            def turn(g, j, first=False):
                n = 4 * g + j
                pe.wait_ge(s["normed"], n + 1)
                if not (first and j == 0):
                    pe.wait_ge(s["xt_lo"], n)
                for k in range(2):
                    for t in range(2):
                        i = pe.transpose(psT[:, k, t * P:(t + 1) * P], xn[j][:, t, k * P:(k + 1) * P], ident[:, :])
                i.then_inc(s["turned"], 1)

            def project(g, j, G, first=False):
                n = 4 * g + j
                if G == 0:
                    pe.wait_ge(s["xt_lo"], n + 1)
                if not (first and j == 0):
                    pe.wait_ge(s["rotated"], 3 * (2 * n + G - 1))
                for a in range(2):
                    m = 2 * G + a
                    for k in range(2):
                        i = mm3(pe, psK[G][:, a, :], (wkh[:, k, m * P:(m + 1) * P], wkl[:, k, m * P:(m + 1) * P]),
                                (xh[j % 2][:, k, :], xl[j % 2][:, k, :]), k == 0, k == 1)
                i.then_inc(s["projected"], 1)

            def score(g, j, first=False):
                n = 4 * g + j
                pe.wait_ge(s["tails"], n + 1)
                pe.wait_ge(s["blocks"], 4 * (n + 1))
                for G in range(2):
                    pe.wait_ge(s["keys"], 2 * n + G + 1)
                    if not (first and j == 0):
                        pe.wait_ge(s["exped"], 2 * n + G - 1)
                    for a in range(2):
                        i = pe.matmul(psS[G][:, 0:KEYS], Q[j % 2][:, 2 * G + a, :], K[j % 2][:, 2 * G + a, :],
                                      start=(a == 0), stop=(a == 1))
                    i.then_inc(s["scored"], 1)

            def turn_probs(g, j, first=False):
                n = 4 * g + j
                pe.wait_ge(s["probs"], 2 * (n + 1))
                for G in range(2):
                    if not (first and j == 0):
                        pe.wait_ge(s["pt_out"], 2 * (2 * n + G - 1))
                    for t in range(3):
                        w = P if t < 2 else TAIL
                        i = pe.transpose(psP[G][0:w, t * P:(t + 1) * P], pr[j % 2][:, G, t * P:t * P + w], ident[:, :])
                    i.then_inc(s["pturned"], 1)

            def attend(g, j, first=False):
                n = 4 * g + j
                pe.wait_ge(s["pt_out"], 4 * (n + 1))
                pe.wait_ge(t_in[j], 16 * (g + 1))
                if not (first and j == 0):
                    pe.wait_ge(s["px_out"], 2 * n)
                for k in range(2):
                    for t in range(3):
                        w, v = (P, xn[j][:, t, k * P:(k + 1) * P]) if t < 2 else (TAIL, xt[j][:, k * P:(k + 1) * P])
                        i = pe.matmul(psV[:, 256 * k:256 * k + 256], v, pT[j % 2][0:w, t, :], start=(t == 0), stop=(t == 2))
                i.then_inc(s["attended"], 1)

            def value(g):
                pe.wait_ge(s["px_out"], 8 * (g + 1))
                for h in range(H):
                    for k in range(2):
                        i = pe.matmul(psV[64 * (h % 2):64 * (h % 2) + 64, P * (h // 2):P * (h // 2) + P],
                                      wv[:, k, DH * h:DH * h + DH], px[:, k, h, :, :], start=(k == 0), stop=(k == 1))
                i.then_inc(s["valued"], 1)

            def out(g):
                pe.wait_ge(s["u_out"], g + 1)
                for m in range(4):
                    i = pe.matmul(psV[:, 0:D], uT[:, m, :], wo[:, m, :], start=(m == 0), stop=(m == 3))
                i.then_inc(s["outed"], 1)

            def slot(g, j, first=False, last=False, batches=(True, True)):
                prev = (g, j - 1) if j else (g - 1, 3)
                prev2 = (g, j - 2) if j >= 2 else (g - 1, j + 2)
                attends = not (first and j < 2) and not (not batches[0] and j == 2)
                if batches[0]:
                    project(g, j, 0, first)
                if attends:
                    turn_probs(*prev2, first)
                if j == 2 and not first:
                    value(g - 1)
                if batches[1] and not (first and j == 0):
                    score(*prev, first)
                if batches[0] and not (last and j == 3):
                    turn(g + (j + 1) // 4, (j + 1) % 4)
                if j == 2 and not first:
                    out(g - 1)
                if batches[0]:
                    project(g, j, 1, first)
                if attends:
                    if j == 2 and not first:
                        pe.wait_ge(s["added"], g)
                    attend(*prev2, first)

            turn(0, 0, True)
            for j in range(4):
                slot(0, j, first=True)
            with pe.Fori(1, LASTG) as g:
                for j in range(4):
                    slot(g, j)
            for j in range(4):
                slot(LASTG, j, last=True)
            slot(GRP, 0, batches=(False, True))
            slot(GRP, 1, batches=(False, False))
            slot(GRP, 2, batches=(False, False))

DI, NH, CONVT, ZT = 512, 8, 6, 4


def past(eng, sem, value):
    if isinstance(value, int) and value <= 0:
        return
    eng.wait_ge(sem, value)


def slots(eng, slot, units, peeled, depth):
    for n in range(peeled):
        slot(n, n % 2)
    with eng.Fori(peeled // 2, units // 2 - 1) as i:
        slot(2 * i, 0)
        slot(2 * i + 1, 1)
    for n in range(units - 2, units + depth):
        slot(n, n % 2)


def unit(n):
    return not isinstance(n, int) or 0 <= n < GRP


def mamba_phase(nc, sem, io, X):
    with ExitStack() as ctx:
        def sb(name, shape, dt=F32):
            return ctx.enter_context(nc.sbuf_tensor("m_" + name, shape, dt))

        def pb(name, shape):
            return ctx.enter_context(nc.psum_tensor("m_" + name, shape, F32))

        DIN = 2 * DI + 2 * P
        w = sb("w", [P, 2, DIN + NH])
        wh, wl = sb("wh", [P, 2, DIN], F32R), sb("wl", [P, 2, DIN], F32R)
        wout = sb("wout", [P, 4, D])
        ident = sb("ident", [P, P])
        tri = sb("tri", [P, P])
        aft = sb("aft", [P, P])
        cols = sb("cols", [P, CONVT * 5 + 8])
        rows = sb("rows", [P, 2, NH])
        A = sb("A", [P, NH])
        tick = sb("tick", [P, 1])
        half = sb("half", [P, 1])
        ones = sb("ones", [P, 1])
        xn = [sb(f"xn{i}", [P, D]) for i in range(2)]
        xh = [sb(f"xh{i}", [P, 2, P], F32R) for i in range(2)]
        xl = [sb(f"xl{i}", [P, 2, P], F32R) for i in range(2)]
        st = sb("st", [P, 2, 6])
        mv = sb("mv", [P, 2, 2])
        ve = sb("ve", [P, 2])
        rs = sb("rs", [P, 2])
        pad = sb("pad", [P, CONVT, BPG, L + 3])
        acc = sb("acc", [P, CONVT, P])
        xa = [sb(f"xa{i}", [P, CONVT, P]) for i in range(2)]
        zs = [sb(f"zs{i}", [P, ZT, P]) for i in range(2)]
        sp = sb("sp", [P, 8, NH])
        dt = sb("dt", [P, GRP, NH])
        da = sb("da", [P, GRP, NH])
        ta = sb("ta", [P, NH, P])
        dec = sb("dec", [P, NH, P])
        gm = sb("gm", [P, P])
        mm = sb("mm", [P, NH, P])
        xd = sb("xd", [P, DI])
        yd = sb("yd", [P, ZT, P])
        yz = [sb(f"yz{i}", [P, ZT, P]) for i in range(2)]
        y2 = [sb(f"y2{i}", [P, ZT, P]) for i in range(2)]
        fe = sb("fe", [P, 2])
        fr = sb("fr", [P, 2])

        psT = pb("psT", [P, 512])
        psA = pb("psA", [P, 4, P])
        psB = pb("psB", [P, 512])
        psO = pb("psO", [P, 512])
        psL = pb("psL", [P, 2, 4, P])
        psX = pb("psX", [P, 512])
        psY = pb("psY", [P, 4, P])
        DT, SS = psT[:, 256:256 + NH], psO[:, 256:257]

        s = {n: sem("m_" + n) for n in (
            "w_in", "w_hi", "w_lo", "consts", "a_exp", "a_set", "wout_set",
            "stats", "aggr", "var", "rstd", "xn", "added", "turned", "xt_hi", "xt_lo",
            "projA", "projB", "projZ", "dt_mm", "padA", "padB", "tap", "taps", "conv", "xact", "zact",
            "sp_v", "sp_n", "sp_min", "sp_exp", "sp_u", "sp_ln", "sp_c", "sp_s", "dt", "da",
            "ta", "logs", "dec", "cb", "gm", "mm", "xturn", "xd", "y", "yd", "yz", "y2",
            "out", "f_var", "f_rstd", "f_out")}
        block = ctx.enter_context(nc.Block())
        WIN = 7
        tap = lambda m, k: cols[:, 4 * m + k:4 * m + k + 1]
        cbias = lambda m: cols[:, 24 + m:25 + m]
        skip = lambda q: cols[:, 30 + q:31 + q]
        normw = lambda q: cols[:, 34 + q:35 + q]

        @block.sync
        def _(sy):
            for d, src in ((w, "m_w"), (cols, "m_cols"), (rows, "m_rows"), (ident, "ident"), (tri, "tri"), (aft, "aft"),
                           (wout, "m_out")):
                sy.dma_start(d[tuple(slice(None) for _ in d.shape)], io[src]).then_inc(s["w_in"], 16)
            sy.wait_ge(s["w_in"], 16 * WIN)

        @block.gpsimd
        def _(pool):
            pool.memset(half[:, :], -0.5).then_inc(s["consts"], 1)
            pool.memset(ones[:, :], 1.0).then_inc(s["consts"], 1)
            pool.memset(pad[:, :, :, :], 0.0).then_inc(s["consts"], 1)
            pool.wait_ge(s["consts"], 3)
            pool.wait_ge(s["w_in"], 16 * WIN)

            def ln_power(n, p):
                if not unit(n):
                    return
                pool.wait_ge(s["var"], n + 1)
                pool.tensor_tensor(rs[:, p:p + 1], ve[:, p:p + 1], half[:, :], ALU.pow).then_inc(s["rstd"], 1)

            def ln_add(n, p):
                if not unit(n):
                    return
                pool.wait_ge(s["xn"], n + 1)
                pool.tensor_tensor(X[:, n, :], X[:, n, :], xn[p][:, :], ALU.add).then_inc(s["added"], 1)

            def decays(n):
                if not unit(n):
                    return
                pool.wait_ge(s["da"], n + 1)
                past(pool, s["logs"], n)
                pool.tensor_tensor(ta[:, :, :], tri[:, :].unsqueeze(1).to_broadcast([P, NH, P]),
                                   da[:, n, :].unsqueeze(2).to_broadcast([P, NH, P]), ALU.mult).then_inc(s["ta"], 1)

            def out_power(n, p):
                if not unit(n):
                    return
                pool.wait_ge(s["f_var"], n + 1)
                pool.tensor_tensor(fr[:, p:p + 1], fe[:, p:p + 1], half[:, :], ALU.pow).then_inc(s["f_rstd"], 1)

            def gate(n, p):
                if not unit(n):
                    return
                pool.wait_ge(s["yd"], 4 * (n + 1))
                pool.wait_ge(s["zact"], n + 1)
                past(pool, s["out"], n - 1)
                past(pool, s["y2"], n - 1)
                pool.tensor_tensor(yz[p][:, :, :], yd[:, :, :], zs[p][:, :, :], ALU.mult).then_inc(s["yz"], 1)

            def slot(n, p):
                out_power(n - 2, p)
                ln_power(n + 2, p)
                decays(n)
                ln_add(n + 2, p)
                gate(n - 1, 1 - p)

            for n in range(2):
                ln_power(n, n)
                ln_add(n, n)
            slots(pool, slot, GRP, 4, 2)

        @block.vector
        def _(dve):
            dve.wait_ge(s["w_in"], 16 * WIN)
            dve.wait_ge(s["consts"], 3)
            dve.tensor_copy(wh[:, :, :], w[:, :, 0:DIN]).then_inc(s["w_hi"], 1)
            dve.wait_ge(s["w_hi"], 1)
            dve.tensor_tensor(wl[:, :, :], w[:, :, 0:DIN], wh[:, :, :].bitcast(F32), ALU.subtract).then_inc(s["w_lo"], 1)
            for q in range(4):
                dve.tensor_scalar(wout[:, q, :], wout[:, q, :], normw(q), None, ALU.mult).then_inc(s["wout_set"], 1)
            dve.wait_ge(s["a_exp"], 1)
            dve.tensor_scalar(A[:, :], A[:, :], -1.0, None, ALU.mult).then_inc(s["a_set"], 1)

            def ln_stats(n, p):
                if not unit(n):
                    return
                dve.bn_stats(st[:, p, :], X[:, n, :]).then_inc(s["stats"], 1)
                wait_ahead(dve, s["stats"], n + 1, tick)
                dve.bn_aggr(mv[:, p, :], st[:, p, :]).then_inc(s["aggr"], 1)
                dve.wait_ge(s["aggr"], n + 1)
                dve.tensor_scalar(ve[:, p:p + 1], mv[:, p, 1:2], EPS, None, ALU.add).then_inc(s["var"], 1)

            def ln_apply(n, p):
                if not unit(n):
                    return
                dve.wait_ge(s["rstd"], n + 1)
                past(dve, s["turned"], n - 1)
                past(dve, s["added"], n - 1)
                dve.tensor_scalar(xn[p][:, :], X[:, n, :], mv[:, p, 0:1], rs[:, p:p + 1],
                                  ALU.subtract, ALU.mult).then_inc(s["xn"], 1)

            def low(n, p):
                if not unit(n):
                    return
                dve.wait_ge(s["xt_hi"], n + 1)
                dve.tensor_tensor(xl[p][:, :, :], psT[:, 0:256].rearrange("p (k t) -> p k t", k=2),
                                  xh[p][:, :, :].bitcast(F32), ALU.subtract).then_inc(s["xt_lo"], 1)

            def conv(n, tiles, padded):
                if not unit(n):
                    return
                dve.wait_ge(s[padded], n + 1)
                for k in range(2, -1, -1):
                    for m in tiles:
                        if k == 2:
                            dve.wait_ge(s["tap"], CONVT * n + m + 1)
                        else:
                            dve.wait_ge(s["taps"], 3 * CONVT * n + 3 * tiles[0] + (m - tiles[0]) + len(tiles) * (1 - k) + 1)
                        a = acc[:, m, :].rearrange("p (b t) -> p b t", t=L)
                        dve.scalar_tensor_tensor(a, pad[:, m, :, k:k + L], tap(m, k), a, ALU.mult, ALU.add).then_inc(s["taps"], 1)

            def softplus_a(n):
                if not unit(n):
                    return
                dve.wait_ge(s["dt_mm"], n + 1)
                past(dve, s["dt"], n)
                dve.tensor_tensor(sp[:, 0, :], DT, rows[:, 0, :], ALU.add).then_inc(s["sp_v"], 1)
                dve.wait_ge(s["sp_v"], n + 1)
                dve.tensor_scalar(sp[:, 1, :], sp[:, 0, :], -1.0, None, ALU.mult).then_inc(s["sp_n"], 1)
                dve.wait_ge(s["sp_n"], n + 1)
                dve.tensor_tensor(sp[:, 2, :], sp[:, 0, :], sp[:, 1, :], ALU.min).then_inc(s["sp_min"], 1)

            def softplus_b(n):
                if not unit(n):
                    return
                dve.wait_ge(s["sp_exp"], n + 1)
                dve.tensor_scalar(sp[:, 4, :], sp[:, 3, :], 1.0, None, ALU.add).then_inc(s["sp_u"], 1)

            def softplus_c(n):
                if not unit(n):
                    return
                dve.wait_ge(s["sp_u"], n + 1)
                dve.scalar_tensor_tensor(sp[:, 6, :], sp[:, 4, :], 1.0, sp[:, 3, :], ALU.subtract, ALU.subtract).then_inc(s["sp_c"], 1)
                dve.wait_ge(s["sp_ln"], n + 1)
                dve.wait_ge(s["sp_c"], n + 1)
                dve.tensor_tensor(sp[:, 7, :], sp[:, 5, :], sp[:, 6, :], ALU.subtract).then_inc(s["sp_s"], 1)
                dve.wait_ge(s["sp_s"], n + 1)
                dve.scalar_tensor_tensor(dt[:, n, :], sp[:, 0, :], 0.0, sp[:, 7, :], ALU.max, ALU.add).then_inc(s["dt"], 1)
                dve.wait_ge(s["dt"], n + 1)
                if isinstance(n, int) and n == 0:
                    dve.wait_ge(s["a_set"], 1)
                dve.tensor_tensor(da[:, n, :], dt[:, n, :], A[:, :], ALU.mult).then_inc(s["da"], 1)

            def scan(n, p):
                if not unit(n):
                    return
                dve.wait_ge(s["cb"], n + 1)
                dve.tensor_tensor(gm[:, :], psO[:, 384:512], tri[:, :], ALU.mult).then_inc(s["gm"], 1)
                dve.wait_ge(s["gm"], n + 1)
                dve.wait_ge(s["dec"], 2 * (n + 1))
                past(dve, s["y"], n)
                dve.tensor_tensor(mm[:, :, :], dec[:, :, :], gm[:, :].unsqueeze(1).to_broadcast([P, NH, P]),
                                  ALU.mult).then_inc(s["mm"], 1)
                dve.wait_ge(s["xturn"], n + 1)
                dve.tensor_tensor(xd[:, :].rearrange("p (h c) -> p h c", h=NH), psX[:, :].rearrange("p (h c) -> p h c", h=NH),
                                  dt[:, n, :].unsqueeze(2).to_broadcast([P, NH, DI // NH]), ALU.mult).then_inc(s["xd"], 1)

            def skips(n, p):
                if not unit(n):
                    return
                dve.wait_ge(s["y"], n + 1)
                past(dve, s["yz"], n)
                for q in range(ZT):
                    dve.scalar_tensor_tensor(yd[:, q, :], xa[p][:, q, :], skip(q), psY[:, q, :],
                                             ALU.mult, ALU.add).then_inc(s["yd"], 1)

            def out_var(n, p):
                if not unit(n):
                    return
                dve.wait_ge(s["out"], n + 1)
                dve.tensor_scalar(fe[:, p:p + 1], SS, 1.0 / DI, EPS, ALU.mult, ALU.add).then_inc(s["f_var"], 1)

            def finish(n, p):
                if not unit(n):
                    return
                dve.wait_ge(s["f_rstd"], n + 1)
                dve.wait_ge(s["added"], n + 1)
                dve.scalar_tensor_tensor(X[:, n, :], psO[:, 0:D], fr[:, p:p + 1], X[:, n, :],
                                         ALU.mult, ALU.add).then_inc(s["f_out"], 1)

            def slot(n, p):
                low(n + 1, 1 - p)
                out_var(n - 2, p)
                ln_stats(n + 2, p)
                finish(n - 2, p)
                scan(n - 1, 1 - p)
                conv(n, (0, 1, 2, 3), "padA")
                softplus_a(n + 1)
                conv(n, (4, 5), "padB")
                softplus_b(n + 1)
                skips(n - 1, 1 - p)
                softplus_c(n + 1)
                ln_apply(n + 2, p)

            for n in range(2):
                ln_stats(n, n)
                ln_apply(n, n)
            low(0, 0)
            softplus_a(0)
            softplus_b(0)
            softplus_c(0)
            slots(dve, slot, GRP, 4, 2)

        @block.scalar
        def _(act):
            act.wait_ge(s["w_in"], 16 * WIN)
            act.wait_ge(s["consts"], 3)
            act.activation(A[:, :], rows[:, 1, :], ACT.Exp).then_inc(s["a_exp"], 1)

            def high(n, p):
                if not unit(n):
                    return
                act.wait_ge(s["turned"], n + 1)
                past(act, s["projZ"], n - 1)
                act.activation(xh[p][:, :, :], psT[:, 0:256].rearrange("p (k t) -> p k t", k=2), ACT.Copy).then_inc(s["xt_hi"], 1)

            def decay(n):
                if not unit(n):
                    return
                act.wait_ge(s["logs"], n + 1)
                past(act, s["mm"], n)
                for i in range(2):
                    act.activation(dec[:, 4 * i:4 * i + 4, :], psL[:, i, :, :], ACT.Exp).then_inc(s["dec"], 1)

            def pads(n, tiles, ps, proj, padded):
                if not unit(n):
                    return
                act.wait_ge(s[proj], n + 1)
                past(act, s["xact"], n)
                past(act, s["taps"], 3 * CONVT * n)
                for m in tiles:
                    act.activation(acc[:, m, :], ps(m), ACT.Identity, bias=cbias(m), scale=tap(m, 3)).then_inc(s["tap"], 1)
                    i = act.activation(pad[:, m, :, 3:3 + L], ps(m).rearrange("p (b t) -> p b t", t=L), ACT.Copy)
                i.then_inc(s[padded], 1)

            def softplus_exp(n):
                if not unit(n):
                    return
                act.wait_ge(s["sp_min"], n + 1)
                act.activation(sp[:, 3, :], sp[:, 2, :], ACT.Exp).then_inc(s["sp_exp"], 1)

            def softplus_ln(n):
                if not unit(n):
                    return
                act.wait_ge(s["sp_u"], n + 1)
                act.activation(sp[:, 5, :], sp[:, 4, :], ACT.Ln).then_inc(s["sp_ln"], 1)

            def silus(n, p):
                if not unit(n):
                    return
                act.wait_ge(s["projZ"], n + 1)
                past(act, s["yz"], n - 1)
                act.activation(zs[p][:, :, :], psA[:, :, :], ACT.Silu).then_inc(s["zact"], 1)
                act.wait_ge(s["taps"], 3 * CONVT * (n + 1))
                past(act, s["yd"], 4 * (n - 1))
                past(act, s["xturn"], n - 1)
                past(act, s["cb"], n - 1)
                act.activation(xa[p][:, :, :], acc[:, :, :], ACT.Silu).then_inc(s["xact"], 1)

            def squares(n, p):
                if not unit(n):
                    return
                act.wait_ge(s["yz"], n + 1)
                past(act, s["out"], n - 1)
                act.activation(y2[p][:, :, :], yz[p][:, :, :], ACT.Square).then_inc(s["y2"], 1)

            def slot(n, p):
                high(n + 1, 1 - p)
                decay(n - 1)
                pads(n, (0, 1, 2, 3), lambda m: psA[:, m, :], "projA", "padA")
                pads(n, (4, 5), lambda m: psB[:, P * (m - 4):P * (m - 3)], "projB", "padB")
                softplus_exp(n + 1)
                softplus_ln(n + 1)
                silus(n, p)
                squares(n - 1, 1 - p)

            high(0, 0)
            softplus_exp(0)
            softplus_ln(0)
            slots(act, slot, GRP, 4, 2)

        @block.tensor
        def _(pe):
            pe.wait_ge(s["w_lo"], 1)
            pe.wait_ge(s["consts"], 3)

            def turn(n, p):
                if not unit(n):
                    return
                pe.wait_ge(s["xn"], n + 1)
                past(pe, s["xt_lo"], n)
                past(pe, s["sp_v"], n)
                for k in range(2):
                    i = pe.transpose(psT[:, k * P:(k + 1) * P], xn[p][:, k * P:(k + 1) * P], ident[:, :])
                i.then_inc(s["turned"], 1)

            def project(n, p, out, w0, tiles, done):
                for m in tiles:
                    for k in range(2):
                        c = w0 + m * P
                        i = mm3(pe, out(m), (wh[:, k, c:c + P], wl[:, k, c:c + P]), (xh[p][:, k, :], xl[p][:, k, :]),
                                k == 0, k == 1)
                i.then_inc(s[done], 1)

            def project_a(n, p):
                if not unit(n):
                    return
                pe.wait_ge(s["xt_lo"], n + 1)
                past(pe, s["zact"], n)
                project(n, p, lambda m: psA[:, m, :], DI, (0, 1, 2, 3), "projA")

            def project_b(n, p):
                if not unit(n):
                    return
                past(pe, s["padB"], n)
                project(n, p, lambda m: psB[:, P * (m - 4):P * (m - 3)], DI, (4, 5), "projB")

            def project_z(n, p):
                if not unit(n):
                    return
                pe.wait_ge(s["padA"], n + 1)
                project(n, p, lambda m: psA[:, m, :], 0, (0, 1, 2, 3), "projZ")

            def steps(n, p):
                if not unit(n):
                    return
                pe.wait_ge(s["xt_lo"], n + 1)
                parts = [(x[p], k) for k in range(2) for x in (xh, xl)]
                for i, (x, k) in enumerate(parts):
                    t = pe.matmul(DT, x[:, k, :].bitcast(F32), w[:, k, DIN:DIN + NH], start=(i == 0), stop=(i == 3))
                t.then_inc(s["dt_mm"], 1)

            def logs(n):
                if not unit(n):
                    return
                pe.wait_ge(s["ta"], n + 1)
                past(pe, s["dec"], 2 * n)
                for i in range(2):
                    t = pe.matmul(psL[:, i, :, :], aft[:, :], ta[:, 4 * i:4 * i + 4, :], start=True, stop=True)
                t.then_inc(s["logs"], 1)

            def cb_and_x(n, p):
                if not unit(n):
                    return
                pe.wait_ge(s["xact"], n + 1)
                past(pe, s["f_out"], n)
                pe.matmul(psO[:, 384:512], xa[p][:, 4, :], xa[p][:, 5, :], start=True, stop=True).then_inc(s["cb"], 1)
                past(pe, s["xd"], n)
                for q in range(4):
                    t = pe.transpose(psX[:, q * P:(q + 1) * P], xa[p][:, q, :], ident[:, :])
                t.then_inc(s["xturn"], 1)

            def scan(n):
                if not unit(n):
                    return
                pe.wait_ge(s["mm"], n + 1)
                pe.wait_ge(s["xd"], n + 1)
                past(pe, s["yd"], 4 * n)
                for h in range(NH):
                    t = pe.matmul(psY[64 * (h % 2):64 * (h % 2) + 64, h // 2, :], xd[:, 64 * h:64 * h + 64], mm[:, h, :],
                                  start=True, stop=True)
                t.then_inc(s["y"], 1)

            def out(n, p):
                if not unit(n):
                    return
                pe.wait_ge(s["y2"], n + 1)
                pe.wait_ge(s["gm"], n + 1)
                for q in range(ZT):
                    pe.matmul(SS, y2[p][:, q, :], ones[:, :], start=(q == 0), stop=(q == 3))
                for q in range(ZT):
                    t = pe.matmul(psO[:, 0:D], yz[p][:, q, :], wout[:, q, :], start=(q == 0), stop=(q == 3))
                t.then_inc(s["out"], 1)

            def slot(n, p):
                turn(n + 1, 1 - p)
                out(n - 2, p)
                logs(n - 1)
                project_a(n, p)
                cb_and_x(n - 1, 1 - p)
                project_b(n, p)
                steps(n + 1, 1 - p)
                project_z(n, p)
                scan(n - 1)

            turn(0, 0)
            steps(0, 0)
            pe.wait_ge(s["wout_set"], 4)
            slots(pe, slot, GRP, 4, 2)

NHF, DF = 16, 16
E, FH = 8, 1024


def attention_phase(nc, sem, io, X, keep):
    tokens, logits = keep["tokens"], keep["logits"]
    with ExitStack() as ctx:
        def sb(name, shape, dt=F32):
            return ctx.enter_context(nc.sbuf_tensor("s_" + name, shape, dt))

        def pb(name, shape):
            return ctx.enter_context(nc.psum_tensor("s_" + name, shape, F32))

        wq, wk, wv, wp = (sb(n, [P, 2, D]) for n in ("wq", "wk", "wv", "wp"))
        gw = sb("gw", [P, 2, E])
        cols = sb("cols", [P, 8, 2])
        rows = sb("rows", [P, D])
        gbias = sb("gbias", [P, E])
        ident = sb("ident", [P, P])
        heads = sb("heads", [P, 8])
        causal = sb("causal", [P, L])
        tick = sb("tick", [P, 1])
        half = sb("half", [P, 1])
        h0 = sb("h0", [P, GRP, D])
        xn = [sb(f"xn{i}", [P, D]) for i in range(2)]
        hT = [sb(f"hT{i}", [P, 2, P]) for i in range(2)]
        stat = [sb(f"st{i}", [P, 2, 6]) for i in range(3)]
        mv = [sb(f"mv{i}", [P, 2, 2]) for i in range(3)]
        ve = [sb(f"ve{i}", [P, 2]) for i in range(3)]
        rs = [sb(f"rs{i}", [P, 2]) for i in range(3)]
        qT = [sb(f"qT{i}", [P, 2, P]) for i in range(2)]
        kT = [sb(f"kT{i}", [P, 2, P]) for i in range(2)]
        qx = sb("qx", [P, 2, BPG, 8, L])
        vx = [sb(f"vx{i}", [P, BPG, 4, 4, DF]) for i in range(2)]
        sc = sb("sc", [P, 16, L])
        mx = sb("mx", [P, 16])
        su = sb("su", [P, 16])
        ri = sb("ri", [P, 16])
        pr = sb("pr", [P, 16, L])
        pT = [sb(f"pT{i}", [P, 16, L]) for i in range(2)]
        yT = [sb(f"yT{i}", [P, 2, P]) for i in range(2)]
        h1 = [sb(f"h1{i}", [P, D]) for i in range(2)]
        n2 = [sb(f"n2{i}", [P, D]) for i in range(2)]
        mf = [sb(f"mf{i}", [P, 2, P]) for i in range(2)]

        psT = pb("psT", [P, 4, P])
        psQ = pb("psQ", [P, 4, P])
        psV = pb("psV", [P, 512])
        psS = pb("psS", [P, 16, L])
        psY = pb("psY", [P, 4, P])
        psO = pb("psO", [P, 512])
        psU = pb("psU", [P, 4, P])
        psG = pb("psG", [P, 512])
        s = {n: sem("s_" + n) for n in (
            "w_in", "consts", "stats0", "aggr0", "var0", "rstd0", "norm0", "stats1", "aggr1", "var1", "rstd1", "norm1",
            "stats2", "aggr2", "var2", "rstd2", "norm2", "biased", "turned", "hT", "qk", "v", "q_out", "k_out",
            "qx", "vx_a", "vx_d", "scored", "masked", "peak", "shifted", "exped", "summed", "recip", "probs", "pT",
            "attended", "yT", "outed", "h1", "added", "turned2", "mf", "gate", "logits", "kept")}
        block = ctx.enter_context(nc.Block())
        WIN = 11
        col = lambda i, k: cols[:, i, k:k + 1]

        @block.sync
        def _(sy):
            for d, src in ((wq, "s_wq"), (wk, "s_wk"), (wv, "s_wv"), (wp, "s_wp"), (gw, "s_gw"), (cols, "s_cols"), (rows, "s_bp"),
                           (gbias, "s_gb"), (ident, "ident"), (heads, "heads"), (causal, "causal")):
                sy.dma_start(d[tuple(slice(None) for _ in d.shape)], io[src]).then_inc(s["w_in"], 16)
            sy.wait_ge(s["w_in"], 16 * WIN)

        @block.gpsimd
        def _(pool):
            pool.memset(half[:, :], -0.5).then_inc(s["consts"], 1)
            for i in range(2):
                pool.memset(vx[i][:, :, :, :, :], 0.0).then_inc(s["consts"], 1)
            pool.wait_ge(s["consts"], 3)
            pool.wait_ge(s["w_in"], 16 * WIN)

            def power(which, n, p):
                if not unit(n):
                    return
                pool.wait_ge(s[f"var{which}"], n + 1)
                pool.tensor_tensor(rs[which][:, p:p + 1], ve[which][:, p:p + 1], half[:, :], ALU.pow).then_inc(s[f"rstd{which}"], 1)

            def bias(n):
                if not unit(n):
                    return
                pool.wait_ge(s["norm1"], n + 1)
                pool.tensor_tensor(h0[:, n, :], h0[:, n, :], rows[:, :], ALU.add).then_inc(s["biased"], 1)

            def by_head(n, p):
                if not unit(n):
                    return
                pool.wait_ge(s["q_out"], n + 1)
                past(pool, s["scored"], n)
                for k in range(2):
                    q = qT[p][:, k, :].rearrange("p (b t) -> p b t", t=L).unsqueeze(2).to_broadcast([P, BPG, 8, L])
                    own = heads[:, :].unsqueeze(1).unsqueeze(3).to_broadcast([P, BPG, 8, L])
                    pool.tensor_tensor(qx[:, k, :, :, :], q, own, ALU.mult).then_inc(s["qx"], 1)

            def add(n, p):
                if not unit(n):
                    return
                pool.wait_ge(s["h1"], n + 1)
                pool.tensor_tensor(X[:, n, :], X[:, n, :], h1[p][:, :], ALU.add).then_inc(s["added"], 1)

            def slot(n, p):
                power(2, n - 3, 1 - p)
                power(0, n + 2, p)
                power(1, n + 2, p)
                by_head(n, p)
                add(n - 3, 1 - p)
                bias(n + 2)

            for n in range(2):
                power(0, n, n)
                power(1, n, n)
                bias(n)
            slots(pool, slot, GRP, 6, 4)

        @block.vector
        def _(dve):
            dve.wait_ge(s["w_in"], 16 * WIN)
            dve.wait_ge(s["consts"], 3)

            def norm_stats(which, n, p, src):
                dve.bn_stats(stat[which][:, p, :], src).then_inc(s[f"stats{which}"], 1)
                wait_ahead(dve, s[f"stats{which}"], n + 1, tick)
                dve.bn_aggr(mv[which][:, p, :], stat[which][:, p, :]).then_inc(s[f"aggr{which}"], 1)
                dve.wait_ge(s[f"aggr{which}"], n + 1)
                dve.tensor_scalar(ve[which][:, p:p + 1], mv[which][:, p, 1:2], EPS, None, ALU.add).then_inc(s[f"var{which}"], 1)

            def norm_apply(which, n, p, src, dst):
                dve.wait_ge(s[f"rstd{which}"], n + 1)
                dve.tensor_scalar(dst, src, mv[which][:, p, 0:1], rs[which][:, p:p + 1],
                                  ALU.subtract, ALU.mult).then_inc(s[f"norm{which}"], 1)

            def norms_a(n, p):
                if unit(n):
                    norm_stats(0, n, p, X[:, n, :])

            def norms_b(n, p):
                if unit(n):
                    norm_apply(0, n, p, X[:, n, :], h0[:, n, :])
                    wait_ahead(dve, s["norm0"], n + 1, tick)
                    norm_stats(1, n, p, h0[:, n, :])

            def norms_c(n, p):
                if unit(n):
                    past(dve, s["turned"], n - 1)
                    norm_apply(1, n, p, h0[:, n, :], xn[p][:, :])

            def v_blocks(n, p):
                if not unit(n):
                    return
                dve.wait_ge(s["v"], n + 1)
                dve.wait_ge(s["vx_a"], n + 1)
                past(dve, s["attended"], n - 1)
                for b in range(2, 4):
                    for h in range(4):
                        i = dve.tensor_copy(vx[p][32 * h:32 * h + 32, b, :, h, :],
                                            psV[32 * b:32 * b + 32, 0:D].rearrange("p (g h d) -> p g h d", g=4, h=4)[:, :, h, :])
                i.then_inc(s["vx_d"], 1)

            def shift(n):
                if not unit(n):
                    return
                dve.wait_ge(s["scored"], n + 1)
                past(dve, s["exped"], n)
                dve.tensor_tensor(sc[:, :, :], psS[:, :, :], causal[:, :].unsqueeze(1).to_broadcast([P, 16, L]),
                                  ALU.add).then_inc(s["masked"], 1)
                dve.wait_ge(s["masked"], n + 1)
                dve.reduce_max(mx[:, :], sc[:, :, :], AXX).then_inc(s["peak"], 1)
                dve.wait_ge(s["peak"], n + 1)
                dve.tensor_tensor(sc[:, :, :], sc[:, :, :], mx[:, :].unsqueeze(2).to_broadcast([P, 16, L]),
                                  ALU.subtract).then_inc(s["shifted"], 1)

            def shares(n, p):
                if not unit(n):
                    return
                dve.wait_ge(s["exped"], n + 1)
                dve.reduce_sum(su[:, :], pr[:, :, :], AXX).then_inc(s["summed"], 1)
                dve.wait_ge(s["summed"], n + 1)
                dve.reciprocal(ri[:, :], su[:, :]).then_inc(s["recip"], 1)
                dve.wait_ge(s["recip"], n + 1)
                dve.tensor_tensor(pr[:, :, :], pr[:, :, :], ri[:, :].unsqueeze(2).to_broadcast([P, 16, L]),
                                  ALU.mult).then_inc(s["probs"], 1)
                dve.wait_ge(s["probs"], n + 1)
                past(dve, s["attended"], n - 1)
                dve.transpose(pT[p][:, :, :].rearrange("p a b -> p (a b)"),
                              pr[:, :, :].rearrange("p a b -> p (a b)")).then_inc(s["pT"], 1)

            def residual(n, p):
                if not unit(n):
                    return
                dve.wait_ge(s["outed"], n + 1)
                dve.wait_ge(s["biased"], n + 1)
                past(dve, s["added"], n - 1)
                dve.tensor_tensor(h1[p][:, :], psO[:, 0:D], h0[:, n, :], ALU.add).then_inc(s["h1"], 1)
                dve.wait_ge(s["h1"], n + 1)
                norm_stats(2, n, p, h1[p][:, :])

            def second_norm(n, p):
                if not unit(n):
                    return
                past(dve, s["turned2"], n - 1)
                norm_apply(2, n, p, h1[p][:, :], n2[p][:, :])
                dve.tensor_scalar(tokens[:, n, :], h1[p][:, :], mv[2][:, p, 0:1], rs[2][:, p:p + 1],
                                  ALU.subtract, ALU.mult).then_inc(s["kept"], 1)

            def route(n, p):
                if not unit(n):
                    return
                dve.wait_ge(s["gate"], n + 1)
                dve.tensor_tensor(logits[:, n, :], psG[:, 0:E], gbias[:, :], ALU.add).then_inc(s["logits"], 1)

            def slot(n, p):
                norms_a(n + 2, p)
                residual(n - 3, 1 - p)
                norms_b(n + 2, p)
                shift(n - 1)
                second_norm(n - 3, 1 - p)
                norms_c(n + 2, p)
                v_blocks(n, p)
                route(n - 4, p)
                shares(n - 1, 1 - p)

            for n in range(2):
                norms_a(n, n)
                norms_b(n, n)
                norms_c(n, n)
            slots(dve, slot, GRP, 6, 4)

        @block.scalar
        def _(act):
            act.wait_ge(s["w_in"], 16 * WIN)
            act.wait_ge(s["consts"], 3)

            def affine(n, p):
                if not unit(n):
                    return
                act.wait_ge(s["turned"], n + 1)
                past(act, s["v"], n - 1)
                for k in range(2):
                    act.activation(hT[p][:, k, :], psT[:, k, :], ACT.Identity, bias=col(1, k), scale=col(0, k)).then_inc(s["hT"], 1)

            def biases(n, p):
                if not unit(n):
                    return
                act.wait_ge(s["qk"], n + 1)
                past(act, s["qx"], 2 * (n - 1))
                for k in range(2):
                    i = act.activation(qT[p][:, k, :], psQ[:, k, :], ACT.Identity, bias=col(2, k))
                i.then_inc(s["q_out"], 1)
                past(act, s["scored"], n - 1)
                for k in range(2):
                    i = act.activation(kT[p][:, k, :], psQ[:, 2 + k, :], ACT.Identity, bias=col(3, k))
                i.then_inc(s["k_out"], 1)

            def v_blocks(n, p):
                if not unit(n):
                    return
                act.wait_ge(s["v"], n + 1)
                past(act, s["attended"], n - 1)
                for b in range(2):
                    for h in range(4):
                        i = act.activation(vx[p][32 * h:32 * h + 32, b, :, h, :],
                                           psV[32 * b:32 * b + 32, 0:D].rearrange("p (g h d) -> p g h d", g=4, h=4)[:, :, h, :],
                                           ACT.Copy)
                i.then_inc(s["vx_a"], 1)

            def exps(n):
                if not unit(n):
                    return
                act.wait_ge(s["shifted"], n + 1)
                past(act, s["pT"], n)
                act.activation(pr[:, :, :], sc[:, :, :], ACT.Exp).then_inc(s["exped"], 1)

            def attended(n, p):
                if not unit(n):
                    return
                act.wait_ge(s["attended"], n + 1)
                past(act, s["outed"], n - 1)
                for k in range(2):
                    i = act.activation(yT[p][:, k, :], psY[:, k, :], ACT.Identity, bias=col(4, k))
                i.then_inc(s["yT"], 1)

            def affine2(n, p):
                if not unit(n):
                    return
                act.wait_ge(s["turned2"], n + 1)
                past(act, s["gate"], n - 1)
                for k in range(2):
                    act.activation(mf[p][:, k, :], psU[:, k, :], ACT.Identity, bias=col(6, k), scale=col(5, k)).then_inc(s["mf"], 1)

            def slot(n, p):
                affine(n + 1, 1 - p)
                affine2(n - 4, p)
                biases(n, p)
                v_blocks(n, p)
                exps(n - 1)
                attended(n - 2, p)

            affine(0, 0)
            slots(act, slot, GRP, 6, 4)

        @block.tensor
        def _(pe):
            pe.wait_ge(s["w_in"], 16 * WIN)

            def turn(n, p):
                if not unit(n):
                    return
                pe.wait_ge(s["norm1"], n + 1)
                past(pe, s["hT"], 2 * n)
                for k in range(2):
                    i = pe.transpose(psT[:, k, :], xn[p][:, k * P:(k + 1) * P], ident[:, :])
                i.then_inc(s["turned"], 1)

            def project(n, p):
                if not unit(n):
                    return
                pe.wait_ge(s["hT"], 2 * (n + 1))
                past(pe, s["k_out"], n)
                for i, w in enumerate((wq, wk)):
                    for m in range(2):
                        for k in range(2):
                            t = pe.matmul(psQ[:, 2 * i + m, :], w[:, k, m * P:(m + 1) * P], hT[p][:, k, :],
                                          start=(k == 0), stop=(k == 1))
                t.then_inc(s["qk"], 1)
                past(pe, s["vx_d"], n)
                for k in range(2):
                    t = pe.matmul(psV[:, 0:D], hT[p][:, k, :], wv[:, k, :], start=(k == 0), stop=(k == 1))
                t.then_inc(s["v"], 1)

            def score(n, p):
                if not unit(n):
                    return
                pe.wait_ge(s["qx"], 2 * (n + 1))
                pe.wait_ge(s["k_out"], n + 1)
                past(pe, s["masked"], n)
                for g in range(4):
                    for b in range(BPG):
                        t = pe.matmul(psS[:, BPG * g + b, :], qx[:, g // 2, b, 4 * (g % 2):4 * (g % 2) + 4, :],
                                      kT[p][:, g // 2, L * b:L * b + L], start=True, stop=True)
                t.then_inc(s["scored"], 1)

            def attend(n, p):
                if not unit(n):
                    return
                pe.wait_ge(s["pT"], n + 1)
                pe.wait_ge(s["vx_d"], n + 1)
                past(pe, s["yT"], n)
                for g in range(4):
                    for b in range(BPG):
                        t = pe.matmul(psY[64 * (g % 2):64 * (g % 2) + 64, g // 2, L * b:L * b + L],
                                      vx[p][:, b, g, :, :], pT[p][:, BPG * g + b, :], start=True, stop=True)
                t.then_inc(s["attended"], 1)

            def output(n, p):
                if not unit(n):
                    return
                pe.wait_ge(s["yT"], n + 1)
                past(pe, s["h1"], n)
                for k in range(2):
                    t = pe.matmul(psO[:, 0:D], yT[p][:, k, :], wp[:, k, :], start=(k == 0), stop=(k == 1))
                t.then_inc(s["outed"], 1)

            def turn2(n, p):
                if not unit(n):
                    return
                pe.wait_ge(s["norm2"], n + 1)
                past(pe, s["mf"], 2 * n)
                for k in range(2):
                    t = pe.transpose(psU[:, k, :], n2[p][:, k * P:(k + 1) * P], ident[:, :])
                t.then_inc(s["turned2"], 1)

            def route(n, p):
                if not unit(n):
                    return
                pe.wait_ge(s["mf"], 2 * (n + 1))
                past(pe, s["logits"], n)
                for k in range(2):
                    t = pe.matmul(psG[:, 0:E], mf[p][:, k, :], gw[:, k, :], start=(k == 0), stop=(k == 1))
                t.then_inc(s["gate"], 1)

            def slot(n, p):
                turn(n + 1, 1 - p)
                turn2(n - 4, p)
                output(n - 3, 1 - p)
                project(n, p)
                route(n - 4, p)
                score(n - 1, 1 - p)
                attend(n - 2, p)

            turn(0, 0)
            slots(pe, slot, GRP, 6, 4)


UT = 256
UNITS = 2 * B * L // UT + E
SLOTS = (UNITS + 1) * UT


def routing_phase(nc, sem, io, keep):
    logits, g1, g2, pos, cum, tokens = (keep[n] for n in ("logits", "g1", "g2", "pos", "cum", "tokens"))
    rows = keep["rows"]
    STEPS_TO_EXP = 11
    with ExitStack() as ctx:
        def sb(name, shape):
            return ctx.enter_context(nc.sbuf_tensor("r_" + name, shape, F32))

        idx = sb("idx", [P, E])
        steps = sb("steps", [P, B * L // UT - 1])
        before = sb("before", [P, P])
        ones = sb("ones", [P, P])
        work, one, two, lg2, sel, slot, prod = (sb(n, [P, GRP, E]) for n in
                                                ("work", "one", "two", "lg2", "sel", "slot", "prod"))
        tot = sb("tot", [P, GRP, E])
        run = sb("run", [P, GRP + 1, E])
        more = sb("more", [P, E, B * L // UT - 1])
        units = sb("units", [P, E])
        cumf = sb("cumf", [P, E + 2])
        posf = sb("posf", [P, 2, GRP])
        top, at1, second, at2, gap, eg, den = (sb(n, [P, GRP]) for n in
                                               ("top", "at1", "second", "at2", "gap", "eg", "den"))
        ps = ctx.enter_context(nc.psum_tensor("r_ps", [P, 512], F32))
        pt = ctx.enter_context(nc.psum_tensor("r_pt", [P, 512], F32))
        got, step, exped, chosen, ranked, ones_set, placed, copied = (
            sem("r_" + n) for n in ("got", "step", "exped", "chosen", "ranked", "ones_set", "placed", "copied"))
        block = ctx.enter_context(nc.Block())
        wide = lambda a: a[:, :].unsqueeze(2).to_broadcast([P, GRP, E])
        flat = lambda a: a[:, :, :].rearrange("p a b -> p (a b)")

        @block.sync
        def _(sy):
            for d, src in ((idx, "experts"), (steps, "steps"), (before, "before")):
                sy.dma_start(d[:, :], io[src]).then_inc(got, 16)
            sy.wait_ge(got, 48)

        @block.scalar
        def _(act):
            act.wait_ge(step, STEPS_TO_EXP)
            act.activation(eg[:, :], gap[:, :], ACT.Exp).then_inc(exped, 1)

        @block.tensor
        def _(pe):
            pe.wait_ge(got, 48)
            pe.wait_ge(ones_set, 1)
            pe.wait_ge(chosen, 1)
            pe.matmul(ps[:, 0:P], before[:, :], flat(sel), start=True, stop=True).then_inc(ranked, 1)
            pe.matmul(pt[:, 0:P], ones[:, :], flat(sel), start=True, stop=True).then_inc(ranked, 1)

        @block.gpsimd
        def _(pool):
            pool.memset(ones[:, :], 1.0).then_inc(ones_set, 1)
            pool.wait_ge(placed, 1)
            for k in range(2):
                for g in range(GRP):
                    pool.indirect_dma_start(rows, bass.IndirectOffsetOnAxis(pos[:, k, g:g + 1], 0),
                                            tokens[:, g, :], None).then_inc(copied, 16)
            pool.wait_ge(copied, 16 * 2 * GRP)

        @block.vector
        def _(dve):
            dve.wait_ge(got, 48)
            count = [0]

            def link(i):
                count[0] += 1
                i.then_inc(step, 1)
                dve.wait_ge(step, count[0])

            ix = idx[:, :].unsqueeze(1).to_broadcast([P, GRP, E])

            def largest(src, value, at):
                link(dve.reduce_max(value[:, :], src[:, :, :], AXX))
                link(dve.tensor_tensor(work[:, :, :], src[:, :, :], wide(value), ALU.is_equal))
                link(dve.tensor_tensor(work[:, :, :], work[:, :, :], ix, ALU.mult))
                link(dve.reduce_max(at[:, :], work[:, :, :], AXX))

            largest(logits, top, at1)
            link(dve.tensor_tensor(one[:, :, :], work[:, :, :], wide(at1), ALU.is_equal))
            link(dve.scalar_tensor_tensor(flat(lg2), flat(one), -3.0e38, flat(logits), ALU.mult, ALU.add))
            largest(lg2, second, at2)
            link(dve.tensor_tensor(gap[:, :], second[:, :], top[:, :], ALU.subtract))
            assert count[0] == STEPS_TO_EXP
            link(dve.tensor_tensor(two[:, :, :], work[:, :, :], wide(at2), ALU.is_equal))
            dve.tensor_tensor(sel[:, :, :], one[:, :, :], two[:, :, :], ALU.add).then_inc(chosen, 1)
            dve.wait_ge(exped, 1)
            link(dve.tensor_scalar(den[:, :], eg[:, :], 1.0, None, ALU.add))
            link(dve.reciprocal(g1[:, :], den[:, :]))
            link(dve.tensor_tensor(g2[:, :], eg[:, :], g1[:, :], ALU.mult))
            dve.wait_ge(ranked, 2)
            link(dve.tensor_copy(tot[:, :, :], pt[:, 0:P].rearrange("p (g e) -> p g e", e=E)))
            link(dve.memset(run[:, 0, :], 0.0))
            for g in range(GRP):
                link(dve.tensor_tensor(run[:, g + 1, :], run[:, g, :], tot[:, g, :], ALU.add))
            nk = B * L // UT - 1
            link(dve.tensor_tensor(more[:, :, :], run[:, GRP, :].unsqueeze(2).to_broadcast([P, E, nk]),
                                   steps[:, :].unsqueeze(1).to_broadcast([P, E, nk]), ALU.is_gt))
            link(dve.reduce_sum(units[:, :], more[:, :, :], AXX))
            link(dve.tensor_scalar(units[:, :], units[:, :], 1.0, None, ALU.add))
            link(dve.memset(cumf[:, 0:2], 0.0))
            for e in range(E):
                link(dve.tensor_tensor(cumf[:, e + 2:e + 3], cumf[:, e + 1:e + 2], units[:, e:e + 1], ALU.add))
            link(dve.tensor_copy(cum[:, :], cumf[:, :]))
            link(dve.tensor_tensor(slot[:, :, :], run[:, 0:GRP, :], ps[:, 0:P].rearrange("p (g e) -> p g e", e=E), ALU.add))
            link(dve.scalar_tensor_tensor(slot[:, :, :], cumf[:, 1:E + 1].unsqueeze(1).to_broadcast([P, GRP, E]), float(UT),
                                          slot[:, :, :], ALU.mult, ALU.add))
            for k, choice in enumerate((one, two)):
                link(dve.tensor_tensor(prod[:, :, :], choice[:, :, :], slot[:, :, :], ALU.mult))
                link(dve.reduce_sum(posf[:, k, :], prod[:, :, :], AXX))
            dve.tensor_copy(pos[:, :, :], posf[:, :, :]).then_inc(placed, 1)


def experts_phase(nc, sem, io, keep):
    cum, rows, yrows = keep["cum"], keep["rows"], keep["yrows"]
    FT = FH // P
    with ExitStack() as ctx:
        def sb(name, shape, dt=F32):
            return ctx.enter_context(nc.sbuf_tensor("e_" + name, shape, dt))

        def pb(name):
            return ctx.enter_context(nc.psum_tensor("e_" + name, [P, 512], F32))

        w1 = [sb(f"w1{i}", [P, 2, FH]) for i in range(2)]
        w2 = [sb(f"w2{i}", [P, FT, D]) for i in range(2)]
        w1h = [sb(f"w1h{i}", [P, 2, FH], F32R) for i in range(2)]
        w1l = [sb(f"w1l{i}", [P, 2, FH], F32R) for i in range(2)]
        w2h = [sb(f"w2h{i}", [P, FT, D], F32R) for i in range(2)]
        w2l = [sb(f"w2l{i}", [P, FT, D], F32R) for i in range(2)]
        bs = sb("bs", [P, E, FT + 2])
        be = [sb(f"be{i}", [P, FT + 2]) for i in range(2)]
        ln2 = sb("ln2", [P, 2, 2])
        ident = sb("ident", [P, P])
        tick = sb("tick", [P, 6])
        xs = sb("xs", [P, 2, D])
        xf = sb("xf", [P, 2, UT])
        xh, xl = sb("xh", [P, 2, UT], F32R), sb("xl", [P, 2, UT], F32R)
        mid = [sb(f"mid{i}", [P, UT]) for i in range(2)]
        dh, dl = sb("dh", [P, FT, UT], F32R), sb("dl", [P, FT, UT], F32R)
        yT = sb("yT", [P, 2, UT])
        yr = sb("yr", [P, 2, D])
        ps1 = [pb(f"ps1{i}") for i in range(4)]
        ps2, psX, psR = pb("ps2"), pb("psX"), pb("psR")
        s = {n: sem("e_" + n) for n in ("c_in", "be", "w1h", "w2h", "w1l", "w2l", "x_in", "turned", "xf", "xh", "xl",
                                        "up", "gelu", "hi", "lo", "unit_hid", "down", "yT", "yturned", "yrow", "stored",
                                        "last_stored", "zero")}
        w_in = [sem(f"e_w_in{i}") for i in range(2)]
        block = ctx.enter_context(nc.Block())

        def entry(eng, k):
            return eng.value_load(cum[0:1, bass.ds(k, 1)], min_val=0, max_val=UNITS)

        def experts(eng, expert):
            with eng.Fori(0, E // 2 - 1) as i:
                for p in range(2):
                    expert(2 * i + p, p, entry(eng, 2 * i + p + 1), entry(eng, 2 * i + p + 2))
            for e in (E - 2, E - 1):
                expert(e, e % 2, entry(eng, e + 1), entry(eng, e + 2))

        @block.sync
        def _(sy):
            sy.dma_start(bs[:, :, :], io["e_b"]).then_inc(s["c_in"], 16)
            sy.dma_start(ln2[:, :, :], io["s_cols"][:, 5:7, :]).then_inc(s["c_in"], 16)
            sy.dma_start(ident[:, :], io["ident"]).then_inc(s["c_in"], 16)

            def unit_rows(dram, u):
                return dram[bass.ds(u * UT, UT), :].rearrange("(j p) d -> p j d", p=P)

            sy.dma_start(xs[:, :, :], unit_rows(rows, 0)).then_inc(s["x_in"], 16)
            sy.wait_ge(s["zero"], 1)
            sy.dma_start(unit_rows(yrows, 0), yr[:, :, :]).then_inc(s["stored"], 16)
            last = entry(sy, E + 1)
            with sy.Fori(0, last) as u:
                sy.wait_ge(s["turned"], u + 1)
                sy.dma_start(xs[:, :, :], unit_rows(rows, u + 1)).then_inc(s["x_in"], 16)
                sy.wait_ge(s["yrow"], u + 2)
                sy.dma_start(unit_rows(yrows, u), yr[:, :, :]).then_inc(s["stored"], 16)
            sy.wait_ge(s["yrow"], last + 2)
            sy.dma_start(unit_rows(yrows, last), yr[:, :, :]).then_inc(s["last_stored"], 16)
            sy.wait_ge(s["last_stored"], 16)

        @block.gpsimd
        def _(pool):
            def low_parts(e, p):
                pool.wait_ge(s["w1h"], e + 1)
                pool.tensor_tensor(w1l[p][:, :, :], w1[p][:, :, :], w1h[p][:, :, :].bitcast(F32), ALU.subtract).then_inc(s["w1l"], 1)
                pool.wait_ge(s["w2h"], e + 1)
                pool.tensor_tensor(w2l[p][:, :, :], w2[p][:, :, :], w2h[p][:, :, :].bitcast(F32), ALU.subtract).then_inc(s["w2l"], 1)

            with pool.Fori(0, E // 2) as i:
                low_parts(2 * i, 0)
                low_parts(2 * i + 1, 1)

        @block.scalar
        def _(act):
            def load(e, p):
                act.dma_start(w1[p][:, :, :], io["e_w1"][e]).then_inc(w_in[p], 16)
                act.dma_start(w2[p][:, :, :], io["e_w2"][e]).then_inc(w_in[p], 16)

            def high_parts(e, p, before):
                act.wait_ge(w_in[p], 32 * ((e - p) // 2 + 1) if isinstance(e, int) else 16 * (e - p) + 32)
                act.wait_ge(s["down"], before + 1)
                act.activation(w1h[p][:, :, :], w1[p][:, :, :], ACT.Copy).then_inc(s["w1h"], 1)
                act.activation(w2h[p][:, :, :], w2[p][:, :, :], ACT.Copy).then_inc(s["w2h"], 1)

            def expert(e, p, first, end):
                last = isinstance(e, int) and e == E - 1
                act.activation(be[p][:, :], bs[:, e, :], ACT.Copy).then_inc(s["be"], 1)
                if not last:
                    high_parts(e + 1, 1 - p, first)
                if not (isinstance(e, int) and e >= E - 2):
                    act.wait_ge(s["w2l"], e + 1)
                    load(e + 2, p)
                act.wait_ge(s["be"], e + 1)
                with act.Fori(first, end) as u:
                    for f in range(FT):
                        act.wait_ge(s["up"], 8 * u + f + 1)
                        if f < 2:
                            act.wait_ge(s["unit_hid"], u + 1)
                        else:
                            act.wait_ge(s["lo"], 8 * u + f - 1)
                        act.activation(mid[f % 2][:, :], ps1[f % 4][:, 0:UT], ACT.Gelu, bias=be[p][:, f:f + 1]).then_inc(s["gelu"], 1)
                    turn_out(u + 1)
                    act.wait_ge(s["down"], u + 2)
                    act.wait_ge(s["yturned"], u + 1)
                    for k in range(2):
                        act.activation(yT[:, k, :], ps2[:, UT * k:UT * k + UT], ACT.Identity,
                                       bias=be[p][:, FT + k:FT + k + 1]).then_inc(s["yT"], 1)

            def turn_out(u):
                act.wait_ge(s["turned"], u + 1)
                for k in range(2):
                    act.activation(xf[:, k, :], psX[:, UT * k:UT * k + UT], ACT.Identity,
                                   bias=ln2[:, 1, k:k + 1], scale=ln2[:, 0, k:k + 1]).then_inc(s["xf"], 1)
                act.wait_ge(s["xf"], 2 * (u + 1))
                act.activation(xh[:, :, :], xf[:, :, :], ACT.Copy).then_inc(s["xh"], 1)

            load(0, 0)
            load(1, 1)
            act.wait_ge(s["c_in"], 48)
            act.wait_ge(s["zero"], 4)
            turn_out(0)
            high_parts(0, 0, 0)
            experts(act, expert)

        @block.vector
        def _(dve):
            dve.memset(yr[:, :, :], 0.0).then_inc(s["zero"], 1)
            dve.memset(yT[:, :, :], 0.0).then_inc(s["zero"], 1)
            for i, n in enumerate(("unit_hid", "down", "yrow", "zero", "zero")):
                dve.memset(tick[:, i:i + 1], 0.0).then_inc(s[n], 1)

            def x_low(u):
                dve.wait_ge(s["xh"], u + 1)
                dve.tensor_tensor(xl[:, :, :], xf[:, :, :], xh[:, :, :].bitcast(F32), ALU.subtract).then_inc(s["xl"], 1)

            def row_out(u):
                dve.wait_ge(s["yturned"], u + 1)
                dve.wait_ge(s["stored"], 16 * (u + 1))
                dve.tensor_copy(yr[:, :, :], psR[:, :].rearrange("p (j d) -> p j d", j=2)).then_inc(s["yrow"], 1)

            def expert(e, p, first, end):
                with dve.Fori(first, end) as u:
                    for f in range(FT):
                        dve.wait_ge(s["gelu"], 8 * u + f + 1)
                        dve.tensor_copy(dh[:, f, :], mid[f % 2][:, :]).then_inc(s["hi"], 1)
                        dve.wait_ge(s["hi"], 8 * u + f + 1)
                        dve.tensor_tensor(dl[:, f, :], mid[f % 2][:, :], dh[:, f, :].bitcast(F32), ALU.subtract).then_inc(s["lo"], 1)
                    dve.wait_ge(s["lo"], 8 * u + 8)
                    dve.memset(tick[:, 5:6], 0.0).then_inc(s["unit_hid"], 1)
                    row_out(u)
                    x_low(u + 1)

            x_low(0)
            experts(dve, expert)
            row_out(entry(dve, E + 1))

        @block.tensor
        def _(pe):
            pe.wait_ge(s["c_in"], 48)
            pe.wait_ge(s["zero"], 4)

            def turn(u):
                pe.wait_ge(s["x_in"], 16 * (u + 1))
                for k in range(2):
                    for j in range(2):
                        t = pe.transpose(psX[:, UT * k + P * j:UT * k + P * j + P], xs[:, j, k * P:(k + 1) * P], ident[:, :])
                t.then_inc(s["turned"], 1)

            def turn_back(u):
                pe.wait_ge(s["yrow"], u + 1)
                for j in range(2):
                    for k in range(2):
                        t = pe.transpose(psR[:, D * j + P * k:D * j + P * k + P], yT[:, k, j * P:(j + 1) * P], ident[:, :])
                t.then_inc(s["yturned"], 1)

            def expert(e, p, first, end):
                with pe.Fori(first, end) as u:
                    pe.wait_ge(s["w1l"], e + 1)
                    pe.wait_ge(s["xl"], u + 1)
                    pe.wait_ge(s["unit_hid"], u + 1)
                    for f in range(FT):
                        if f >= 4:
                            pe.wait_ge(s["gelu"], 8 * u + f - 3)
                        for k in range(2):
                            t = mm3(pe, ps1[f % 4][:, 0:UT], (w1h[p][:, k, f * P:(f + 1) * P], w1l[p][:, k, f * P:(f + 1) * P]),
                                    (xh[:, k, :], xl[:, k, :]), k == 0, k == 1)
                        t.then_inc(s["up"], 1)
                    turn_back(u)
                    turn(u + 1)
                    pe.wait_ge(s["w2l"], e + 1)
                    for f in range(FT):
                        pe.wait_ge(s["lo"], 8 * u + f + 1)
                        for k in range(2):
                            a = (w2h[p][:, f, k * P:(k + 1) * P], w2l[p][:, f, k * P:(k + 1) * P])
                            out = ps2[:, UT * k:UT * k + UT]
                            start = f == 0 and k == 0
                            pe.matmul(out, a[0], dh[:, f, :], start=start, stop=False, skip_group_check=True)
                            pe.matmul(out, a[0], dl[:, f, :], start=False, stop=False, skip_group_check=True)
                            t = pe.matmul(out, a[1], dh[:, f, :], start=False, stop=(f == FT - 1), skip_group_check=True)
                    t.then_inc(s["down"], 1)

            turn(0)
            experts(pe, expert)
            end = entry(pe, E + 1)
            pe.wait_ge(s["yT"], 2 * end)
            turn_back(end)


def combine_phase(nc, sem, io, out, X, keep):
    g1, g2, pos, yrows = (keep[n] for n in ("g1", "g2", "pos", "yrows"))
    with ExitStack() as ctx:
        yg = ctx.enter_context(nc.sbuf_tensor("c_yg", [P, GRP, 2, D], F32))
        got = [sem(f"c_got{g}") for g in range(GRP)]
        first, done, stored = sem("c_first"), sem("c_done"), sem("c_stored")
        block = ctx.enter_context(nc.Block())

        @block.gpsimd
        def _(pool):
            for g in range(GRP):
                for k in range(2):
                    pool.indirect_dma_start(yg[:, g, k, :], None, yrows, bass.IndirectOffsetOnAxis(pos[:, k, g:g + 1], 0),
                                            element_offset=UT * D).then_inc(got[g], 16)

        @block.vector
        def _(dve):
            for g in range(GRP):
                dve.wait_ge(got[g], 32)
                dve.scalar_tensor_tensor(X[:, g, :], yg[:, g, 0, :], g1[:, g:g + 1], X[:, g, :], ALU.mult, ALU.add).then_inc(first, 1)
                dve.wait_ge(first, g + 1)
                dve.scalar_tensor_tensor(X[:, g, :], yg[:, g, 1, :], g2[:, g:g + 1], X[:, g, :], ALU.mult, ALU.add).then_inc(done, 1)

        @block.sync
        def _(sy):
            for g in range(0, GRP, 4):
                sy.wait_ge(done, g + 4)
                sy.dma_start(out[:, g:g + 4, :], X[:, g:g + 4, :]).then_inc(stored, 16)
            sy.wait_ge(stored, 16 * (GRP // 4))


def phase(nc, run, *args):
    with ExitStack() as ctx:
        made = []

        def sem(name):
            made.append(ctx.enter_context(nc.semaphore(name)))
            return made[-1]

        run(nc, sem, *args)
        nums = sorted(x.num for x in made)
        with nc.Block() as block:
            @block.sync
            def _(sp):
                while nums:
                    n = 1
                    while n < len(nums) and nums[n] == nums[0] + n:
                        n += 1
                    sp.sem_clear(range(nums[0], nums[0] + n))
                    del nums[:n]


def store_phase(nc, sem, out, X):
    stored = sem("z_stored")
    with nc.Block() as block:
        @block.sync
        def _(sp):
            sp.dma_start(out, X[:, :, :]).then_inc(stored, 16)
            sp.wait_ge(stored, 16)


def zero_phase(nc, sem, rows, yrows):
    with ExitStack() as ctx:
        zero = ctx.enter_context(nc.sbuf_tensor("zero", [P, D], F32))
        set_, stored = sem("z_set"), sem("z_stored")
        block = ctx.enter_context(nc.Block())

        @block.vector
        def _(dve):
            dve.memset(zero[:, :], 0.0).then_inc(set_, 1)

        @block.sync
        def _(sp):
            sp.wait_ge(set_, 1)
            for dram in (rows, yrows):
                dst = dram.rearrange("(p j) d -> p j d", p=P)
                sp.dma_start(dst, zero[:, :].unsqueeze(1).to_broadcast([P, SLOTS // P, D])).then_inc(stored, 16)
            sp.wait_ge(stored, 32)


def program(nc, io, out):
    with ExitStack() as ctx:
        X = ctx.enter_context(nc.sbuf_tensor("X", [P, GRP, D], F32))
        if STAGES > 2:
            rows = nc.dram_tensor("token_rows", (SLOTS, D), F32, kind="Internal").ap()
            yrows = nc.dram_tensor("expert_rows", (SLOTS, D), F32, kind="Internal").ap()
            phase(nc, zero_phase, rows, yrows)
        with ExitStack() as c2:
            kv = {
                "qT": c2.enter_context(nc.sbuf_tensor("qT", [P, 4, B * L], F32)),
                "KX": c2.enter_context(nc.sbuf_tensor("KX", [P, 4, B, TAIL], F32)),
                "xe": nc.dram_tensor("tail_values", (B, TAIL, D), F32, kind="Internal").ap(),
            }
            phase(nc, latents_phase, io, X, kv)
            phase(nc, xattn_phase, io, X, kv)
        if STAGES > 1:
            phase(nc, mamba_phase, io, X)
        if STAGES > 2:
            keep = {n: ctx.enter_context(nc.sbuf_tensor(n, shape, dt)) for n, shape, dt in (
                ("tokens", [P, GRP, D], F32), ("logits", [P, GRP, E], F32), ("g1", [P, GRP], F32), ("g2", [P, GRP], F32),
                ("pos", [P, 2, GRP], mybir.dt.uint32), ("cum", [P, E + 2], mybir.dt.int32))}
            keep["rows"] = rows
            keep["yrows"] = yrows
            phase(nc, attention_phase, io, X, keep)
            phase(nc, routing_phase, io, keep)
            phase(nc, experts_phase, io, keep)
            phase(nc, combine_phase, io, out, X, keep)
        else:
            phase(nc, store_phase, out, X)


def rope_tables():
    inv = (np.float32(1.0) / np.float32(10000.0) ** (np.arange(0, DH, 2, dtype=np.float32) / np.float32(DH))).astype(np.float32)
    theta = (np.arange(S, dtype=np.float32)[:, None] * inv[None, :]).astype(np.float32)
    cos, sin = np.cos(theta).T.astype(np.float32), np.sin(theta).T.astype(np.float32)
    return np.tile(cos, (4, 1)), np.tile(sin, (4, 1))


def layouts(v):
    c = np.ascontiguousarray

    def rows(w):
        return c(w.reshape(-1, P, w.shape[-1]).transpose(1, 0, 2))

    def every(*vs):
        return c(np.tile(np.stack(vs)[None], (P, 1, 1)))

    def split_heads(w):
        return rows(w.reshape(D, 2, 4, 2, 32).transpose(0, 1, 3, 2, 4).reshape(D, 512))

    a = {}
    a["x"] = rows(v["x"].reshape(B * L, D))
    a["ctx"] = c(v["ctx_1024"][:, :256].reshape(B, 2, P, D).transpose(0, 2, 1, 3))
    a["ctx_last"] = c(v["ctx_1024"][:, 256])
    a["wq"] = split_heads(v["L0_xattn_Wq"])
    a["wk"] = split_heads(v["L0_xattn_Wkv"][:, :512])
    a["wv"] = rows(v["L0_xattn_Wkv"][:, 512:])
    a["wo"] = rows(v["L0_xattn_Wo"])
    a["gb"] = every(v["L0_xattn_gamma_x"], v["L0_xattn_beta_x"], v["L0_xattn_gamma_l"], v["L0_xattn_beta_l"])
    a["ident"] = np.eye(P, dtype=np.float32)
    cos, sin = rope_tables()
    a["cos"] = c(cos[:, :256])
    a["sin"] = c(np.stack([-sin[:, :256], sin[:, :256]], 1))
    a["edge"] = c(np.stack([cos[:, 256], sin[:, 256]], 1))
    if STAGES > 1:
        more_layouts(a, v)
    return a


def more_layouts(a, v):
    c = np.ascontiguousarray

    def rows(w):
        return c(w.reshape(-1, P, w.shape[-1]).transpose(1, 0, 2))

    def column(x):
        return x.reshape(-1, P).T

    a["m_w"] = rows(v["L0_attn_in_proj_w"].T)
    a["m_out"] = rows(v["L0_attn_out_proj_w"].T)
    cw = v["L0_attn_conv_w"].reshape(CONVT, P, 4).transpose(1, 0, 2).reshape(P, 4 * CONVT)
    a["m_cols"] = c(np.concatenate([cw, column(v["L0_attn_conv_b"]), column(np.repeat(v["L0_attn_D"], DI // NH)),
                                    column(v["L0_attn_norm_w"])], 1))
    a["m_rows"] = c(np.tile(np.stack([v["L0_attn_dt_bias"], v["L0_attn_A_log"]])[None], (P, 1, 1)))
    i = np.arange(P)
    same = (i[:, None] // L) == (i[None, :] // L)
    a["tri"] = (same & (i[:, None] <= i[None, :])).astype(np.float32)
    a["aft"] = (same & (i[:, None] > i[None, :])).astype(np.float32)
    if STAGES > 2:
        for n in ("q", "k", "v", "p"):
            a["s_w" + n] = rows(v["L0_ffn_W" + n])
        a["s_gw"] = rows(v["L0_ffn_gate_W"])
        vs = [v["L0_ffn_" + n] for n in ("ln1_g", "ln1_b", "bq", "bk", "bv", "ln2_g", "ln2_b", "ln2_b")]
        a["s_cols"] = c(np.stack([column(x) for x in vs], 1))
        a["s_bp"] = c(np.tile(v["L0_ffn_bp"][None], (P, 1)))
        a["s_gb"] = c(np.tile(v["L0_ffn_gate_b"][None], (P, 1)))
        a["heads"] = np.where(i[:, None] // DF == np.arange(8)[None], np.float32(DF ** -0.5), np.float32(0))
        a["causal"] = np.where(np.arange(L)[None] > (i % L)[:, None], np.float32(-1e30), np.float32(0))
        a["experts"] = np.tile(np.arange(E, 0, -1, dtype=np.float32)[None], (P, 1))
        a["e_w1"] = c(v["L0_ffn_exp_W1"].reshape(E, 2, P, FH).transpose(0, 2, 1, 3))
        a["e_w2"] = c(v["L0_ffn_exp_W2"].reshape(E, FH // P, P, D).transpose(0, 2, 1, 3))
        a["e_b"] = c(np.concatenate([v["L0_ffn_exp_b1"], v["L0_ffn_exp_b2"]], 1).reshape(E, (FH + D) // P, P).transpose(2, 0, 1))
        a["steps"] = np.tile(np.arange(1, 8, dtype=np.float32)[None] * UT, (P, 1))
        a["before"] = (i[:, None] < i[None, :]).astype(np.float32)

STAGES = 3


def kernel(**inputs):
    import concourse.bacc as bacc
    from concourse.bass_utils import run_bass_kernel_spmd

    arrays = layouts({k: np.asarray(v) for k, v in inputs.items()})
    nc = bacc.Bacc("TRN2", target_bir_lowering=False, num_devices=1)
    io = {k: nc.dram_tensor("in_" + k, a.shape, mybir.dt.from_np(a.dtype), kind="ExternalInput").ap() for k, a in arrays.items()}
    out = nc.dram_tensor("out_0", (P, GRP, D), F32, kind="ExternalOutput").ap()
    program(nc, io, out)
    r = run_bass_kernel_spmd(nc, [{"in_" + k: a for k, a in arrays.items()}], core_ids=[0])
    return np.ascontiguousarray(r.results[0]["out_0"].transpose(1, 0, 2)).reshape(B, L, D)
```

```python
from contextlib import ExitStack

import concourse.bass as bass
import numpy as np
from concourse import mybir

F32 = mybir.dt.float32
F32R = mybir.dt.float32r
ALU = mybir.AluOpType
ACT = mybir.ActivationFunctionType
AXX = mybir.AxisListType.X

P = 128
B, L, D = 64, 32, 256
S = 257
H, DH = 8, 64
GRP = B * L // P
BPG = P // L
KEYS = S + L
TAIL = KEYS - 256
EPS = 1e-5


def mm3(eng, out, a, b, start, stop):
    eng.matmul(out, a[0], b[0], start=start, stop=False)
    eng.matmul(out, a[0], b[1], start=False, stop=False)
    return eng.matmul(out, a[1], b[0], start=False, stop=stop)


def wait_ahead(dve, sem, value, tick):
    dve.wait_ge(sem, value)
    dve.memset(tick[:, :], 0.0)


def latents_phase(nc, sem, io, X, kv):
    qT, KX, xe = kv["qT"], kv["KX"], kv["xe"]
    C = 4
    WIN = 5
    with ExitStack() as ctx:
        def sb(name, shape, dt=F32):
            return ctx.enter_context(nc.sbuf_tensor("l_" + name, shape, dt))

        wq = sb("wq", [P, 2, 512])
        wk = sb("wk", [P, 2, 512])
        wqh, wql = sb("wqh", [P, 2, 512], F32R), sb("wql", [P, 2, 512], F32R)
        wkh, wkl, gb, ident = (kv[n] for n in ("wkh", "wkl", "gb", "ident"))
        edge = sb("edge", [P, 2])
        last = sb("last", [B, D])
        n1 = sb("n1", [P, GRP, D])
        ln = sb("ln", [P, GRP, D])
        st = sb("st", [P, GRP, 6])
        mv = sb("mv", [P, GRP, 2])
        ve = sb("ve", [P, GRP])
        rs = sb("rs", [P, GRP])
        half = sb("half", [P, GRP])
        st2 = sb("st2", [B, 6])
        mv2 = sb("mv2", [B, 2])
        ve2 = sb("ve2", [B, 2])
        xl = sb("xl", [B, D])
        lnTh = sb("lnTh", [P, 2, 2, 512], F32R)
        lnTl = sb("lnTl", [P, 2, 2, 512], F32R)
        lastT = sb("lastT", [P, 2, B])
        t1 = sb("t1", [P, 2, B])
        t2 = sb("t2", [P, 2, B])
        psT = ctx.enter_context(nc.psum_tensor("l_psT", [P, 2, 512], F32))
        psJ = ctx.enter_context(nc.psum_tensor("l_psJ", [P, 4, 512], F32))
        psL = ctx.enter_context(nc.psum_tensor("l_psL", [P, 2, 512], F32))

        x_in, w_in, gb_in, zero_set = [sem(f"l_x_in{c}") for c in range(C)], sem("l_w_in"), sem("l_gb_in"), sem("l_zero_set")
        half_set, stats, aggr, var, rstd = (sem("l_" + n) for n in ("half_set", "stats", "aggr", "var", "rstd"))
        norm, scaled, ln_ready = sem("l_norm"), sem("l_scaled"), sem("l_ln_ready")
        w_hi, w_lo, lnT_lo = sem("l_w_hi"), sem("l_w_lo"), sem("l_lnT_lo")
        a_in = sem("l_a_in")
        turned, turned_out, proj, proj_out = (sem("l_" + n) for n in ("turned", "turned_out", "proj", "proj_out"))
        stored = sem("l_stored")
        last_ready, last_var, last_rstd, last_t, last_tout, last_k, last_mul, last_keys = (
            sem("l_last" + n) for n in "abcdefgh")
        block = ctx.enter_context(nc.Block())

        @block.sync
        def _(sp):
            for c in range(C):
                sp.dma_start(X[:, 4 * c:4 * c + 4, :], io["x"][:, 4 * c:4 * c + 4, :]).then_inc(x_in[c], 16)
            sp.wait_ge(w_in, 16 * WIN)
            for n in ("cos", "wv", "sin", "wo"):
                sp.dma_start(kv[n][tuple(slice(None) for _ in kv[n].shape)], io[n]).then_inc(a_in, 16)
            for c in range(C):
                sp.wait_ge(ln_ready, c + 1)
                for g in range(4 * c, 4 * c + 4):
                    for b in range(BPG):
                        sp.dma_start(xe[4 * g + b, 0:L, :], ln[L * b:L * b + L, g, :]).then_inc(stored, 16)
            sp.wait_ge(last_ready, 4)
            sp.dma_start(xe[:, L, :], xl[:, :]).then_inc(stored, 16)
            sp.wait_ge(stored, 16 * (B + 1))
            sp.wait_ge(a_in, 16 * 4)

        @block.gpsimd
        def _(pool):
            pool.memset(half[:, :], -0.5).then_inc(half_set, 1)
            pool.wait_ge(half_set, 1)

            def power(i):
                c = i // 2
                pool.wait_ge(var, i + 1)
                pool.tensor_tensor(rs[:, 4 * c:4 * c + 4], ve[:, 4 * c:4 * c + 4], half[:, 0:4], ALU.pow).then_inc(rstd, 1)

            power(0)
            power(1)
            for i, (w, hi, lo) in enumerate(((wq, wqh, wql), (wk, wkh, wkl))):
                pool.wait_ge(w_hi, i + 1)
                pool.tensor_tensor(lo[:, :, :], w[:, :, :], hi[:, :, :].bitcast(F32), ALU.subtract).then_inc(w_lo, 1)
            for i in range(2, 2 * C):
                power(i)
            pool.wait_ge(last_var, 1)
            pool.tensor_tensor(ve2[:, 1:2], ve2[:, 0:1], half[0:B, 0:1], ALU.pow).then_inc(last_rstd, 1)

        @block.vector
        def _(dve):
            if kv["zeros"]:
                dve.memset(kv["zeros"][2][:, :], 0.0).then_inc(zero_set, 1)
            dve.wait_ge(gb_in, 16)

            def statistics(i, c, src):
                for g in range(4 * c, 4 * c + 4):
                    dve.bn_stats(st[:, g, :], src[:, g, :]).then_inc(stats, 1)
                dve.wait_ge(stats, 4 * (i + 1))
                for g in range(4 * c, 4 * c + 4):
                    dve.bn_aggr(mv[:, g, :], st[:, g, :]).then_inc(aggr, 1)
                dve.wait_ge(aggr, 4 * (i + 1))
                dve.tensor_scalar(ve[:, 4 * c:4 * c + 4], mv[:, 4 * c:4 * c + 4, 1], EPS, None, ALU.add).then_inc(var, 1)

            def low(c):
                dve.wait_ge(turned_out, c + 1)
                if c >= 2:
                    dve.wait_ge(proj, 8 * (c - 1))
                dve.tensor_tensor(lnTl[:, c % 2, :, :], psT[:, :, :], lnTh[:, c % 2, :, :].bitcast(F32),
                                  ALU.subtract).then_inc(lnT_lo, 1)

            for c in range(C):
                a, z = 4 * c, 4 * c + 4
                dve.wait_ge(x_in[c], 16)
                statistics(2 * c, c, X)
                if c:
                    low(c - 1)
                dve.wait_ge(rstd, 2 * c + 1)
                for g in range(a, z):
                    dve.tensor_scalar(n1[:, g, :], X[:, g, :], mv[:, g, 0:1], rs[:, g:g + 1],
                                      ALU.subtract, ALU.mult).then_inc(norm, 1)
                dve.wait_ge(norm, z)
                statistics(2 * c + 1, c, n1)
                for g in range(a, z):
                    dve.scalar_tensor_tensor(n1[:, g, :], n1[:, g, :], mv[:, g, 0:1], gb[:, 2, :],
                                             ALU.subtract, ALU.mult).then_inc(scaled, 1)
                dve.wait_ge(rstd, 2 * c + 2)
                dve.wait_ge(scaled, z)
                for g in range(a, z):
                    t = dve.scalar_tensor_tensor(ln[:, g, :], n1[:, g, :], rs[:, g:g + 1], gb[:, 3, :], ALU.mult, ALU.add)
                t.then_inc(ln_ready, 1)
            low(C - 1)
            dve.wait_ge(w_in, 16 * WIN)
            dve.bn_stats(st2[:, :], last[:, :]).then_inc(last_ready, 1)
            dve.wait_ge(last_ready, 1)
            dve.bn_aggr(mv2[:, :], st2[:, :]).then_inc(last_ready, 1)
            dve.wait_ge(last_ready, 2)
            dve.tensor_scalar(ve2[:, 0:1], mv2[:, 1:2], EPS, None, ALU.add).then_inc(last_var, 1)
            dve.scalar_tensor_tensor(xl[:, :], last[:, :], mv2[:, 0:1], gb[0:B, 0, :],
                                     ALU.subtract, ALU.mult).then_inc(last_ready, 1)
            dve.wait_ge(last_ready, 3)
            dve.wait_ge(last_rstd, 1)
            dve.scalar_tensor_tensor(xl[:, :], xl[:, :], ve2[:, 1:2], gb[0:B, 1, :],
                                     ALU.mult, ALU.add).then_inc(last_ready, 1)
            dve.wait_ge(last_k, 1)
            k = psL[:, 1, 0:4 * B].rearrange("p (g a b) -> p g a b", g=2, a=2)
            dve.tensor_scalar(t1[:, :, :], k[:, :, 1, :], edge[:, 1:2], None, ALU.mult).then_inc(last_mul, 1)
            dve.tensor_scalar(t2[:, :, :], k[:, :, 0, :], edge[:, 1:2], None, ALU.mult).then_inc(last_mul, 1)
            dve.wait_ge(last_mul, 2)
            for g in range(2):
                dve.scalar_tensor_tensor(KX[:, 2 * g, :, L], k[:, g, 0, :], edge[:, 0:1], t1[:, g, :],
                                         ALU.mult, ALU.subtract)
                dve.scalar_tensor_tensor(KX[:, 2 * g + 1, :, L], k[:, g, 1, :], edge[:, 0:1], t2[:, g, :],
                                         ALU.mult, ALU.add).then_inc(last_keys, 1)

        @block.tensor
        def _(pe):
            pe.wait_ge(w_in, 16 * WIN)
            n = 0
            for c in range(C):
                pe.wait_ge(ln_ready, c + 1)
                if c:
                    pe.wait_ge(lnT_lo, c)
                for k in range(2):
                    for j in range(4):
                        t = pe.transpose(psT[:, k, j * P:(j + 1) * P], ln[:, 4 * c + j, k * P:(k + 1) * P], ident[:, :])
                t.then_inc(turned, 1)
                pe.wait_ge(lnT_lo, c + 1)
                for i, (hi, lo) in enumerate(((wqh, wql), (wkh, wkl))):
                    pe.wait_ge(w_lo, i + 1)
                    for m in range(4):
                        if n >= 4:
                            pe.wait_ge(proj_out, n - 3)
                        for k in range(2):
                            t = mm3(pe, psJ[:, n % 4, :], (hi[:, k, m * P:(m + 1) * P], lo[:, k, m * P:(m + 1) * P]),
                                    (lnTh[:, c % 2, k, :], lnTl[:, c % 2, k, :]), k == 0, k == 1)
                        t.then_inc(proj, 1)
                        n += 1
            pe.wait_ge(last_ready, 4)
            for k in range(2):
                t = pe.transpose(psL[:, 0, k * B:(k + 1) * B], xl[:, k * P:(k + 1) * P], ident[0:B, 0:B])
            t.then_inc(last_t, 1)
            pe.wait_ge(last_tout, 1)
            for m in range(4):
                for k in range(2):
                    t = pe.matmul(psL[:, 1, m * B:(m + 1) * B], wk[:, k, m * P:(m + 1) * P], lastT[:, k, :],
                                  start=(k == 0), stop=(k == 1))
            t.then_inc(last_k, 1)

        @block.scalar
        def _(act):
            act.dma_start(gb[:, :, :], io["gb"]).then_inc(gb_in, 16)
            for d, src in ((ident, "ident"), (wq, "wq"), (wk, "wk"), (edge, "edge"), (last, "ctx_last")):
                act.dma_start(d[tuple(slice(None) for _ in d.shape)], io[src]).then_inc(w_in, 16)
            act.wait_ge(w_in, 16 * WIN)
            for w, hi in ((wq, wqh), (wk, wkh)):
                act.activation(hi[:, :, :], w[:, :, :], ACT.Copy).then_inc(w_hi, 1)
            if kv["zeros"]:
                act.wait_ge(x_in[C - 1], 16)
                act.wait_ge(zero_set, 1)
                for dram in kv["zeros"][:2]:
                    act.dma_start(dram.rearrange("(p j) d -> p j d", p=P),
                                  kv["zeros"][2][:, :].unsqueeze(1).to_broadcast([P, SLOTS // P, D])).then_inc(kv["zeros"][3], 16)
            n = 0
            for c in range(C):
                act.wait_ge(turned, c + 1)
                if c >= 2:
                    act.wait_ge(proj, 8 * (c - 1))
                act.activation(lnTh[:, c % 2, :, :], psT[:, :, :], ACT.Copy).then_inc(turned_out, 1)
                for w in range(2):
                    for m in range(4):
                        act.wait_ge(proj, n + 1)
                        if w == 0:
                            act.activation(qT[:, m, 512 * c:512 * c + 512], psJ[:, n % 4, :], ACT.Copy,
                                           scale=DH ** -0.5).then_inc(proj_out, 1)
                        else:
                            act.activation(KX[:, m, 16 * c:16 * c + 16, 0:L],
                                           psJ[:, n % 4, :].rearrange("p (b i) -> p b i", i=L),
                                           ACT.Copy).then_inc(proj_out, 1)
                        n += 1
            act.wait_ge(last_t, 1)
            act.activation(lastT[:, :, :], psL[:, 0, 0:2 * B].rearrange("p (k b) -> p k b", k=2),
                           ACT.Copy).then_inc(last_tout, 1)


def xattn_phase(nc, sem, io, X, kv):
    qT, KX, xe = kv["qT"], kv["KX"], kv["xe"]
    with ExitStack() as ctx:
        def sb(name, shape, dt=F32):
            return ctx.enter_context(nc.sbuf_tensor("a_" + name, shape, dt))

        def pb(name, shape):
            return ctx.enter_context(nc.psum_tensor("a_" + name, shape, F32))

        wkh, wkl, wv, wo, gb, ident, cos, sin = (kv[n] for n in ("wkh", "wkl", "wv", "wo", "gb", "ident", "cos", "sin"))
        C = [sb(f"C{i}", [P, 2, D]) for i in range(2)]
        cen = [sb(f"cen{i}", [P, 2, D]) for i in range(2)]
        xn = [sb(f"xn{i}", [P, 2, D]) for i in range(2)]
        vh = [sb(f"vh{i}", [P, 2, D], F32R) for i in range(4)]
        vl = [sb(f"vl{i}", [P, 2, D], F32R) for i in range(4)]
        xt = [sb(f"xt{i}", [TAIL, D]) for i in range(4)]
        xh = [sb(f"xh{i}", [P, 2, 256], F32R) for i in range(2)]
        xl = [sb(f"xl{i}", [P, 2, 256], F32R) for i in range(2)]
        st = [sb(f"st{i}", [P, 2, 6]) for i in range(2)]
        mv = [sb(f"mv{i}", [P, 2, 2]) for i in range(2)]
        ve = [sb(f"ve{i}", [P, 2]) for i in range(2)]
        rs = [sb(f"rs{i}", [P, 2]) for i in range(2)]
        tick = sb("tick", [P, 1])
        half = sb("half", [P, 2])
        r1 = [sb(f"r1{i}", [P, 2, 256]) for i in range(2)]
        r2 = [sb(f"r2{i}", [P, 2, 256]) for i in range(2)]
        K = [sb(f"K{i}", [P, 4, KEYS]) for i in range(2)]
        Q = [sb(f"Q{i}", [P, 4, P]) for i in range(2)]
        mx = [sb(f"mx{i}", [P, 2]) for i in range(2)]
        nm = [sb(f"nm{i}", [P, 2]) for i in range(2)]
        sm = [sb(f"sm{i}", [P, 2]) for i in range(2)]
        ri = [sb(f"ri{i}", [P, 2]) for i in range(2)]
        pr = [sb(f"pr{i}", [P, 2, KEYS]) for i in range(2)]
        ph = [sb(f"ph{i}", [P, 2, 256], F32R) for i in range(2)]
        pl = [sb(f"pl{i}", [P, 2, 256], F32R) for i in range(2)]
        pt = [sb(f"pt{i}", [TAIL, 256]) for i in range(2)]
        px = sb("px", [P, 2, H, BPG, L])
        uT = sb("uT", [P, 4, P])

        psT = pb("psT", [P, 2, 256])
        psK = [pb(f"psK{i}", [P, 2, 256]) for i in range(2)]
        psS = [pb(f"psS{i}", [P, 512]) for i in range(2)]
        psP = [pb(f"psP{i}", [P, 512]) for i in range(2)]
        psV = pb("psV", [P, 512])

        names = ("half_set", "zeroed", "stats", "aggr", "var", "rstd", "centred", "normed",
                 "turned", "xt_hi", "xt_lo", "projected", "rotated", "keys", "tails", "blocks", "scored", "peak",
                 "peak_neg", "exped", "recip", "probs", "pturned", "pt_out", "p_lo", "v_hi", "v_lo", "attended", "px_out", "valued", "u_out",
                 "outed", "added")
        s = {n: sem("a_" + n) for n in names}
        c_in = [sem(f"a_c_in{i}") for i in range(2)]
        t_in = [sem(f"a_t_in{i}") for i in range(4)]
        block = ctx.enter_context(nc.Block())
        LASTG = GRP - 1


        @block.sync
        def _(sp):
            def load(g, j, first=False):
                n = 4 * g + j
                if not (first and j < 2):
                    sp.wait_ge(s["normed"], n - 1)
                sp.dma_start(C[j % 2][:, :, :], io["ctx"][n]).then_inc(c_in[j % 2], 16)

            def load_tail(g, j, first=False):
                if not first:
                    sp.wait_ge(s["attended"], 4 * g + j - 3)
                sp.dma_start(xt[j][:, :], xe[4 * g + j]).then_inc(t_in[j], 16)

            for j in range(4):
                load(0, j, True)
                if j >= 2:
                    load_tail(0, j - 2, True)
            load(1, 0)
            load_tail(0, 2, True)
            load(1, 1)
            load_tail(0, 3, True)
            load(1, 2)
            load_tail(1, 0)
            load(1, 3)
            load_tail(1, 1)
            with sp.Fori(2, GRP) as g:
                for j in range(4):
                    load(g, j)
                    load_tail(g - (j < 2), (j + 2) % 4)
            load_tail(LASTG, 2)
            load_tail(LASTG, 3)

        @block.gpsimd
        def _(pool):
            pool.memset(half[:, :], -0.5).then_inc(s["half_set"], 1)
            for i in range(2):
                pool.memset(Q[i][:, :, :], 0.0).then_inc(s["zeroed"], 1)
            pool.wait_ge(s["half_set"], 1)

            def power(g, j):
                n = 4 * g + j
                pool.wait_ge(s["var"], n + 1)
                pool.tensor_tensor(rs[j % 2][:, :], ve[j % 2][:, :], half[:, :], ALU.pow).then_inc(s["rstd"], 1)

            def rope_add(g, j, G, first=False):
                n = 4 * g + j
                if not (first and j < 2) and G == 0:
                    pool.wait_ge(s["scored"], 2 * (n - 1))
                pool.wait_ge(s["rotated"], 3 * (2 * n + G + 1))
                pool.tensor_tensor(K[j % 2][:, 2 * G:2 * G + 2, 0:256], r1[G][:, :, :], r2[G][:, :, :],
                                   ALU.add).then_inc(s["keys"], 1)

            def values_low(g, j, first=False):
                pool.wait_ge(s["v_hi"], 4 * g + j + 1)
                pool.tensor_tensor(vl[j][:, :, :], xn[j % 2][:, :, :], vh[j][:, :, :].bitcast(F32), ALU.subtract).then_inc(s["v_lo"], 1)

            def slot(g, j, first=False, last=False):
                rope_add(g, j, 0, first)
                if not (last and j == 3):
                    values_low(g + (j + 1) // 4, (j + 1) % 4)
                if not (last and j >= 2):
                    power(g, j + 2) if j < 2 else power(g + 1, j - 2)
                rope_add(g, j, 1, first)

            power(0, 0)
            power(0, 1)
            values_low(0, 0)
            for j in range(4):
                slot(0, j, first=True)
            with pool.Fori(1, LASTG) as g:
                for j in range(4):
                    slot(g, j)
            for j in range(4):
                slot(LASTG, j, last=True)

        @block.vector
        def _(dve):
            def statistics(g, j):
                n = 4 * g + j
                dve.wait_ge(c_in[j % 2], 16 * (2 * g + j // 2 + 1))
                for t in range(2):
                    dve.bn_stats(st[j % 2][:, t, :], C[j % 2][:, t, :]).then_inc(s["stats"], 1)
                wait_ahead(dve, s["stats"], 2 * (n + 1), tick)
                for t in range(2):
                    dve.bn_aggr(mv[j % 2][:, t, :], st[j % 2][:, t, :]).then_inc(s["aggr"], 1)
                dve.wait_ge(s["aggr"], 2 * (n + 1))
                dve.tensor_scalar(ve[j % 2][:, :], mv[j % 2][:, :, 1], EPS, None, ALU.add).then_inc(s["var"], 1)

            def normalise(g, j, first=False):
                n = 4 * g + j
                for t in range(2):
                    dve.scalar_tensor_tensor(cen[j % 2][:, t, :], C[j % 2][:, t, :], mv[j % 2][:, t, 0:1], gb[:, 0, :],
                                             ALU.subtract, ALU.mult).then_inc(s["centred"], 1)
                dve.wait_ge(s["rstd"], n + 1)
                dve.wait_ge(s["centred"], 2 * (n + 1))
                if not first:
                    dve.wait_ge(s["turned"], n - 1)
                    dve.wait_ge(s["v_lo"], n - 1)
                dve.scalar_tensor_tensor(xn[j % 2][:, 0, :], cen[j % 2][:, 0, :], rs[j % 2][:, 0:1], gb[:, 1, :],
                                         ALU.mult, ALU.add)
                dve.scalar_tensor_tensor(xn[j % 2][:, 1, :], cen[j % 2][:, 1, :], rs[j % 2][:, 1:2], gb[:, 1, :],
                                         ALU.mult, ALU.add).then_inc(s["normed"], 1)

            def low(g, j):
                n = 4 * g + j
                dve.wait_ge(s["xt_hi"], n + 1)
                dve.tensor_tensor(xl[j % 2][:, :, :], psT[:, :, :], xh[j % 2][:, :, :].bitcast(F32),
                                  ALU.subtract).then_inc(s["xt_lo"], 1)

            def probs_low(g, j):
                n = 4 * g + j
                for G in range(2):
                    dve.wait_ge(s["pt_out"], 2 * (2 * n + G + 1))
                    cols = slice(G * P, (G + 1) * P)
                    dve.tensor_tensor(pl[j % 2][:, :, cols], psP[G][:, 0:256].rearrange("p (t c) -> p t c", t=2),
                                      ph[j % 2][:, :, cols].bitcast(F32), ALU.subtract).then_inc(s["p_lo"], 1)

            def rotate(g, j, G, first=False):
                n = 4 * g + j
                dve.wait_ge(s["projected"], 2 * n + G + 1)
                if not (first and j == 0):
                    dve.wait_ge(s["keys"], 2 * n + G - 1)
                dve.tensor_tensor(r1[G][:, :, :], psK[G][:, :, :], cos[:, :].unsqueeze(1).to_broadcast([P, 2, 256]),
                                  ALU.mult).then_inc(s["rotated"], 1)
                for a in range(2):
                    dve.tensor_tensor(r2[G][:, a, :], psK[G][:, 1 - a, :], sin[:, a, :], ALU.mult).then_inc(s["rotated"], 1)

            def peaks(g, j):
                n = 4 * g + j
                for G in range(2):
                    dve.wait_ge(s["scored"], 2 * n + G + 1)
                    dve.reduce_max(mx[j % 2][:, G:G + 1], psS[G][:, 0:KEYS], AXX).then_inc(s["peak"], 1)
                dve.wait_ge(s["peak"], 2 * (n + 1))
                dve.tensor_scalar(nm[j % 2][:, :], mx[j % 2][:, :], -1.0, None, ALU.mult).then_inc(s["peak_neg"], 1)

            def shares(g, j):
                n = 4 * g + j
                dve.wait_ge(s["exped"], 2 * (n + 1))
                dve.reciprocal(ri[j % 2][:, :], sm[j % 2][:, :]).then_inc(s["recip"], 1)

            def residual(g):
                dve.wait_ge(s["outed"], g + 1)
                dve.tensor_tensor(X[:, g, :], X[:, g, :], psV[:, 0:D], ALU.add).then_inc(s["added"], 1)

            def slot(g, j, first=False, last=False, batches=(True, True)):
                prev = (g, j - 1) if j else (g - 1, 3)
                prev2 = (g, j - 2) if j >= 2 else (g - 1, j + 2)
                if batches[0] and not (last and j == 3):
                    normalise(g + (j + 1) // 4, (j + 1) % 4, first and j == 0)
                if batches[0]:
                    rotate(g, j, 0, first)
                if not (first and j < 2) and not (not batches[0] and j == 2):
                    probs_low(*prev2)
                if batches[1] and not (first and j == 0):
                    peaks(*prev)
                if batches[0] and not (last and j == 3):
                    low(g + (j + 1) // 4, (j + 1) % 4)
                if batches[0] and not (last and j >= 2):
                    statistics(g + (j + 2) // 4, (j + 2) % 4)
                if batches[1] and not (first and j == 0):
                    shares(*prev)
                if j == 2 and not first:
                    residual(g - 1)
                if batches[0]:
                    rotate(g, j, 1, first)

            for j in range(2):
                statistics(0, j)
            normalise(0, 0, True)
            low(0, 0)
            for j in range(4):
                slot(0, j, first=True)
            with dve.Fori(1, LASTG) as g:
                for j in range(4):
                    slot(g, j)
            for j in range(4):
                slot(LASTG, j, last=True)
            slot(GRP, 0, batches=(False, True))
            slot(GRP, 1, batches=(False, False))
            slot(GRP, 2, batches=(False, False))

        @block.scalar
        def _(act):
            act.wait_ge(s["zeroed"], 2)

            def operands(g, j, first=False):
                n = 4 * g + j
                if not (first and j < 2):
                    act.wait_ge(s["scored"], 2 * (n - 1))
                act.activation(K[j % 2][:, :, 256:KEYS], KX[:, :, n, :], ACT.Copy).then_inc(s["tails"], 1)
                for h in range(4):
                    act.activation(Q[j % 2][32 * h:32 * h + 32, :, 32 * h:32 * h + 32],
                                   qT[32 * h:32 * h + 32, :, bass.ds(n * L, L)], ACT.Copy).then_inc(s["blocks"], 1)

            def high(g, j, first=False):
                n = 4 * g + j
                act.wait_ge(s["turned"], n + 1)
                if not (first and j < 2):
                    act.wait_ge(s["projected"], 2 * (n - 1))
                act.activation(xh[j % 2][:, :, :], psT[:, :, :], ACT.Copy).then_inc(s["xt_hi"], 1)

            def values_high(g, j, first=False):
                n = 4 * g + j
                act.wait_ge(s["normed"], n + 1)
                if not first:
                    act.wait_ge(s["attended"], n - 3)
                act.activation(vh[j][:, :, :], xn[j % 2][:, :, :], ACT.Copy).then_inc(s["v_hi"], 1)

            def exps(g, j, first=False):
                n = 4 * g + j
                act.wait_ge(s["peak_neg"], n + 1)
                if not (first and j < 2):
                    act.wait_ge(s["pturned"], 2 * (n - 1))
                for G in range(2):
                    act.activation(pr[j % 2][:, G, :], psS[G][:, 0:KEYS], ACT.Exp, bias=nm[j % 2][:, G:G + 1],
                                   accum_out=sm[j % 2][:, G:G + 1]).then_inc(s["exped"], 1)

            def scaled(g, j):
                act.wait_ge(s["recip"], 4 * g + j + 1)
                for G in range(2):
                    act.activation(pr[j % 2][:, G, :], pr[j % 2][:, G, :], ACT.Copy, scale=ri[j % 2][:, G:G + 1]).then_inc(s["probs"], 1)

            def turned_probs(g, j, first=False):
                n = 4 * g + j
                if not (first and j < 2):
                    act.wait_ge(s["attended"], n - 1)
                for G in range(2):
                    act.wait_ge(s["pturned"], 2 * n + G + 1)
                    p3 = psP[G][:, 0:384].rearrange("p (t c) -> p t c", t=3)
                    act.activation(ph[j % 2][:, :, G * P:(G + 1) * P], p3[:, 0:2, :], ACT.Copy).then_inc(s["pt_out"], 1)
                    act.activation(pt[j % 2][:, G * P:(G + 1) * P], p3[0:TAIL, 2, :],
                                   ACT.Copy).then_inc(s["pt_out"], 1)

            def mixed(g, j, first=False):
                n = 4 * g + j
                act.wait_ge(s["attended"], n + 1)
                if j == 0 and not first:
                    act.wait_ge(s["valued"], g)
                for k in range(2):
                    act.activation(px[:, k, :, j, :], psV[:, 256 * k:256 * k + 256].rearrange("p (h i) -> p h i", h=H),
                                   ACT.Copy).then_inc(s["px_out"], 1)

            def values(g):
                act.wait_ge(s["valued"], g + 1)
                act.activation(uT[:, :, :], psV[:, :].rearrange("p (m t) -> p m t", m=4), ACT.Copy).then_inc(s["u_out"], 1)

            def slot(g, j, first=False, last=False, batches=(True, True)):
                prev = (g, j - 1) if j else (g - 1, 3)
                prev2 = (g, j - 2) if j >= 2 else (g - 1, j + 2)
                attends = not (first and j < 2) and not (not batches[0] and j == 2)
                if batches[0]:
                    operands(g, j, first)
                if attends:
                    turned_probs(*prev2, first)
                if j == 2 and not first:
                    values(g - 1)
                if batches[0] and not (last and j == 3):
                    values_high(g + (j + 1) // 4, (j + 1) % 4, first and j < 3)
                    high(g + (j + 1) // 4, (j + 1) % 4, first and j == 0)
                if batches[1] and not (first and j == 0):
                    exps(*prev, first and j - 1 < 2)
                    scaled(*prev)
                if attends:
                    mixed(*prev2, first)

            values_high(0, 0, True)
            high(0, 0, True)
            for j in range(4):
                slot(0, j, first=True)
            with act.Fori(1, LASTG) as g:
                for j in range(4):
                    slot(g, j)
            for j in range(4):
                slot(LASTG, j, last=True)
            slot(GRP, 0, batches=(False, True))
            slot(GRP, 1, batches=(False, False))
            slot(GRP, 2, batches=(False, False))

        @block.tensor
        def _(pe):
            def turn(g, j, first=False):
                n = 4 * g + j
                pe.wait_ge(s["normed"], n + 1)
                if not (first and j == 0):
                    pe.wait_ge(s["xt_lo"], n)
                for k in range(2):
                    for t in range(2):
                        i = pe.transpose(psT[:, k, t * P:(t + 1) * P], xn[j % 2][:, t, k * P:(k + 1) * P], ident[:, :])
                i.then_inc(s["turned"], 1)

            def project(g, j, G, first=False):
                n = 4 * g + j
                if G == 0:
                    pe.wait_ge(s["xt_lo"], n + 1)
                if not (first and j == 0):
                    pe.wait_ge(s["rotated"], 3 * (2 * n + G - 1))
                for a in range(2):
                    m = 2 * G + a
                    for k in range(2):
                        i = mm3(pe, psK[G][:, a, :], (wkh[:, k, m * P:(m + 1) * P], wkl[:, k, m * P:(m + 1) * P]),
                                (xh[j % 2][:, k, :], xl[j % 2][:, k, :]), k == 0, k == 1)
                i.then_inc(s["projected"], 1)

            def score(g, j, first=False):
                n = 4 * g + j
                pe.wait_ge(s["tails"], n + 1)
                pe.wait_ge(s["blocks"], 4 * (n + 1))
                for G in range(2):
                    pe.wait_ge(s["keys"], 2 * n + G + 1)
                    if not (first and j == 0):
                        pe.wait_ge(s["exped"], 2 * n + G - 1)
                    for a in range(2):
                        i = pe.matmul(psS[G][:, 0:KEYS], Q[j % 2][:, 2 * G + a, :], K[j % 2][:, 2 * G + a, :],
                                      start=(a == 0), stop=(a == 1))
                    i.then_inc(s["scored"], 1)

            def turn_probs(g, j, first=False):
                n = 4 * g + j
                pe.wait_ge(s["probs"], 2 * (n + 1))
                for G in range(2):
                    if not (first and j == 0):
                        pe.wait_ge(s["p_lo"], 2 * n + G - 1)
                    for t in range(3):
                        w = P if t < 2 else TAIL
                        i = pe.transpose(psP[G][0:w, t * P:(t + 1) * P], pr[j % 2][:, G, t * P:t * P + w], ident[:, :])
                    i.then_inc(s["pturned"], 1)

            def attend(g, j, first=False):
                n = 4 * g + j
                pe.wait_ge(s["pt_out"], 4 * (n + 1))
                pe.wait_ge(t_in[j], 16 * (g + 1))
                if not (first and j == 0):
                    pe.wait_ge(s["px_out"], 2 * n)
                pe.wait_ge(s["p_lo"], 2 * (n + 1))
                pe.wait_ge(s["v_lo"], n + 1)
                for k in range(2):
                    out, c = psV[:, 256 * k:256 * k + 256], slice(k * P, (k + 1) * P)
                    for t in range(2):
                        mm3(pe, out, (vh[j][:, t, c], vl[j][:, t, c]), (ph[j % 2][:, t, :], pl[j % 2][:, t, :]), t == 0, False)
                    i = pe.matmul(out, xt[j][:, c], pt[j % 2][:, :], start=False, stop=True)
                i.then_inc(s["attended"], 1)

            def value(g):
                pe.wait_ge(s["px_out"], 8 * (g + 1))
                for h in range(H):
                    for k in range(2):
                        i = pe.matmul(psV[64 * (h % 2):64 * (h % 2) + 64, P * (h // 2):P * (h // 2) + P],
                                      wv[:, k, DH * h:DH * h + DH], px[:, k, h, :, :], start=(k == 0), stop=(k == 1))
                i.then_inc(s["valued"], 1)

            def out(g):
                pe.wait_ge(s["u_out"], g + 1)
                for m in range(4):
                    i = pe.matmul(psV[:, 0:D], uT[:, m, :], wo[:, m, :], start=(m == 0), stop=(m == 3))
                i.then_inc(s["outed"], 1)

            def slot(g, j, first=False, last=False, batches=(True, True)):
                prev = (g, j - 1) if j else (g - 1, 3)
                prev2 = (g, j - 2) if j >= 2 else (g - 1, j + 2)
                attends = not (first and j < 2) and not (not batches[0] and j == 2)
                if batches[0]:
                    project(g, j, 0, first)
                if attends:
                    turn_probs(*prev2, first)
                if j == 2 and not first:
                    value(g - 1)
                if batches[1] and not (first and j == 0):
                    score(*prev, first)
                if batches[0] and not (last and j == 3):
                    turn(g + (j + 1) // 4, (j + 1) % 4)
                if j == 2 and not first:
                    out(g - 1)
                if batches[0]:
                    project(g, j, 1, first)
                if attends:
                    if j == 2 and not first:
                        pe.wait_ge(s["added"], g)
                    attend(*prev2, first)

            turn(0, 0, True)
            for j in range(4):
                slot(0, j, first=True)
            with pe.Fori(1, LASTG) as g:
                for j in range(4):
                    slot(g, j)
            for j in range(4):
                slot(LASTG, j, last=True)
            slot(GRP, 0, batches=(False, True))
            slot(GRP, 1, batches=(False, False))
            slot(GRP, 2, batches=(False, False))

DI, NH, CONVT, ZT = 512, 8, 6, 4


def past(eng, sem, value):
    if isinstance(value, int) and value <= 0:
        return
    eng.wait_ge(sem, value)


def slots(eng, slot, units, peeled, depth):
    for n in range(peeled):
        slot(n, n % 2)
    with eng.Fori(peeled // 2, units // 2 - 1) as i:
        slot(2 * i, 0)
        slot(2 * i + 1, 1)
    for n in range(units - 2, units + depth):
        slot(n, n % 2)


def unit(n):
    return not isinstance(n, int) or 0 <= n < GRP


def mamba_phase(nc, sem, io, X, later):
    with ExitStack() as ctx:
        def sb(name, shape, dt=F32):
            return ctx.enter_context(nc.sbuf_tensor("m_" + name, shape, dt))

        def pb(name, shape):
            return ctx.enter_context(nc.psum_tensor("m_" + name, shape, F32))

        DIN = 2 * DI + 2 * P
        w = sb("w", [P, 2, DIN + NH])
        wh, wl = sb("wh", [P, 2, DIN], F32R), sb("wl", [P, 2, DIN], F32R)
        wout = sb("wout", [P, 4, D])
        ident = sb("ident", [P, P])
        tri = sb("tri", [P, P])
        aft = sb("aft", [P, P])
        afr = sb("afr", [P, P], F32R)
        cols = sb("cols", [P, CONVT * 5 + 4])
        rows = sb("rows", [P, 2, NH])
        drow = sb("drow", [P, DI])
        A = sb("A", [P, NH])
        tick = sb("tick", [P, 1])
        half = sb("half", [P, 1])
        xn = [sb(f"xn{i}", [P, D]) for i in range(2)]
        xh = [sb(f"xh{i}", [P, 2, P], F32R) for i in range(2)]
        xl = [sb(f"xl{i}", [P, 2, P], F32R) for i in range(2)]
        st = sb("st", [P, 2, 6])
        mv = sb("mv", [P, 2, 2])
        ve = sb("ve", [P, 2])
        rs = sb("rs", [P, 2])
        pad = sb("pad", [P, CONVT, BPG, L + 3])
        acc = sb("acc", [P, CONVT, P])
        xa = [sb(f"xa{i}", [P, CONVT, P]) for i in range(2)]
        zs = [sb(f"zs{i}", [P, DI]) for i in range(2)]
        sp = sb("sp", [P, 8, NH])
        dt = sb("dt", [P, GRP, NH])
        da = sb("da", [P, NH])
        dah, dal = sb("dah", [P, NH], F32R), sb("dal", [P, NH], F32R)
        tah, tal = sb("tah", [P, NH, P], F32R), sb("tal", [P, NH, P], F32R)
        dec = sb("dec", [P, NH, P])
        gm = sb("gm", [P, P])
        mm = sb("mm", [P, NH, P])
        xd = sb("xd", [P, DI])
        xskip = sb("xskip", [P, DI])
        yd = sb("yd", [P, DI])
        yz = [sb(f"yz{i}", [P, DI]) for i in range(2)]
        y2 = sb("y2", [P, DI])
        ssq = sb("ssq", [P, 2])
        yzT = sb("yzT", [P, ZT, P])
        fe = sb("fe", [P, 2])
        fr = sb("fr", [P, 2])

        psT = pb("psT", [P, 512])
        psA = pb("psA", [P, 4, P])
        psB = pb("psB", [P, 512])
        psO = pb("psO", [P, 512])
        psL = pb("psL", [P, 2, 4, P])
        psX = pb("psX", [P, 512])
        psY = pb("psY", [P, DI])
        DT = psT[:, 256:256 + NH]

        s = {n: sem("m_" + n) for n in (
            "w_in", "big_in", "later_in", "w_hi", "w_lo", "consts", "a_exp", "a_set", "wout_set",
            "stats", "aggr", "var", "rstd", "xn", "added", "turned", "xt_hi", "xt_lo",
            "projA", "projB", "projZ", "dt_mm", "padA", "padB", "tap", "taps", "conv", "xact", "zact",
            "sp_v", "sp_n", "sp_min", "sp_exp", "sp_u", "sp_ln", "sp_c", "sp_s", "dt", "da", "da_hi", "da_lo", "ta_lo", "afr_set", "xskip", "yz_turned", "yz_out",
            "ta", "logs", "dec", "cb", "gm", "mm", "xturn", "xd", "y", "yd", "yz", "y2",
            "out", "f_var", "f_rstd", "f_out")}
        block = ctx.enter_context(nc.Block())
        WIN = 7
        tap = lambda m, k: cols[:, 4 * m + k:4 * m + k + 1]
        cbias = lambda m: cols[:, 24 + m:25 + m]
        normw = lambda q: cols[:, 30 + q:31 + q]

        @block.sync
        def _(sy):
            for k in range(2):
                sy.dma_start(w[:, k, :], io["m_w"][:, k, :]).then_inc(s["big_in"], 16)
            sy.wait_ge(s["big_in"], 32)
            for d, src in later:
                sy.dma_start(d[tuple(slice(None) for _ in d.shape)], io[src]).then_inc(s["later_in"], 16)
            sy.wait_ge(s["later_in"], 16 * len(later))

        @block.gpsimd
        def _(pool):
            pool.memset(half[:, :], -0.5).then_inc(s["consts"], 1)
            pool.memset(pad[:, :, :, :], 0.0).then_inc(s["consts"], 1)
            pool.wait_ge(s["consts"], 2)

            def ln_power(n, p):
                if not unit(n):
                    return
                pool.wait_ge(s["var"], n + 1)
                pool.tensor_tensor(rs[:, p:p + 1], ve[:, p:p + 1], half[:, :], ALU.pow).then_inc(s["rstd"], 1)

            def ln_add(n, p):
                if not unit(n):
                    return
                pool.wait_ge(s["xn"], n + 1)
                pool.tensor_tensor(X[:, n, :], X[:, n, :], xn[p][:, :], ALU.add).then_inc(s["added"], 1)

            def decays(n):
                if not unit(n):
                    return
                pool.wait_ge(s["da_hi"], n + 1)
                past(pool, s["logs"], n)
                pool.tensor_tensor(tah[:, :, :], tri[:, :].unsqueeze(1).to_broadcast([P, NH, P]),
                                   dah[:, :].bitcast(F32).unsqueeze(2).to_broadcast([P, NH, P]), ALU.mult).then_inc(s["ta"], 1)
                pool.wait_ge(s["da_lo"], n + 1)
                pool.tensor_tensor(tal[:, :, :], tri[:, :].unsqueeze(1).to_broadcast([P, NH, P]),
                                   dal[:, :].bitcast(F32).unsqueeze(2).to_broadcast([P, NH, P]), ALU.mult).then_inc(s["ta_lo"], 1)

            def out_power(n, p):
                if not unit(n):
                    return
                pool.wait_ge(s["f_var"], n + 1)
                pool.tensor_tensor(fr[:, p:p + 1], fe[:, p:p + 1], half[:, :], ALU.pow).then_inc(s["f_rstd"], 1)

            def gate(n, p):
                if not unit(n):
                    return
                pool.wait_ge(s["yd"], n + 1)
                pool.wait_ge(s["zact"], n + 1)
                past(pool, s["yz_turned"], n - 1)
                past(pool, s["y2"], n - 1)
                pool.tensor_tensor(yz[p][:, :], yd[:, :], zs[p][:, :], ALU.mult).then_inc(s["yz"], 1)

            def slot(n, p):
                gate(n - 2, p)
                ln_power(n + 2, p)
                out_power(n - 2, p)
                decays(n)
                ln_add(n + 2, p)

            for n in range(2):
                ln_power(n, n)
                ln_add(n, n)
            pool.wait_ge(s["w_in"], 16 * WIN)
            slots(pool, slot, GRP, 4, 2)

        @block.vector
        def _(dve):
            dve.wait_ge(s["consts"], 2)

            def ln_stats(n, p):
                if not unit(n):
                    return
                dve.bn_stats(st[:, p, :], X[:, n, :]).then_inc(s["stats"], 1)
                wait_ahead(dve, s["stats"], n + 1, tick)
                dve.bn_aggr(mv[:, p, :], st[:, p, :]).then_inc(s["aggr"], 1)
                dve.wait_ge(s["aggr"], n + 1)
                dve.tensor_scalar(ve[:, p:p + 1], mv[:, p, 1:2], EPS, None, ALU.add).then_inc(s["var"], 1)

            def ln_apply(n, p):
                if not unit(n):
                    return
                dve.wait_ge(s["rstd"], n + 1)
                past(dve, s["turned"], n - 1)
                past(dve, s["added"], n - 1)
                dve.tensor_scalar(xn[p][:, :], X[:, n, :], mv[:, p, 0:1], rs[:, p:p + 1],
                                  ALU.subtract, ALU.mult).then_inc(s["xn"], 1)

            def low(n, p):
                if not unit(n):
                    return
                dve.wait_ge(s["xt_hi"], n + 1)
                dve.tensor_tensor(xl[p][:, :, :], psT[:, 0:256].rearrange("p (k t) -> p k t", k=2),
                                  xh[p][:, :, :].bitcast(F32), ALU.subtract).then_inc(s["xt_lo"], 1)

            def conv(n, tiles, padded):
                if not unit(n):
                    return
                dve.wait_ge(s[padded], n + 1)
                for k in range(2, -1, -1):
                    for m in tiles:
                        if k == 2:
                            dve.wait_ge(s["tap"], CONVT * n + m + 1)
                        else:
                            dve.wait_ge(s["taps"], 3 * CONVT * n + 3 * tiles[0] + (m - tiles[0]) + len(tiles) * (1 - k) + 1)
                        a = acc[:, m, :].rearrange("p (b t) -> p b t", t=L)
                        dve.scalar_tensor_tensor(a, pad[:, m, :, k:k + L], tap(m, k), a, ALU.mult, ALU.add).then_inc(s["taps"], 1)

            def softplus_a(n):
                if not unit(n):
                    return
                dve.wait_ge(s["dt_mm"], n + 1)
                past(dve, s["dt"], n)
                dve.tensor_tensor(sp[:, 0, :], DT, rows[:, 0, :], ALU.add).then_inc(s["sp_v"], 1)
                dve.wait_ge(s["sp_v"], n + 1)
                dve.tensor_scalar(sp[:, 1, :], sp[:, 0, :], -1.0, None, ALU.mult).then_inc(s["sp_n"], 1)
                dve.wait_ge(s["sp_n"], n + 1)
                dve.tensor_tensor(sp[:, 2, :], sp[:, 0, :], sp[:, 1, :], ALU.min).then_inc(s["sp_min"], 1)

            def softplus_b(n):
                if not unit(n):
                    return
                dve.wait_ge(s["sp_exp"], n + 1)
                dve.tensor_scalar(sp[:, 4, :], sp[:, 3, :], 1.0, None, ALU.add).then_inc(s["sp_u"], 1)

            def softplus_c(n):
                if not unit(n):
                    return
                dve.wait_ge(s["sp_u"], n + 1)
                dve.scalar_tensor_tensor(sp[:, 6, :], sp[:, 4, :], 1.0, sp[:, 3, :], ALU.subtract, ALU.subtract).then_inc(s["sp_c"], 1)
                dve.wait_ge(s["sp_ln"], n + 1)
                dve.wait_ge(s["sp_c"], n + 1)
                dve.tensor_tensor(sp[:, 7, :], sp[:, 5, :], sp[:, 6, :], ALU.subtract).then_inc(s["sp_s"], 1)
                dve.wait_ge(s["sp_s"], n + 1)
                dve.scalar_tensor_tensor(dt[:, n, :], sp[:, 0, :], 0.0, sp[:, 7, :], ALU.max, ALU.add).then_inc(s["dt"], 1)
                dve.wait_ge(s["dt"], n + 1)
                if isinstance(n, int) and n == 0:
                    dve.wait_ge(s["a_set"], 1)
                past(dve, s["da_lo"], n)
                dve.tensor_tensor(da[:, :], dt[:, n, :], A[:, :], ALU.mult).then_inc(s["da"], 1)
                past(dve, s["ta"], n)
                dve.wait_ge(s["da"], n + 1)
                dve.tensor_copy(dah[:, :], da[:, :]).then_inc(s["da_hi"], 1)

            def decays_low(n):
                if not unit(n):
                    return
                dve.wait_ge(s["da_hi"], n + 1)
                past(dve, s["ta_lo"], n)
                dve.tensor_tensor(dal[:, :], da[:, :], dah[:, :].bitcast(F32), ALU.subtract).then_inc(s["da_lo"], 1)

            def scan_mix(n):
                if not unit(n):
                    return
                dve.wait_ge(s["gm"], n + 1)
                dve.wait_ge(s["dec"], 2 * (n + 1))
                dve.tensor_tensor(mm[:, :, :], dec[:, :, :], gm[:, :].unsqueeze(1).to_broadcast([P, NH, P]),
                                  ALU.mult).then_inc(s["mm"], 1)

            def scan_in(n):
                if not unit(n):
                    return
                dve.wait_ge(s["cb"], n + 1)
                past(dve, s["y"], n)
                dve.tensor_tensor(gm[:, :], psO[:, 384:512], tri[:, :], ALU.mult).then_inc(s["gm"], 1)
                dve.wait_ge(s["xturn"], n + 1)
                dve.tensor_tensor(xd[:, :].rearrange("p (h c) -> p h c", h=NH), psX[:, :].rearrange("p (h c) -> p h c", h=NH),
                                  dt[:, n, :].unsqueeze(2).to_broadcast([P, NH, DI // NH]), ALU.mult).then_inc(s["xd"], 1)
                past(dve, s["yd"], n)
                dve.tensor_tensor(xskip[:, :], psX[:, :], drow[:, :], ALU.mult).then_inc(s["xskip"], 1)

            def skips(n, p):
                if not unit(n):
                    return
                dve.wait_ge(s["y"], n + 1)
                past(dve, s["yz"], n)
                dve.wait_ge(s["xskip"], n + 1)
                dve.tensor_tensor(yd[:, :], psY[:, :], xskip[:, :], ALU.add).then_inc(s["yd"], 1)

            def out_var(n, p):
                if not unit(n):
                    return
                dve.wait_ge(s["y2"], n + 1)
                dve.tensor_scalar(fe[:, p:p + 1], ssq[:, p:p + 1], 1.0 / DI, EPS, ALU.mult, ALU.add).then_inc(s["f_var"], 1)

            def finish(n, p):
                if not unit(n):
                    return
                dve.wait_ge(s["f_rstd"], n + 1)
                dve.wait_ge(s["out"], n + 1)
                dve.wait_ge(s["added"], n + 1)
                dve.scalar_tensor_tensor(X[:, n, :], psO[:, 0:D], fr[:, p:p + 1], X[:, n, :],
                                         ALU.mult, ALU.add).then_inc(s["f_out"], 1)

            def slot(n, p):
                skips(n - 2, p)
                low(n + 1, 1 - p)
                ln_stats(n + 2, p)
                scan_in(n - 1)
                softplus_b(n)
                conv(n, (0, 1, 2, 3), "padA")
                out_var(n - 2, p)
                scan_mix(n - 1)
                softplus_c(n)
                softplus_a(n + 1)
                decays_low(n)
                ln_apply(n + 2, p)
                conv(n, (4, 5), "padB")
                finish(n - 2, p)

            for n in range(2):
                ln_stats(n, n)
                ln_apply(n, n)
            dve.wait_ge(s["w_in"], 16 * WIN)
            dve.wait_ge(s["big_in"], 32)
            dve.tensor_copy(wh[:, :, :], w[:, :, 0:DIN]).then_inc(s["w_hi"], 1)
            dve.wait_ge(s["w_hi"], 1)
            dve.tensor_tensor(wl[:, :, :], w[:, :, 0:DIN], wh[:, :, :].bitcast(F32), ALU.subtract).then_inc(s["w_lo"], 1)
            dve.tensor_copy(afr[:, :], aft[:, :]).then_inc(s["afr_set"], 1)
            for q in range(4):
                dve.tensor_scalar(wout[:, q, :], wout[:, q, :], normw(q), None, ALU.mult).then_inc(s["wout_set"], 1)
            dve.wait_ge(s["a_exp"], 1)
            dve.tensor_scalar(A[:, :], A[:, :], -1.0, None, ALU.mult).then_inc(s["a_set"], 1)
            low(0, 0)
            softplus_a(0)
            slots(dve, slot, GRP, 4, 2)

        @block.scalar
        def _(act):
            for d, src in ((ident, "ident"), (cols, "m_cols"), (rows, "m_rows"), (tri, "tri"), (aft, "aft"),
                           (wout, "m_out"), (drow, "m_d")):
                act.dma_start(d[tuple(slice(None) for _ in d.shape)], io[src]).then_inc(s["w_in"], 16)
            act.wait_ge(s["w_in"], 16 * WIN)
            act.wait_ge(s["consts"], 2)
            act.activation(A[:, :], rows[:, 1, :], ACT.Exp).then_inc(s["a_exp"], 1)

            def high(n, p):
                if not unit(n):
                    return
                act.wait_ge(s["turned"], n + 1)
                past(act, s["projZ"], n - 1)
                act.activation(xh[p][:, :, :], psT[:, 0:256].rearrange("p (k t) -> p k t", k=2), ACT.Copy).then_inc(s["xt_hi"], 1)

            def decay(n):
                if not unit(n):
                    return
                act.wait_ge(s["logs"], n + 1)
                past(act, s["mm"], n)
                for i in range(2):
                    act.activation(dec[:, 4 * i:4 * i + 4, :], psL[:, i, :, :], ACT.Exp).then_inc(s["dec"], 1)

            def pads(n, tiles, ps, proj, padded):
                if not unit(n):
                    return
                act.wait_ge(s[proj], n + 1)
                past(act, s["xact"], n)
                past(act, s["taps"], 3 * CONVT * n)
                for m in tiles:
                    act.activation(acc[:, m, :], ps(m), ACT.Identity, bias=cbias(m), scale=tap(m, 3)).then_inc(s["tap"], 1)
                    i = act.activation(pad[:, m, :, 3:3 + L], ps(m).rearrange("p (b t) -> p b t", t=L), ACT.Copy)
                i.then_inc(s[padded], 1)

            def softplus_exp(n):
                if not unit(n):
                    return
                act.wait_ge(s["sp_min"], n + 1)
                act.activation(sp[:, 3, :], sp[:, 2, :], ACT.Exp).then_inc(s["sp_exp"], 1)

            def softplus_ln(n):
                if not unit(n):
                    return
                act.wait_ge(s["sp_u"], n + 1)
                act.activation(sp[:, 5, :], sp[:, 4, :], ACT.Ln).then_inc(s["sp_ln"], 1)

            def silus(n, p):
                if not unit(n):
                    return
                act.wait_ge(s["projZ"], n + 1)
                past(act, s["yz"], n - 1)
                act.activation(zs[p][:, :], psA[:, :, :].rearrange("p a b -> p (a b)"), ACT.Silu).then_inc(s["zact"], 1)
                act.wait_ge(s["taps"], 3 * CONVT * (n + 1))
                past(act, s["xturn"], n - 1)
                past(act, s["cb"], n - 1)
                act.activation(xa[p][:, :, :], acc[:, :, :], ACT.Silu).then_inc(s["xact"], 1)

            def squares(n, p):
                if not unit(n):
                    return
                act.wait_ge(s["yz"], n + 1)
                past(act, s["f_var"], n - 1)
                act.activation(y2[:, :], yz[p][:, :], ACT.Square, accum_out=ssq[:, p:p + 1]).then_inc(s["y2"], 1)

            def gated_turned(n):
                if not unit(n):
                    return
                act.wait_ge(s["yz_turned"], n + 1)
                past(act, s["out"], n)
                act.activation(yzT[:, :, :], psL[:, 0, :, :], ACT.Copy).then_inc(s["yz_out"], 1)

            def slot(n, p):
                high(n + 1, 1 - p)
                softplus_exp(n)
                pads(n, (0, 1, 2, 3), lambda m: psA[:, m, :], "projA", "padA")
                gated_turned(n - 2)
                pads(n, (4, 5), lambda m: psB[:, P * (m - 4):P * (m - 3)], "projB", "padB")
                squares(n - 2, p)
                decay(n - 1)
                softplus_ln(n)
                silus(n, p)

            high(0, 0)
            slots(act, slot, GRP, 4, 2)

        @block.tensor
        def _(pe):
            pe.wait_ge(s["w_lo"], 1)
            pe.wait_ge(s["consts"], 2)

            def turn(n, p):
                if not unit(n):
                    return
                pe.wait_ge(s["xn"], n + 1)
                past(pe, s["xt_lo"], n)
                past(pe, s["sp_v"], n)
                for k in range(2):
                    i = pe.transpose(psT[:, k * P:(k + 1) * P], xn[p][:, k * P:(k + 1) * P], ident[:, :])
                i.then_inc(s["turned"], 1)

            def project(n, p, out, w0, tiles, done):
                for m in tiles:
                    for k in range(2):
                        c = w0 + m * P
                        i = mm3(pe, out(m), (wh[:, k, c:c + P], wl[:, k, c:c + P]), (xh[p][:, k, :], xl[p][:, k, :]),
                                k == 0, k == 1)
                i.then_inc(s[done], 1)

            def project_a(n, p):
                if not unit(n):
                    return
                pe.wait_ge(s["xt_lo"], n + 1)
                past(pe, s["zact"], n)
                project(n, p, lambda m: psA[:, m, :], DI, (0, 1, 2, 3), "projA")

            def project_b(n, p):
                if not unit(n):
                    return
                past(pe, s["padB"], n)
                project(n, p, lambda m: psB[:, P * (m - 4):P * (m - 3)], DI, (4, 5), "projB")

            def project_z(n, p):
                if not unit(n):
                    return
                pe.wait_ge(s["padA"], n + 1)
                z = psA[:, :, :].rearrange("p a b -> p (a b)")
                for k in range(2):
                    i = mm3(pe, z, (xh[p][:, k, :], xl[p][:, k, :]), (wh[:, k, 0:DI], wl[:, k, 0:DI]), k == 0, k == 1)
                i.then_inc(s["projZ"], 1)

            def steps(n, p):
                if not unit(n):
                    return
                pe.wait_ge(s["xt_lo"], n + 1)
                parts = [(x[p], k) for k in range(2) for x in (xh, xl)]
                for i, (x, k) in enumerate(parts):
                    t = pe.matmul(DT, x[:, k, :].bitcast(F32), w[:, k, DIN:DIN + NH], start=(i == 0), stop=(i == 3))
                t.then_inc(s["dt_mm"], 1)

            def logs(n):
                if not unit(n):
                    return
                pe.wait_ge(s["ta"], n + 1)
                pe.wait_ge(s["ta_lo"], n + 1)
                past(pe, s["dec"], 2 * n)
                past(pe, s["yz_out"], n)
                for i in range(2):
                    pe.matmul(psL[:, i, :, :], afr[:, :], tah[:, 4 * i:4 * i + 4, :], start=True, stop=False)
                    t = pe.matmul(psL[:, i, :, :], afr[:, :], tal[:, 4 * i:4 * i + 4, :], start=False, stop=True)
                t.then_inc(s["logs"], 1)

            def cb_and_x(n, p):
                if not unit(n):
                    return
                pe.wait_ge(s["xact"], n + 1)
                past(pe, s["f_out"], n - 1)
                pe.matmul(psO[:, 384:512], xa[p][:, 4, :], xa[p][:, 5, :], start=True, stop=True).then_inc(s["cb"], 1)
                past(pe, s["xd"], n)
                for q in range(4):
                    t = pe.transpose(psX[:, q * P:(q + 1) * P], xa[p][:, q, :], ident[:, :])
                t.then_inc(s["xturn"], 1)

            def scan(n):
                if not unit(n):
                    return
                pe.wait_ge(s["mm"], n + 1)
                pe.wait_ge(s["xd"], n + 1)
                past(pe, s["yd"], n)
                for h in range(NH):
                    t = pe.matmul(psY[:, 64 * h:64 * h + 64], mm[:, h, :], xd[:, 64 * h:64 * h + 64], start=True, stop=True)
                t.then_inc(s["y"], 1)

            def turn_gated(n, p):
                if not unit(n):
                    return
                pe.wait_ge(s["yz"], n + 1)
                pe.wait_ge(s["dec"], 2 * (n + 1))
                for q in range(ZT):
                    t = pe.transpose(psL[:, 0, q, :], yz[p][:, q * P:(q + 1) * P], ident[:, :])
                t.then_inc(s["yz_turned"], 1)

            def out(n):
                if not unit(n):
                    return
                pe.wait_ge(s["yz_out"], n + 1)
                pe.wait_ge(s["gm"], n + 1 + unit(n + 1))
                past(pe, s["f_out"], n)
                for q in range(ZT):
                    t = pe.matmul(psO[:, 0:D], yzT[:, q, :], wout[:, q, :], start=(q == 0), stop=(q == 3))
                t.then_inc(s["out"], 1)

            def slot(n, p):
                scan(n - 2)
                turn(n + 1, 1 - p)
                project_a(n, p)
                cb_and_x(n - 1, 1 - p)
                turn_gated(n - 2, p)
                project_b(n, p)
                logs(n - 1)
                project_z(n, p)
                steps(n + 1, 1 - p)
                out(n - 2)

            turn(0, 0)
            steps(0, 0)
            pe.wait_ge(s["wout_set"], 4)
            pe.wait_ge(s["afr_set"], 1)
            slots(pe, slot, GRP, 4, 2)

NHF, DF = 16, 16
E, FH = 8, 1024


def attention_phase(nc, sem, io, X, keep):
    tokens, logits = keep["tokens"], keep["logits"]
    with ExitStack() as ctx:
        def sb(name, shape, dt=F32):
            return ctx.enter_context(nc.sbuf_tensor("s_" + name, shape, dt))

        def pb(name, shape):
            return ctx.enter_context(nc.psum_tensor("s_" + name, shape, F32))

        wq, wk, wv, wp, gw, cols, rows, gbias, ident, heads, causal = (keep[n] for n in (
            "wq", "wk", "wv", "wp", "gw", "cols", "bp", "gbias", "ident", "heads", "causal"))
        tick = sb("tick", [P, 1])
        half = sb("half", [P, 1])
        h0 = sb("h0", [P, GRP, D])
        xn = [sb(f"xn{i}", [P, D]) for i in range(2)]
        hT = [sb(f"hT{i}", [P, 2, P]) for i in range(2)]
        stat = [sb(f"st{i}", [P, 2, 6]) for i in range(3)]
        mv = [sb(f"mv{i}", [P, 2, 2]) for i in range(3)]
        ve = [sb(f"ve{i}", [P, 2]) for i in range(3)]
        rs = [sb(f"rs{i}", [P, 2]) for i in range(3)]
        qT = [sb(f"qT{i}", [P, 2, P]) for i in range(2)]
        kT = [sb(f"kT{i}", [P, 2, P]) for i in range(2)]
        qx = sb("qx", [P, 2, BPG, 8, L])
        vx = [sb(f"vx{i}", [P, BPG, 4, 4, DF]) for i in range(2)]
        sc = sb("sc", [P, 16, L])
        mx = sb("mx", [P, 16])
        su = sb("su", [P, 16])
        ri = sb("ri", [P, 16])
        pr = sb("pr", [P, 16, L])
        pT = [sb(f"pT{i}", [P, 16, L]) for i in range(2)]
        yT = [sb(f"yT{i}", [P, 2, P]) for i in range(2)]
        h1 = [sb(f"h1{i}", [P, D]) for i in range(2)]
        n2 = [sb(f"n2{i}", [P, D]) for i in range(2)]
        mf = [sb(f"mf{i}", [P, 2, P]) for i in range(2)]

        psT = pb("psT", [P, 4, P])
        psQ = pb("psQ", [P, 4, P])
        psV = pb("psV", [P, 512])
        psS = pb("psS", [P, 16, L])
        psY = pb("psY", [P, 4, P])
        psO = pb("psO", [P, 512])
        psU = pb("psU", [P, 4, P])
        psG = pb("psG", [P, 512])
        s = {n: sem("s_" + n) for n in (
            "consts", "stats0", "aggr0", "var0", "rstd0", "norm0", "stats1", "aggr1", "var1", "rstd1", "norm1",
            "stats2", "aggr2", "var2", "rstd2", "norm2", "biased", "turned", "hT", "qk", "v", "q_out", "k_out",
            "qx", "vx_a", "vx_d", "scored", "masked", "peak", "shifted", "exped", "summed", "recip", "probs", "pT",
            "attended", "yT", "outed", "h1", "added", "turned2", "mf", "gate", "logits", "kept")}
        block = ctx.enter_context(nc.Block())
        col = lambda i, k: cols[:, i, k:k + 1]

        @block.gpsimd
        def _(pool):
            pool.memset(half[:, :], -0.5).then_inc(s["consts"], 1)
            for i in range(2):
                pool.memset(vx[i][:, :, :, :, :], 0.0).then_inc(s["consts"], 1)
            pool.wait_ge(s["consts"], 3)

            def power(which, n, p):
                if not unit(n):
                    return
                pool.wait_ge(s[f"var{which}"], n + 1)
                pool.tensor_tensor(rs[which][:, p:p + 1], ve[which][:, p:p + 1], half[:, :], ALU.pow).then_inc(s[f"rstd{which}"], 1)

            def bias(n):
                if not unit(n):
                    return
                pool.wait_ge(s["norm1"], n + 1)
                pool.tensor_tensor(h0[:, n, :], h0[:, n, :], rows[:, :], ALU.add).then_inc(s["biased"], 1)

            def by_head(n, p):
                if not unit(n):
                    return
                pool.wait_ge(s["q_out"], n + 1)
                past(pool, s["scored"], n)
                for k in range(2):
                    q = qT[p][:, k, :].rearrange("p (b t) -> p b t", t=L).unsqueeze(2).to_broadcast([P, BPG, 8, L])
                    own = heads[:, :].unsqueeze(1).unsqueeze(3).to_broadcast([P, BPG, 8, L])
                    pool.tensor_tensor(qx[:, k, :, :, :], q, own, ALU.mult).then_inc(s["qx"], 1)

            def add(n, p):
                if not unit(n):
                    return
                pool.wait_ge(s["h1"], n + 1)
                pool.tensor_tensor(X[:, n, :], X[:, n, :], h1[p][:, :], ALU.add).then_inc(s["added"], 1)

            def slot(n, p):
                power(0, n + 2, p)
                power(1, n + 2, p)
                power(2, n - 3, 1 - p)
                by_head(n, p)
                add(n - 3, 1 - p)
                bias(n + 2)

            for n in range(2):
                power(0, n, n)
                power(1, n, n)
                bias(n)
            slots(pool, slot, GRP, 6, 4)

        @block.vector
        def _(dve):
            dve.wait_ge(s["consts"], 3)

            def norm_stats(which, n, p, src):
                dve.bn_stats(stat[which][:, p, :], src).then_inc(s[f"stats{which}"], 1)
                wait_ahead(dve, s[f"stats{which}"], n + 1, tick)
                dve.bn_aggr(mv[which][:, p, :], stat[which][:, p, :]).then_inc(s[f"aggr{which}"], 1)
                dve.wait_ge(s[f"aggr{which}"], n + 1)
                dve.tensor_scalar(ve[which][:, p:p + 1], mv[which][:, p, 1:2], EPS, None, ALU.add).then_inc(s[f"var{which}"], 1)

            def norm_apply(which, n, p, src, dst):
                dve.wait_ge(s[f"rstd{which}"], n + 1)
                dve.tensor_scalar(dst, src, mv[which][:, p, 0:1], rs[which][:, p:p + 1],
                                  ALU.subtract, ALU.mult).then_inc(s[f"norm{which}"], 1)

            def norms_a(n, p):
                if unit(n):
                    norm_stats(0, n, p, X[:, n, :])

            def norms_b(n, p):
                if unit(n):
                    norm_apply(0, n, p, X[:, n, :], h0[:, n, :])
                    wait_ahead(dve, s["norm0"], n + 1, tick)
                    norm_stats(1, n, p, h0[:, n, :])

            def norms_c(n, p):
                if unit(n):
                    past(dve, s["turned"], n - 1)
                    norm_apply(1, n, p, h0[:, n, :], xn[p][:, :])

            def v_blocks(n, p):
                if not unit(n):
                    return
                dve.wait_ge(s["v"], n + 1)
                dve.wait_ge(s["vx_a"], n + 1)
                past(dve, s["attended"], n - 1)
                for b in range(2, 4):
                    for h in range(4):
                        i = dve.tensor_copy(vx[p][32 * h:32 * h + 32, b, :, h, :],
                                            psV[32 * b:32 * b + 32, 0:D].rearrange("p (g h d) -> p g h d", g=4, h=4)[:, :, h, :])
                i.then_inc(s["vx_d"], 1)

            def shift(n):
                if not unit(n):
                    return
                dve.wait_ge(s["scored"], n + 1)
                past(dve, s["exped"], n)
                dve.tensor_tensor(sc[:, :, :], psS[:, :, :], causal[:, :].unsqueeze(1).to_broadcast([P, 16, L]),
                                  ALU.add).then_inc(s["masked"], 1)
                dve.wait_ge(s["masked"], n + 1)
                dve.reduce_max(mx[:, :], sc[:, :, :], AXX).then_inc(s["peak"], 1)
                dve.wait_ge(s["peak"], n + 1)
                dve.tensor_tensor(sc[:, :, :], sc[:, :, :], mx[:, :].unsqueeze(2).to_broadcast([P, 16, L]),
                                  ALU.subtract).then_inc(s["shifted"], 1)

            def shares(n, p):
                if not unit(n):
                    return
                dve.wait_ge(s["exped"], n + 1)
                dve.reduce_sum(su[:, :], pr[:, :, :], AXX).then_inc(s["summed"], 1)
                dve.wait_ge(s["summed"], n + 1)
                dve.reciprocal(ri[:, :], su[:, :]).then_inc(s["recip"], 1)
                dve.wait_ge(s["recip"], n + 1)
                dve.tensor_tensor(pr[:, :, :], pr[:, :, :], ri[:, :].unsqueeze(2).to_broadcast([P, 16, L]),
                                  ALU.mult).then_inc(s["probs"], 1)
                dve.wait_ge(s["probs"], n + 1)
                past(dve, s["attended"], n - 1)
                dve.transpose(pT[p][:, :, :].rearrange("p a b -> p (a b)"),
                              pr[:, :, :].rearrange("p a b -> p (a b)")).then_inc(s["pT"], 1)

            def residual(n, p):
                if not unit(n):
                    return
                dve.wait_ge(s["outed"], n + 1)
                dve.wait_ge(s["biased"], n + 1)
                past(dve, s["added"], n - 1)
                dve.tensor_tensor(h1[p][:, :], psO[:, 0:D], h0[:, n, :], ALU.add).then_inc(s["h1"], 1)
                dve.wait_ge(s["h1"], n + 1)
                norm_stats(2, n, p, h1[p][:, :])

            def second_norm(n, p):
                if not unit(n):
                    return
                past(dve, s["turned2"], n - 1)
                norm_apply(2, n, p, h1[p][:, :], n2[p][:, :])
                dve.tensor_scalar(tokens[:, n, :], h1[p][:, :], mv[2][:, p, 0:1], rs[2][:, p:p + 1],
                                  ALU.subtract, ALU.mult).then_inc(s["kept"], 1)

            def route(n, p):
                if not unit(n):
                    return
                dve.wait_ge(s["gate"], n + 1)
                dve.tensor_tensor(logits[:, n, :], psG[:, 0:E], gbias[:, :], ALU.add).then_inc(s["logits"], 1)

            def slot(n, p):
                norms_a(n + 2, p)
                norms_b(n + 2, p)
                residual(n - 3, 1 - p)
                norms_c(n + 2, p)
                second_norm(n - 3, 1 - p)
                shift(n - 1)
                v_blocks(n, p)
                route(n - 4, p)
                shares(n - 1, 1 - p)

            for n in range(2):
                norms_a(n, n)
                norms_b(n, n)
                norms_c(n, n)
            slots(dve, slot, GRP, 6, 4)

        @block.scalar
        def _(act):
            act.wait_ge(s["consts"], 3)

            def affine(n, p):
                if not unit(n):
                    return
                act.wait_ge(s["turned"], n + 1)
                past(act, s["v"], n - 1)
                for k in range(2):
                    act.activation(hT[p][:, k, :], psT[:, k, :], ACT.Identity, bias=col(1, k), scale=col(0, k)).then_inc(s["hT"], 1)

            def biases(n, p):
                if not unit(n):
                    return
                act.wait_ge(s["qk"], n + 1)
                past(act, s["qx"], 2 * (n - 1))
                for k in range(2):
                    i = act.activation(qT[p][:, k, :], psQ[:, k, :], ACT.Identity, bias=col(2, k))
                i.then_inc(s["q_out"], 1)
                past(act, s["scored"], n - 1)
                for k in range(2):
                    i = act.activation(kT[p][:, k, :], psQ[:, 2 + k, :], ACT.Identity, bias=col(3, k))
                i.then_inc(s["k_out"], 1)

            def v_blocks(n, p):
                if not unit(n):
                    return
                act.wait_ge(s["v"], n + 1)
                past(act, s["attended"], n - 1)
                for b in range(2):
                    for h in range(4):
                        i = act.activation(vx[p][32 * h:32 * h + 32, b, :, h, :],
                                           psV[32 * b:32 * b + 32, 0:D].rearrange("p (g h d) -> p g h d", g=4, h=4)[:, :, h, :],
                                           ACT.Copy)
                i.then_inc(s["vx_a"], 1)

            def exps(n):
                if not unit(n):
                    return
                act.wait_ge(s["shifted"], n + 1)
                past(act, s["pT"], n)
                act.activation(pr[:, :, :], sc[:, :, :], ACT.Exp).then_inc(s["exped"], 1)

            def attended(n, p):
                if not unit(n):
                    return
                act.wait_ge(s["attended"], n + 1)
                past(act, s["outed"], n - 1)
                for k in range(2):
                    i = act.activation(yT[p][:, k, :], psY[:, k, :], ACT.Identity, bias=col(4, k))
                i.then_inc(s["yT"], 1)

            def affine2(n, p):
                if not unit(n):
                    return
                act.wait_ge(s["turned2"], n + 1)
                past(act, s["gate"], n - 1)
                for k in range(2):
                    act.activation(mf[p][:, k, :], psU[:, k, :], ACT.Identity, bias=col(6, k), scale=col(5, k)).then_inc(s["mf"], 1)

            def slot(n, p):
                affine(n + 1, 1 - p)
                affine2(n - 4, p)
                biases(n, p)
                v_blocks(n, p)
                attended(n - 2, p)
                exps(n - 1)

            affine(0, 0)
            slots(act, slot, GRP, 6, 4)

        @block.tensor
        def _(pe):

            def turn(n, p):
                if not unit(n):
                    return
                pe.wait_ge(s["norm1"], n + 1)
                past(pe, s["hT"], 2 * n)
                for k in range(2):
                    i = pe.transpose(psT[:, k, :], xn[p][:, k * P:(k + 1) * P], ident[:, :])
                i.then_inc(s["turned"], 1)

            def project(n, p):
                if not unit(n):
                    return
                pe.wait_ge(s["hT"], 2 * (n + 1))
                past(pe, s["k_out"], n)
                for i, w in enumerate((wq, wk)):
                    for m in range(2):
                        for k in range(2):
                            t = pe.matmul(psQ[:, 2 * i + m, :], w[:, k, m * P:(m + 1) * P], hT[p][:, k, :],
                                          start=(k == 0), stop=(k == 1))
                t.then_inc(s["qk"], 1)
                past(pe, s["vx_d"], n)
                for k in range(2):
                    t = pe.matmul(psV[:, 0:D], hT[p][:, k, :], wv[:, k, :], start=(k == 0), stop=(k == 1))
                t.then_inc(s["v"], 1)

            def score(n, p):
                if not unit(n):
                    return
                pe.wait_ge(s["qx"], 2 * (n + 1))
                pe.wait_ge(s["k_out"], n + 1)
                past(pe, s["masked"], n)
                for g in range(4):
                    for b in range(BPG):
                        t = pe.matmul(psS[:, BPG * g + b, :], qx[:, g // 2, b, 4 * (g % 2):4 * (g % 2) + 4, :],
                                      kT[p][:, g // 2, L * b:L * b + L], start=True, stop=True)
                t.then_inc(s["scored"], 1)

            def attend(n, p):
                if not unit(n):
                    return
                pe.wait_ge(s["pT"], n + 1)
                pe.wait_ge(s["vx_d"], n + 1)
                past(pe, s["yT"], n)
                for g in range(4):
                    for b in range(BPG):
                        t = pe.matmul(psY[64 * (g % 2):64 * (g % 2) + 64, g // 2, L * b:L * b + L],
                                      vx[p][:, b, g, :, :], pT[p][:, BPG * g + b, :], start=True, stop=True)
                t.then_inc(s["attended"], 1)

            def output(n, p):
                if not unit(n):
                    return
                pe.wait_ge(s["yT"], n + 1)
                past(pe, s["h1"], n)
                for k in range(2):
                    t = pe.matmul(psO[:, 0:D], yT[p][:, k, :], wp[:, k, :], start=(k == 0), stop=(k == 1))
                t.then_inc(s["outed"], 1)

            def turn2(n, p):
                if not unit(n):
                    return
                pe.wait_ge(s["norm2"], n + 1)
                past(pe, s["mf"], 2 * n)
                for k in range(2):
                    t = pe.transpose(psU[:, k, :], n2[p][:, k * P:(k + 1) * P], ident[:, :])
                t.then_inc(s["turned2"], 1)

            def route(n, p):
                if not unit(n):
                    return
                pe.wait_ge(s["mf"], 2 * (n + 1))
                past(pe, s["logits"], n)
                for k in range(2):
                    t = pe.matmul(psG[:, 0:E], mf[p][:, k, :], gw[:, k, :], start=(k == 0), stop=(k == 1))
                t.then_inc(s["gate"], 1)

            def slot(n, p):
                turn(n + 1, 1 - p)
                turn2(n - 4, p)
                project(n, p)
                output(n - 3, 1 - p)
                route(n - 4, p)
                score(n - 1, 1 - p)
                attend(n - 2, p)

            turn(0, 0)
            slots(pe, slot, GRP, 6, 4)


UT = 256
UNITS = 2 * B * L // UT + E
SLOTS = (UNITS + 1) * UT


def routing_phase(nc, sem, io, keep):
    logits, g1, g2, pos, cum = (keep[n] for n in ("logits", "g1", "g2", "pos", "cum"))
    STEPS_TO_EXP = 11
    with ExitStack() as ctx:
        def sb(name, shape):
            return ctx.enter_context(nc.sbuf_tensor("r_" + name, shape, F32))

        idx, steps, before = (keep[n] for n in ("experts", "steps", "before"))
        ones = sb("ones", [P, P])
        work, one, two, lg2, sel, slot, prod = (sb(n, [P, GRP, E]) for n in
                                                ("work", "one", "two", "lg2", "sel", "slot", "prod"))
        tot = sb("tot", [P, GRP, E])
        run = sb("run", [P, GRP + 1, E])
        more = sb("more", [P, E, B * L // UT - 1])
        units = sb("units", [P, E])
        cumf = sb("cumf", [P, E + 2])
        posf = sb("posf", [P, 2, GRP])
        top, at1, second, at2, gap, eg, den = (sb(n, [P, GRP]) for n in
                                               ("top", "at1", "second", "at2", "gap", "eg", "den"))
        ps = ctx.enter_context(nc.psum_tensor("r_ps", [P, 512], F32))
        pt = ctx.enter_context(nc.psum_tensor("r_pt", [P, 512], F32))
        step, exped, chosen, ranked, ones_set = (
            sem("r_" + n) for n in ("step", "exped", "chosen", "ranked", "ones_set"))
        block = ctx.enter_context(nc.Block())
        wide = lambda a: a[:, :].unsqueeze(2).to_broadcast([P, GRP, E])
        flat = lambda a: a[:, :, :].rearrange("p a b -> p (a b)")

        @block.scalar
        def _(act):
            act.wait_ge(step, STEPS_TO_EXP)
            act.activation(eg[:, :], gap[:, :], ACT.Exp).then_inc(exped, 1)

        @block.tensor
        def _(pe):
            pe.wait_ge(ones_set, 1)
            pe.wait_ge(chosen, 1)
            pe.matmul(ps[:, 0:P], before[:, :], flat(sel), start=True, stop=True).then_inc(ranked, 1)
            pe.matmul(pt[:, 0:P], ones[:, :], flat(sel), start=True, stop=True).then_inc(ranked, 1)

        @block.gpsimd
        def _(pool):
            pool.memset(ones[:, :], 1.0).then_inc(ones_set, 1)

        @block.vector
        def _(dve):
            count = [0]

            def link(i):
                count[0] += 1
                i.then_inc(step, 1)
                dve.wait_ge(step, count[0])

            ix = idx[:, :].unsqueeze(1).to_broadcast([P, GRP, E])

            def largest(src, value, at):
                link(dve.reduce_max(value[:, :], src[:, :, :], AXX))
                link(dve.tensor_tensor(work[:, :, :], src[:, :, :], wide(value), ALU.is_equal))
                link(dve.tensor_tensor(work[:, :, :], work[:, :, :], ix, ALU.mult))
                link(dve.reduce_max(at[:, :], work[:, :, :], AXX))

            largest(logits, top, at1)
            link(dve.tensor_tensor(one[:, :, :], work[:, :, :], wide(at1), ALU.is_equal))
            link(dve.scalar_tensor_tensor(flat(lg2), flat(one), -3.0e38, flat(logits), ALU.mult, ALU.add))
            largest(lg2, second, at2)
            link(dve.tensor_tensor(gap[:, :], second[:, :], top[:, :], ALU.subtract))
            assert count[0] == STEPS_TO_EXP
            link(dve.tensor_tensor(two[:, :, :], work[:, :, :], wide(at2), ALU.is_equal))
            dve.tensor_tensor(sel[:, :, :], one[:, :, :], two[:, :, :], ALU.add).then_inc(chosen, 1)
            dve.wait_ge(exped, 1)
            link(dve.tensor_scalar(den[:, :], eg[:, :], 1.0, None, ALU.add))
            link(dve.reciprocal(g1[:, :], den[:, :]))
            link(dve.tensor_tensor(g2[:, :], eg[:, :], g1[:, :], ALU.mult))
            dve.wait_ge(ranked, 2)
            link(dve.tensor_copy(tot[:, :, :], pt[:, 0:P].rearrange("p (g e) -> p g e", e=E)))
            link(dve.memset(run[:, 0, :], 0.0))
            for g in range(GRP):
                link(dve.tensor_tensor(run[:, g + 1, :], run[:, g, :], tot[:, g, :], ALU.add))
            nk = B * L // UT - 1
            link(dve.tensor_tensor(more[:, :, :], run[:, GRP, :].unsqueeze(2).to_broadcast([P, E, nk]),
                                   steps[:, :].unsqueeze(1).to_broadcast([P, E, nk]), ALU.is_gt))
            link(dve.reduce_sum(units[:, :], more[:, :, :], AXX))
            link(dve.tensor_scalar(units[:, :], units[:, :], 1.0, None, ALU.add))
            link(dve.memset(cumf[:, 0:2], 0.0))
            for e in range(E):
                link(dve.tensor_tensor(cumf[:, e + 2:e + 3], cumf[:, e + 1:e + 2], units[:, e:e + 1], ALU.add))
            link(dve.tensor_copy(cum[:, :], cumf[:, :]))
            link(dve.tensor_tensor(slot[:, :, :], run[:, 0:GRP, :], ps[:, 0:P].rearrange("p (g e) -> p g e", e=E), ALU.add))
            link(dve.scalar_tensor_tensor(slot[:, :, :], cumf[:, 1:E + 1].unsqueeze(1).to_broadcast([P, GRP, E]), float(UT),
                                          slot[:, :, :], ALU.mult, ALU.add))
            for k, choice in enumerate((one, two)):
                link(dve.tensor_tensor(prod[:, :, :], choice[:, :, :], slot[:, :, :], ALU.mult))
                link(dve.reduce_sum(posf[:, k, :], prod[:, :, :], AXX))
            dve.tensor_copy(pos[:, :, :], posf[:, :, :])


def experts_phase(nc, sem, io, keep):
    cum, rows, yrows, pos, tokens = (keep[n] for n in ("cum", "rows", "yrows", "pos", "tokens"))
    FT = FH // P
    with ExitStack() as ctx:
        def sb(name, shape, dt=F32):
            return ctx.enter_context(nc.sbuf_tensor("e_" + name, shape, dt))

        def pb(name):
            return ctx.enter_context(nc.psum_tensor("e_" + name, [P, 512], F32))

        w1 = [sb(f"w1{i}", [P, 2, FH]) for i in range(2)]
        w2 = [sb(f"w2{i}", [P, FT, D]) for i in range(2)]
        w1h = [sb(f"w1h{i}", [P, 2, FH], F32R) for i in range(2)]
        w1l = [sb(f"w1l{i}", [P, 2, FH], F32R) for i in range(2)]
        w2h = [sb(f"w2h{i}", [P, FT, D], F32R) for i in range(2)]
        w2l = [sb(f"w2l{i}", [P, FT, D], F32R) for i in range(2)]
        bs = sb("bs", [P, E, FT + 2])
        be = [sb(f"be{i}", [P, FT + 2]) for i in range(2)]
        ln2 = sb("ln2", [P, 2, 2])
        ident = sb("ident", [P, P])
        tick = sb("tick", [P, 6])
        nought = sb("nought", [P, 1])
        xs = sb("xs", [P, 2, D])
        xf = sb("xf", [P, 2, UT])
        xh, xl = sb("xh", [P, 2, UT], F32R), sb("xl", [P, 2, UT], F32R)
        mid = [sb(f"mid{i}", [P, UT]) for i in range(2)]
        dh, dl = sb("dh", [P, FT, UT], F32R), sb("dl", [P, FT, UT], F32R)
        yT = sb("yT", [P, 2, UT])
        yr = sb("yr", [P, 2, D])
        ps1 = [pb(f"ps1{i}") for i in range(4)]
        ps2, psX, psR = pb("ps2"), pb("psX"), pb("psR")
        s = {n: sem("e_" + n) for n in ("c_in", "be", "w1h", "w2h", "w1l", "w2l", "x_in", "turned", "xf", "xh", "xl",
                                        "up", "gelu", "hi", "lo", "unit_hid", "down", "yT", "yturned", "yrow", "stored",
                                        "last_stored", "zero", "copied", "nought")}
        w_in = [[sem(f"e_w{i + 1}_in{p}") for p in range(2)] for i in range(2)]
        block = ctx.enter_context(nc.Block())

        def entry(eng, k):
            return eng.value_load(cum[0:1, bass.ds(k, 1)], min_val=0, max_val=UNITS)

        def experts(eng, expert):
            with eng.Fori(0, E // 2 - 1) as i:
                for p in range(2):
                    expert(2 * i + p, p, entry(eng, 2 * i + p + 1), entry(eng, 2 * i + p + 2))
            for e in (E - 2, E - 1):
                expert(e, e % 2, entry(eng, e + 1), entry(eng, e + 2))

        @block.sync
        def _(sy):
            sy.dma_start(bs[:, :, :], io["e_b"]).then_inc(s["c_in"], 16)
            sy.dma_start(ln2[:, :, :], io["s_cols"][:, 5:7, :]).then_inc(s["c_in"], 16)
            sy.dma_start(ident[:, :], io["ident"]).then_inc(s["c_in"], 16)

            def unit_rows(dram, u):
                return dram[bass.ds(u * UT, UT), :].rearrange("(j p) d -> p j d", p=P)

            sy.wait_ge(s["copied"], 16 * 2 * GRP)
            sy.dma_start(xs[:, :, :], unit_rows(rows, 0)).then_inc(s["x_in"], 16)
            sy.wait_ge(s["zero"], 1)
            sy.dma_start(unit_rows(yrows, 0), yr[:, :, :]).then_inc(s["stored"], 16)
            last = entry(sy, E + 1)
            with sy.Fori(0, last) as u:
                sy.wait_ge(s["turned"], u + 1)
                sy.dma_start(xs[:, :, :], unit_rows(rows, u + 1)).then_inc(s["x_in"], 16)
                sy.wait_ge(s["yrow"], u + 2)
                sy.dma_start(unit_rows(yrows, u), yr[:, :, :]).then_inc(s["stored"], 16)
            sy.wait_ge(s["yrow"], last + 2)
            sy.dma_start(unit_rows(yrows, last), yr[:, :, :]).then_inc(s["last_stored"], 16)
            sy.wait_ge(s["last_stored"], 16)

        raws, highs, lows = (w1, w2), (w1h, w2h), (w1l, w2l)

        def load(eng, i, e, p):
            eng.dma_start(raws[i][p][:, :, :], io[("e_w1", "e_w2")[i]][e]).then_inc(w_in[i][p], 16)

        def low_part(eng, i, e, p):
            eng.wait_ge(s[("w1h", "w2h")[i]], e + 1)
            eng.tensor_tensor(lows[i][p][:, :, :], raws[i][p][:, :, :], highs[i][p][:, :, :].bitcast(F32),
                              ALU.subtract).then_inc(s[("w1l", "w2l")[i]], 1)

        @block.gpsimd
        def _(pool):
            pool.memset(nought[:, :], 0.0).then_inc(s["nought"], 1)
            for e in range(2):
                for i in range(2):
                    load(pool, i, e, e)
            pool.wait_ge(keep["zeroed"], 32)
            for k in range(2):
                for g in range(GRP):
                    pool.indirect_dma_start(rows, bass.IndirectOffsetOnAxis(pos[:, k, g:g + 1], 0),
                                            tokens[:, g, :], None).then_inc(s["copied"], 16)
            pool.wait_ge(s["nought"], 1)
            for e in range(E):
                p = e % 2
                for i in range(2):
                    if e:
                        pool.wait_ge(w_in[i][p], 16 * (e // 2 + 1))
                        if i == 0 and e >= 2:
                            pool.wait_ge(s["down"], entry(pool, e) + 1)
                        pool.tensor_tensor(highs[i][p][:, :, :], raws[i][p][:, :, :],
                                           nought[:, :].unsqueeze(2).to_broadcast(list(raws[i][p].shape)),
                                           ALU.add).then_inc(s[("w1h", "w2h")[i]], 1)
                        low_part(pool, i, e, p)
                    if e < E - 2:
                        pool.wait_ge(s[("w1l", "w2l")[i]], e + 1)
                        load(pool, i, e + 2, p)

        @block.scalar
        def _(act):
            def expert(e, p, first, end):
                act.activation(be[p][:, :], bs[:, e, :], ACT.Copy).then_inc(s["be"], 1)
                act.wait_ge(s["be"], e + 1)
                with act.Fori(first, end) as u:
                    for f in range(FT):
                        act.wait_ge(s["up"], 8 * u + f + 1)
                        if f < 2:
                            act.wait_ge(s["unit_hid"], u + 1)
                        else:
                            act.wait_ge(s["lo"], 8 * u + f - 1)
                        act.activation(mid[f % 2][:, :], ps1[f % 4][:, 0:UT], ACT.Gelu, bias=be[p][:, f:f + 1]).then_inc(s["gelu"], 1)
                    turn_out(u + 1)
                    act.wait_ge(s["down"], u + 2)
                    act.wait_ge(s["yturned"], u + 1)
                    for k in range(2):
                        act.activation(yT[:, k, :], ps2[:, UT * k:UT * k + UT], ACT.Identity,
                                       bias=be[p][:, FT + k:FT + k + 1]).then_inc(s["yT"], 1)

            def turn_out(u):
                act.wait_ge(s["turned"], u + 1)
                for k in range(2):
                    act.activation(xf[:, k, :], psX[:, UT * k:UT * k + UT], ACT.Identity,
                                   bias=ln2[:, 1, k:k + 1], scale=ln2[:, 0, k:k + 1]).then_inc(s["xf"], 1)
                act.wait_ge(s["xf"], 2 * (u + 1))
                act.activation(xh[:, :, :], xf[:, :, :], ACT.Copy).then_inc(s["xh"], 1)

            act.wait_ge(s["c_in"], 48)
            act.wait_ge(s["zero"], 4)
            for i in range(2):
                act.wait_ge(w_in[i][0], 16)
                act.activation(highs[i][0][:, :, :], raws[i][0][:, :, :], ACT.Copy).then_inc(s[("w1h", "w2h")[i]], 1)
            turn_out(0)
            experts(act, expert)

        @block.vector
        def _(dve):
            dve.memset(yr[:, :, :], 0.0).then_inc(s["zero"], 1)
            dve.memset(yT[:, :, :], 0.0).then_inc(s["zero"], 1)
            for i, n in enumerate(("unit_hid", "down", "yrow", "zero", "zero")):
                dve.memset(tick[:, i:i + 1], 0.0).then_inc(s[n], 1)

            def x_low(u):
                dve.wait_ge(s["xh"], u + 1)
                dve.tensor_tensor(xl[:, :, :], xf[:, :, :], xh[:, :, :].bitcast(F32), ALU.subtract).then_inc(s["xl"], 1)

            def row_out(u):
                dve.wait_ge(s["yturned"], u + 1)
                dve.wait_ge(s["stored"], 16 * (u + 1))
                dve.tensor_copy(yr[:, :, :], psR[:, :].rearrange("p (j d) -> p j d", j=2)).then_inc(s["yrow"], 1)

            def expert(e, p, first, end):
                with dve.Fori(first, end) as u:
                    for f in range(FT):
                        dve.wait_ge(s["gelu"], 8 * u + f + 1)
                        dve.tensor_copy(dh[:, f, :], mid[f % 2][:, :]).then_inc(s["hi"], 1)
                        dve.wait_ge(s["hi"], 8 * u + f + 1)
                        dve.tensor_tensor(dl[:, f, :], mid[f % 2][:, :], dh[:, f, :].bitcast(F32), ALU.subtract).then_inc(s["lo"], 1)
                    dve.wait_ge(s["lo"], 8 * u + 8)
                    dve.memset(tick[:, 5:6], 0.0).then_inc(s["unit_hid"], 1)
                    row_out(u)
                    x_low(u + 1)

            for i in range(2):
                low_part(dve, i, 0, 0)
            x_low(0)
            experts(dve, expert)
            row_out(entry(dve, E + 1))

        @block.tensor
        def _(pe):
            pe.wait_ge(s["c_in"], 48)
            pe.wait_ge(s["zero"], 4)

            def turn(u):
                pe.wait_ge(s["x_in"], 16 * (u + 1))
                for k in range(2):
                    for j in range(2):
                        t = pe.transpose(psX[:, UT * k + P * j:UT * k + P * j + P], xs[:, j, k * P:(k + 1) * P], ident[:, :])
                t.then_inc(s["turned"], 1)

            def turn_back(u):
                pe.wait_ge(s["yrow"], u + 1)
                for j in range(2):
                    for k in range(2):
                        t = pe.transpose(psR[:, D * j + P * k:D * j + P * k + P], yT[:, k, j * P:(j + 1) * P], ident[:, :])
                t.then_inc(s["yturned"], 1)

            def expert(e, p, first, end):
                with pe.Fori(first, end) as u:
                    pe.wait_ge(s["w1l"], e + 1)
                    pe.wait_ge(s["xl"], u + 1)
                    pe.wait_ge(s["unit_hid"], u + 1)
                    for f in range(FT):
                        if f >= 4:
                            pe.wait_ge(s["gelu"], 8 * u + f - 3)
                        for k in range(2):
                            t = mm3(pe, ps1[f % 4][:, 0:UT], (w1h[p][:, k, f * P:(f + 1) * P], w1l[p][:, k, f * P:(f + 1) * P]),
                                    (xh[:, k, :], xl[:, k, :]), k == 0, k == 1)
                        t.then_inc(s["up"], 1)
                    turn_back(u)
                    turn(u + 1)
                    pe.wait_ge(s["w2l"], e + 1)
                    for f in range(FT):
                        pe.wait_ge(s["lo"], 8 * u + f + 1)
                        for k in range(2):
                            a = (w2h[p][:, f, k * P:(k + 1) * P], w2l[p][:, f, k * P:(k + 1) * P])
                            out = ps2[:, UT * k:UT * k + UT]
                            start = f == 0 and k == 0
                            pe.matmul(out, a[0], dh[:, f, :], start=start, stop=False, skip_group_check=True)
                            pe.matmul(out, a[0], dl[:, f, :], start=False, stop=False, skip_group_check=True)
                            t = pe.matmul(out, a[1], dh[:, f, :], start=False, stop=(f == FT - 1), skip_group_check=True)
                    t.then_inc(s["down"], 1)

            turn(0)
            experts(pe, expert)
            end = entry(pe, E + 1)
            pe.wait_ge(s["yT"], 2 * end)
            turn_back(end)


def combine_phase(nc, sem, io, out, X, keep):
    g1, g2, pos, yrows = (keep[n] for n in ("g1", "g2", "pos", "yrows"))
    with ExitStack() as ctx:
        yg = ctx.enter_context(nc.sbuf_tensor("c_yg", [P, GRP, 2, D], F32))
        got = [sem(f"c_got{g}") for g in range(GRP)]
        first, done, stored = sem("c_first"), sem("c_done"), sem("c_stored")
        block = ctx.enter_context(nc.Block())

        @block.gpsimd
        def _(pool):
            for g in range(GRP):
                for k in range(2):
                    pool.indirect_dma_start(yg[:, g, k, :], None, yrows, bass.IndirectOffsetOnAxis(pos[:, k, g:g + 1], 0),
                                            element_offset=UT * D).then_inc(got[g], 16)

        @block.vector
        def _(dve):
            for g in range(GRP):
                dve.wait_ge(got[g], 32)
                dve.scalar_tensor_tensor(X[:, g, :], yg[:, g, 0, :], g1[:, g:g + 1], X[:, g, :], ALU.mult, ALU.add).then_inc(first, 1)
                dve.wait_ge(first, g + 1)
                dve.scalar_tensor_tensor(X[:, g, :], yg[:, g, 1, :], g2[:, g:g + 1], X[:, g, :], ALU.mult, ALU.add).then_inc(done, 1)

        @block.sync
        def _(sy):
            for g in range(0, GRP, 4):
                sy.wait_ge(done, g + 4)
                sy.dma_start(out[:, g:g + 4, :], X[:, g:g + 4, :]).then_inc(stored, 16)
            sy.wait_ge(stored, 16 * (GRP // 4))


def phase(nc, run, *args):
    with ExitStack() as ctx:
        made = []

        def sem(name):
            made.append(ctx.enter_context(nc.semaphore(name)))
            return made[-1]

        run(nc, sem, *args)
        nums = sorted(x.num for x in made)
        with nc.Block() as block:
            @block.sync
            def _(sp):
                while nums:
                    n = 1
                    while n < len(nums) and nums[n] == nums[0] + n:
                        n += 1
                    sp.sem_clear(range(nums[0], nums[0] + n))
                    del nums[:n]


def store_phase(nc, sem, out, X):
    stored = sem("z_stored")
    with nc.Block() as block:
        @block.sync
        def _(sp):
            sp.dma_start(out, X[:, :, :]).then_inc(stored, 16)
            sp.wait_ge(stored, 16)


def program(nc, io, out):
    with ExitStack() as ctx:
        X = ctx.enter_context(nc.sbuf_tensor("X", [P, GRP, D], F32))
        if STAGES > 2:
            rows = nc.dram_tensor("token_rows", (SLOTS, D), F32, kind="Internal").ap()
            yrows = nc.dram_tensor("expert_rows", (SLOTS, D), F32, kind="Internal").ap()
            zero = ctx.enter_context(nc.sbuf_tensor("zero", [P, D], F32))
            zeroed = ctx.enter_context(nc.semaphore("zeroed"))
        with ExitStack() as c2:
            kv = {n: c2.enter_context(nc.sbuf_tensor(n, shape, dt)) for n, shape, dt in (
                ("wkh", [P, 2, 512], F32R), ("wkl", [P, 2, 512], F32R), ("wv", [P, 2, 512], F32), ("wo", [P, 4, D], F32),
                ("gb", [P, 4, D], F32),
                ("ident", [P, P], F32), ("cos", [P, 256], F32),
                ("sin", [P, 2, 256], F32))}
            kv |= {
                "qT": c2.enter_context(nc.sbuf_tensor("qT", [P, 4, B * L], F32)),
                "KX": c2.enter_context(nc.sbuf_tensor("KX", [P, 4, B, TAIL], F32)),
                "zeros": (rows, yrows, zero, zeroed) if STAGES > 2 else None,
                "xe": nc.dram_tensor("tail_values", (B, TAIL, D), F32, kind="Internal").ap(),
            }
            phase(nc, latents_phase, io, X, kv)
            phase(nc, xattn_phase, io, X, kv)
        later, keep = [], {}
        if STAGES > 2:
            for n, shape, src in (
                    ("wq", [P, 2, D], "s_wq"), ("wk", [P, 2, D], "s_wk"), ("wv", [P, 2, D], "s_wv"), ("wp", [P, 2, D], "s_wp"),
                    ("gw", [P, 2, E], "s_gw"),
                    ("cols", [P, 8, 2], "s_cols"),
                    ("bp", [P, D], "s_bp"), ("gbias", [P, E], "s_gb"), ("ident", [P, P], "ident"),
                    ("heads", [P, 8], "heads"),
                    ("causal", [P, L], "causal"),
                    ("experts", [P, E], "experts"),
                    ("steps", [P, B * L // UT - 1], "steps"),
                    ("before", [P, P], "before")):
                keep[n] = ctx.enter_context(nc.sbuf_tensor("k_" + n, shape, F32))
                later.append((keep[n], src))
        if STAGES > 1:
            phase(nc, mamba_phase, io, X, later)
        if STAGES > 2:
            keep |= {n: ctx.enter_context(nc.sbuf_tensor(n, shape, dt)) for n, shape, dt in (
                ("tokens", [P, GRP, D], F32), ("logits", [P, GRP, E], F32), ("g1", [P, GRP], F32), ("g2", [P, GRP], F32),
                ("pos", [P, 2, GRP], mybir.dt.uint32), ("cum", [P, E + 2], mybir.dt.int32))}
            keep["rows"] = rows
            keep["zeroed"] = zeroed
            keep["yrows"] = yrows
            phase(nc, attention_phase, io, X, keep)
            phase(nc, routing_phase, io, keep)
            phase(nc, experts_phase, io, keep)
            phase(nc, combine_phase, io, out, X, keep)
        else:
            phase(nc, store_phase, out, X)


def rope_tables():
    inv = (np.float32(1.0) / np.float32(10000.0) ** (np.arange(0, DH, 2, dtype=np.float32) / np.float32(DH))).astype(np.float32)
    theta = (np.arange(S, dtype=np.float32)[:, None] * inv[None, :]).astype(np.float32)
    cos, sin = np.cos(theta).T.astype(np.float32), np.sin(theta).T.astype(np.float32)
    return np.tile(cos, (4, 1)), np.tile(sin, (4, 1))


def layouts(v):
    c = np.ascontiguousarray

    def rows(w):
        return c(w.reshape(-1, P, w.shape[-1]).transpose(1, 0, 2))

    def every(*vs):
        return c(np.tile(np.stack(vs)[None], (P, 1, 1)))

    def split_heads(w):
        return rows(w.reshape(D, 2, 4, 2, 32).transpose(0, 1, 3, 2, 4).reshape(D, 512))

    a = {}
    a["x"] = rows(v["x"].reshape(B * L, D))
    a["ctx"] = c(v["ctx_1024"][:, :256].reshape(B, 2, P, D).transpose(0, 2, 1, 3))
    a["ctx_last"] = c(v["ctx_1024"][:, 256])
    a["wq"] = split_heads(v["L0_xattn_Wq"])
    a["wk"] = split_heads(v["L0_xattn_Wkv"][:, :512])
    a["wv"] = rows(v["L0_xattn_Wkv"][:, 512:])
    a["wo"] = rows(v["L0_xattn_Wo"])
    a["gb"] = every(v["L0_xattn_gamma_x"], v["L0_xattn_beta_x"], v["L0_xattn_gamma_l"], v["L0_xattn_beta_l"])
    a["ident"] = np.eye(P, dtype=np.float32)
    cos, sin = rope_tables()
    a["cos"] = c(cos[:, :256])
    a["sin"] = c(np.stack([-sin[:, :256], sin[:, :256]], 1))
    a["edge"] = c(np.stack([cos[:, 256], sin[:, 256]], 1))
    if STAGES > 1:
        more_layouts(a, v)
    return a


def more_layouts(a, v):
    c = np.ascontiguousarray

    def rows(w):
        return c(w.reshape(-1, P, w.shape[-1]).transpose(1, 0, 2))

    def column(x):
        return x.reshape(-1, P).T

    a["m_w"] = rows(v["L0_attn_in_proj_w"].T)
    a["m_out"] = rows(v["L0_attn_out_proj_w"].T)
    cw = v["L0_attn_conv_w"].reshape(CONVT, P, 4).transpose(1, 0, 2).reshape(P, 4 * CONVT)
    a["m_cols"] = c(np.concatenate([cw, column(v["L0_attn_conv_b"]), column(v["L0_attn_norm_w"])], 1))
    a["m_d"] = c(np.tile(np.repeat(v["L0_attn_D"], DI // NH)[None], (P, 1)))
    a["m_rows"] = c(np.tile(np.stack([v["L0_attn_dt_bias"], v["L0_attn_A_log"]])[None], (P, 1, 1)))
    i = np.arange(P)
    same = (i[:, None] // L) == (i[None, :] // L)
    a["tri"] = (same & (i[:, None] <= i[None, :])).astype(np.float32)
    a["aft"] = (same & (i[:, None] > i[None, :])).astype(np.float32)
    if STAGES > 2:
        for n in ("q", "k", "v", "p"):
            a["s_w" + n] = rows(v["L0_ffn_W" + n])
        a["s_gw"] = rows(v["L0_ffn_gate_W"])
        vs = [v["L0_ffn_" + n] for n in ("ln1_g", "ln1_b", "bq", "bk", "bv", "ln2_g", "ln2_b", "ln2_b")]
        a["s_cols"] = c(np.stack([column(x) for x in vs], 1))
        a["s_bp"] = c(np.tile(v["L0_ffn_bp"][None], (P, 1)))
        a["s_gb"] = c(np.tile(v["L0_ffn_gate_b"][None], (P, 1)))
        a["heads"] = np.where(i[:, None] // DF == np.arange(8)[None], np.float32(DF ** -0.5), np.float32(0))
        a["causal"] = np.where(np.arange(L)[None] > (i % L)[:, None], np.float32(-1e30), np.float32(0))
        a["experts"] = np.tile(np.arange(E, 0, -1, dtype=np.float32)[None], (P, 1))
        a["e_w1"] = c(v["L0_ffn_exp_W1"].reshape(E, 2, P, FH).transpose(0, 2, 1, 3))
        a["e_w2"] = c(v["L0_ffn_exp_W2"].reshape(E, FH // P, P, D).transpose(0, 2, 1, 3))
        a["e_b"] = c(np.concatenate([v["L0_ffn_exp_b1"], v["L0_ffn_exp_b2"]], 1).reshape(E, (FH + D) // P, P).transpose(2, 0, 1))
        a["steps"] = np.tile(np.arange(1, 8, dtype=np.float32)[None] * UT, (P, 1))
        a["before"] = (i[:, None] < i[None, :]).astype(np.float32)

STAGES = 3


def kernel(**inputs):
    import concourse.bacc as bacc
    from concourse.bass_utils import run_bass_kernel_spmd

    arrays = layouts({k: np.asarray(v) for k, v in inputs.items()})
    nc = bacc.Bacc("TRN2", target_bir_lowering=False, num_devices=1)
    io = {k: nc.dram_tensor("in_" + k, a.shape, mybir.dt.from_np(a.dtype), kind="ExternalInput").ap() for k, a in arrays.items()}
    out = nc.dram_tensor("out_0", (P, GRP, D), F32, kind="ExternalOutput").ap()
    program(nc, io, out)
    r = run_bass_kernel_spmd(nc, [{"in_" + k: a for k, a in arrays.items()}], core_ids=[0])
    return np.ascontiguousarray(r.results[0]["out_0"].transpose(1, 0, 2)).reshape(B, L, D)
```
